# Optimizing a Trainium2 kernel written in Bass

```python
import numpy as np
import jax
import jax.numpy as jnp

def _softmax(x, axis=-1):
    return jax.nn.softmax(x, axis=axis)

def _gelu(x):
    return jax.nn.gelu(x, approximate=True)

def _silu(x):
    return jax.nn.silu(x)

def _sigmoid(x):
    return jax.nn.sigmoid(x)

def _layernorm(x, axis=-1, eps=1e-05):
    m = jnp.mean(x, axis=axis, keepdims=True)
    v = jnp.var(x, axis=axis, keepdims=True)
    return (x - m) / jnp.sqrt(v + eps)

def _scatter_add(tgt, idx, src, axis=0):
    return tgt.at[idx].add(src)

def _segment_sum(src, seg, n):
    return jax.ops.segment_sum(src, seg, n)
kernel_name = 'mk_gnn_preln_d2_gnn_r8_6f7f41'

def setup_inputs(seed: int=0):
    np.random.seed(seed)
    _w = jnp.asarray

    def _rec_inputs():
        import jax
        import jax.numpy as jnp
        _gk = jax.random.key(seed)
        x = -0.0001006 + 1 * jax.random.normal(jax.random.fold_in(_gk, 1), (6250, 96), jnp.float32)
        _s = jax.random.randint(jax.random.fold_in(_gk, 2), (50000,), 0, 6250, jnp.int32)
        _d = jax.random.randint(jax.random.fold_in(_gk, 3), (50000,), 0, 6250, jnp.int32)
        _loop = jnp.arange(6250, dtype=jnp.int32)
        src = jnp.concatenate([_s, _d, _loop])
        dst = jnp.concatenate([_d, _s, _loop])
        _o = jnp.argsort(dst, stable=True)
        src = src[_o]
        dst = dst[_o]
        edge_attr_4 = 0.000714719 + 1.00021 * jax.random.normal(jax.random.fold_in(_gk, 12), (106250, 4), jnp.float32)
        edge_weight = jax.random.uniform(jax.random.fold_in(_gk, 14), (106250,), jnp.float32, 0.0, 0.999998)
        return (x, src, dst, edge_attr_4, edge_weight)
    x, src, dst, edge_attr_4, edge_weight = _rec_inputs()

    def _L0_gnn_setup():
        import jax, jax.numpy as jnp
        import numpy as np
        EPS = 1e-05

        def _mlp(h, W, b, gamma, beta):
            h = jax.nn.relu(h @ W + b)
            mu = jnp.mean(h, axis=0)
            var = jnp.mean(jnp.square(h - mu), axis=0)
            return gamma * (h - mu) * jax.lax.rsqrt(var + EPS) + beta
        key = jax.random.key(seed)
        ks = jax.random.split(key, 10)
        N, E, C_in, C_out, E_dim = (6250, 100000, 96, 96, 4)
        x = jax.random.normal(ks[0], (N, C_in), dtype=jnp.float32)
        edge_index = jax.random.randint(ks[1], (2, E), 0, N, dtype=jnp.int64)
        edge_attr = jax.random.normal(ks[2], (E, E_dim), dtype=jnp.float32)
        s = lambda fan_in: 1.0 / np.sqrt(fan_in)
        W_node = jax.random.uniform(ks[3], (C_in, C_out), jnp.float32, -s(C_in), s(C_in))
        b_node = jnp.zeros((C_out,), jnp.float32)
        g_node = jnp.ones((C_out,), jnp.float32)
        beta_node = jnp.zeros((C_out,), jnp.float32)
        W_edge = jax.random.uniform(ks[4], (E_dim, C_out), jnp.float32, -s(E_dim), s(E_dim))
        b_edge = jnp.zeros((C_out,), jnp.float32)
        g_edge = jnp.ones((C_out,), jnp.float32)
        beta_edge = jnp.zeros((C_out,), jnp.float32)
        M_in = 2 * C_in + C_out
        W_msg = jax.random.uniform(ks[5], (M_in, C_out), jnp.float32, -s(M_in), s(M_in))
        b_msg = jnp.zeros((C_out,), jnp.float32)
        g_msg = jnp.ones((C_out,), jnp.float32)
        beta_msg = jnp.zeros((C_out,), jnp.float32)
        return dict(x=x, edge_index=edge_index, edge_attr=edge_attr, W_node=W_node, b_node=b_node, g_node=g_node, beta_node=beta_node, W_edge=W_edge, b_edge=b_edge, g_edge=g_edge, beta_edge=beta_edge, W_msg=W_msg, b_msg=b_msg, g_msg=g_msg, beta_msg=beta_msg)
    _L0_gnn_all = _L0_gnn_setup()
    _L0_gnn_in = {k: v for k, v in _L0_gnn_all.items() if k in ('W_node', 'b_node', 'g_node', 'beta_node', 'W_edge', 'b_edge', 'g_edge', 'beta_edge', 'W_msg', 'b_msg', 'g_msg', 'beta_msg')}
    del _L0_gnn_all

    def _L1_gnn_setup():
        import jax, jax.numpy as jnp
        import numpy as np
        N = 6250
        E = 100000
        D = 96

        def gcn_conv(x, row, col, ew, W, b):
            n = x.shape[0]
            h = x @ W
            deg = jax.ops.segment_sum(ew, col, num_segments=n) + 1.0
            dinv = jnp.where(deg > 0, jax.lax.rsqrt(deg), 0.0)
            norm = dinv[row] * ew * dinv[col]
            agg = jax.ops.segment_sum(h[row] * norm[:, None], col, num_segments=n)
            agg = agg + h * (dinv * dinv)[:, None]
            return agg + b
        key = jax.random.key(seed)
        ks = jax.random.split(key, 8)
        x = jax.random.normal(ks[0], (N, D), dtype=jnp.float32)
        edge_index = jax.random.randint(ks[1], (2, E), 0, N, dtype=jnp.int32)
        edge_weight = jax.random.uniform(ks[2], (E,), dtype=jnp.float32)
        batch = jnp.zeros((N,), dtype=jnp.int32)
        s = 1.0 / np.sqrt(D)
        W1 = jax.random.normal(ks[3], (D, D), dtype=jnp.float32) * s
        b1 = jnp.zeros((D,), dtype=jnp.float32)
        W2 = jax.random.normal(ks[4], (D, D), dtype=jnp.float32) * s
        b2 = jnp.zeros((D,), dtype=jnp.float32)
        return {'x': x, 'edge_index': edge_index, 'edge_weight': edge_weight, 'batch': batch, 'W1': W1, 'b1': b1, 'W2': W2, 'b2': b2}
    _L1_gnn_all = _L1_gnn_setup()
    _L1_gnn_in = {k: v for k, v in _L1_gnn_all.items() if k in ('W1', 'b1', 'W2', 'b2')}
    del _L1_gnn_all
    return {'x': x, 'src': src, 'dst': dst, 'edge_attr_4': edge_attr_4, 'edge_weight': edge_weight, 'L0_gnn_W_node': _L0_gnn_in['W_node'], 'L0_gnn_b_node': _L0_gnn_in['b_node'], 'L0_gnn_g_node': _L0_gnn_in['g_node'], 'L0_gnn_beta_node': _L0_gnn_in['beta_node'], 'L0_gnn_W_edge': _L0_gnn_in['W_edge'], 'L0_gnn_b_edge': _L0_gnn_in['b_edge'], 'L0_gnn_g_edge': _L0_gnn_in['g_edge'], 'L0_gnn_beta_edge': _L0_gnn_in['beta_edge'], 'L0_gnn_W_msg': _L0_gnn_in['W_msg'], 'L0_gnn_b_msg': _L0_gnn_in['b_msg'], 'L0_gnn_g_msg': _L0_gnn_in['g_msg'], 'L0_gnn_beta_msg': _L0_gnn_in['beta_msg'], 'L1_gnn_W1': _L1_gnn_in['W1'], 'L1_gnn_b1': _L1_gnn_in['b1'], 'L1_gnn_W2': _L1_gnn_in['W2'], 'L1_gnn_b2': _L1_gnn_in['b2']}

def reference(x, src, dst, edge_attr_4, edge_weight, L0_gnn_W_node, L0_gnn_b_node, L0_gnn_g_node, L0_gnn_beta_node, L0_gnn_W_edge, L0_gnn_b_edge, L0_gnn_g_edge, L0_gnn_beta_edge, L0_gnn_W_msg, L0_gnn_b_msg, L0_gnn_g_msg, L0_gnn_beta_msg, L1_gnn_W1, L1_gnn_b1, L1_gnn_W2, L1_gnn_b2):
    import jax
    import jax.numpy as jnp

    def _L0_gnn_ref(x, edge_index, edge_attr, W_node, b_node, g_node, beta_node, W_edge, b_edge, g_edge, beta_edge, W_msg, b_msg, g_msg, beta_msg):
        import jax, jax.numpy as jnp
        import numpy as np
        EPS = 1e-05

        def _mlp(h, W, b, gamma, beta):
            h = jax.nn.relu(h @ W + b)
            mu = jnp.mean(h, axis=0)
            var = jnp.mean(jnp.square(h - mu), axis=0)
            return gamma * (h - mu) * jax.lax.rsqrt(var + EPS) + beta
        node_feat = _mlp(x, W_node, b_node, g_node, beta_node)
        edge_feat = _mlp(edge_attr, W_edge, b_edge, g_edge, beta_edge)
        row, col = (edge_index[0], edge_index[1])
        message = jnp.concatenate([x[row], x[col], edge_feat], axis=1)
        message = _mlp(message, W_msg, b_msg, g_msg, beta_msg)
        agg = jax.ops.segment_sum(message, col, num_segments=node_feat.shape[0])
        return agg + node_feat

    def _L1_gnn_ref(x, edge_index, edge_weight, batch, W1, b1, W2, b2):
        import jax, jax.numpy as jnp
        import numpy as np
        N = 6250
        E = 100000
        D = 96

        def gcn_conv(x, row, col, ew, W, b):
            n = x.shape[0]
            h = x @ W
            deg = jax.ops.segment_sum(ew, col, num_segments=n) + 1.0
            dinv = jnp.where(deg > 0, jax.lax.rsqrt(deg), 0.0)
            norm = dinv[row] * ew * dinv[col]
            agg = jax.ops.segment_sum(h[row] * norm[:, None], col, num_segments=n)
            agg = agg + h * (dinv * dinv)[:, None]
            return agg + b
        row, col = (edge_index[0], edge_index[1])
        h = jax.nn.relu(gcn_conv(x, row, col, edge_weight, W1, b1))
        h = jax.nn.relu(gcn_conv(h, row, col, edge_weight, W2, b2))
        return h
    edge_index = jnp.stack([src, dst])
    batch0 = jnp.zeros((6250,), jnp.int32)
    h = jnp.maximum(_layernorm(x, axis=-1), 0.0)
    x = x + _L0_gnn_ref(h, edge_index, edge_attr_4, L0_gnn_W_node, L0_gnn_b_node, L0_gnn_g_node, L0_gnn_beta_node, L0_gnn_W_edge, L0_gnn_b_edge, L0_gnn_g_edge, L0_gnn_beta_edge, L0_gnn_W_msg, L0_gnn_b_msg, L0_gnn_g_msg, L0_gnn_beta_msg)
    h = jnp.maximum(_layernorm(x, axis=-1), 0.0)
    x = x + _L1_gnn_ref(h, edge_index, edge_weight, batch0, L1_gnn_W1, L1_gnn_b1, L1_gnn_W2, L1_gnn_b2)
    return x

_drawn_inputs = setup_inputs


def setup_inputs(seed=0):
    import zlib

    import numpy as np

    out = dict(_drawn_inputs(seed))
    spreads = {'L0_gnn_b_node': (0.0, 0.391),
     'L0_gnn_g_node': (1.0, 0.6),
     'L0_gnn_beta_node': (0.0, 0.8),
     'L0_gnn_b_edge': (0.0, 0.1),
     'L0_gnn_g_edge': (1.0, 0.2),
     'L0_gnn_beta_edge': (0.0, 0.1),
     'L0_gnn_b_msg': (0.0, 0.1),
     'L0_gnn_g_msg': (1.0, 0.2),
     'L0_gnn_beta_msg': (0.0, 0.1),
     'L1_gnn_b1': (0.0, 0.8),
     'L1_gnn_b2': (0.0, 0.8)}
    factors = {'edge_weight': 8.0, 'L1_gnn_W1': 3.479, 'L1_gnn_W2': 2.912}
    for name, (base, spread) in spreads.items():
        noise = np.random.default_rng([zlib.crc32(name.encode()), seed]).standard_normal(out[name].shape)
        drawn = base * np.exp(spread * noise) if base else spread * noise
        out[name] = jnp.asarray(drawn.astype(out[name].dtype))
    for name, factor in factors.items():
        out[name] = (out[name] * factor).astype(out[name].dtype)
    return out
```

```python
import numpy as np
import concourse.bass as bass
from concourse import mybir

ALU = mybir.AluOpType
ACT = mybir.ActivationFunctionType
AX = mybir.AxisListType
F32 = mybir.dt.float32
BF16 = mybir.dt.bfloat16
I32 = mybir.dt.int32
ds = bass.ds

N, D, E, DE = 6250, 96, 106250, 4
EPS = 1e-5
P = 128

TQ, QC, RC = 4, 4, 4
QE = TQ * P
NCH = -(-E // (QE * QC * RC)) * RC
NQ = NCH * QC
NT = NQ * TQ
EP = NT * P
NIT = NCH // RC
QR = QC * RC
TR = QR * TQ
LASTV = E - (NQ - 1) * QE
QB = NQ // 2
NCOL = NT + TR

W = 64
ROUNDS = -(-N // W)
FAR = float(1 << 20)
CLIP = 200.0

NB, NPART = 50, 125
HB = 5
NIB = NB // (2 * HB)
NPAD = N + W

NS = 3
KS = NS * NS * DE
CREDIT = QR


def nth(n):
    return n + 1 + CREDIT


class Kernel:
    pass


def allocate(nc, k):
    def sb(name, shape, dt=F32):
        return nc.alloc_sbuf_tensor(name, shape, dt)

    k.ident = sb("ident", [P, P])
    k.iota = sb("iota", [P, W])
    k.node_of_row = sb("node_of_row", [P, 1])
    k.ones = sb("ones", [P, 1])
    k.eps = sb("eps", [P, 1])
    k.xs = sb("xs", [NPART, NB, D])
    k.nfT = sb("nfT", [P, N])
    k.aggT = sb("aggT", [P, NPAD])
    k.table = sb("table", [NPART, NB, D])
    k.gathered = sb("gathered", [P, TR, D])
    k.src_cols = sb("src_cols", [P, NCOL], I32)
    k.src_stage = sb("src_stage", [P, TR], I32)
    k.edge_cols = sb("edge_cols", [P, NT, 2])
    k.rel_cols = sb("rel_cols", [P, NQ, TQ])
    k.rel_rows = sb("rel_rows", [QB, 2, QE])
    k.rel_clip = sb("rel_clip", [QB, 2, QE], BF16)
    k.base_q = sb("base_q", [QB, 2])
    k.base_all = sb("base_all", [P, NQ])
    k.base_int = sb("base_int", [1, NQ], I32)
    k.flag = sb("flag", [1, 1], I32)
    k.w12 = sb("w12", [P, 2 * D])
    k.w_node = sb("w_node", [P, D])
    k.w3 = sb("w3", [P, D])
    k.w3e = sb("w3e", [P, D])
    k.w_gcn = sb("w_gcn", [P, 2, D])
    k.w_edge_stack = sb("w_edge_stack", [KS, D], BF16)
    k.cols = sb("cols", [D, 16])
    k.b_gcn = sb("b_gcn", [NPART, 2, D])
    k.b_msg_row = sb("b_msg_row", [P, D])
    k.sq_sum = sb("sq_sum", [1, D])
    k.dinv = sb("dinv", [NPART, NB])
    k.rstd = sb("rstd", [NPART, NB])
    k.shift = sb("shift", [NPART, NB])
    k.stats = sb("stats", [NPART, NB, 6])
    k.small = sb("small", [NPART, 4, NB])
    k.edge_stats = sb("edge_stats", [D, NQ, 6])
    k.aff = sb("aff", [D, 24])
    k.aff_lhs = sb("aff_lhs", [D, 2, P])
    k.aff_msg = sb("aff_msg", [P, D + 1])
    k.aff_node = sb("aff_node", [P, D + 1])
    k.hT = sb("hT", [P, 2, NPART])
    k.h = sb("h", [NPART, 2, D])
    k.drow = sb("drow", [P, 2, QC * QE], BF16)
    k.estack = sb("estack", [KS, 2, QC * QE], BF16)
    k.p2w = sb("p2w", [P, 2 * QC, 2 * D], BF16)
    k.onehotT = sb("onehotT", [P, 2, QE], BF16)
    k.onehot = sb("onehot", [P, 2, TQ, W])
    k.edgeT = sb("edgeT", [P, 2, QE])
    k.pre = sb("pre", [P, 2, TQ, D])
    k.msg = sb("msg", [P, 2, TQ, P])
    k.sumT = sb("sumT", [P, 2, NPART])
    k.nodeT = sb("nodeT", [P, 2, NPART])
    k.msg_sq = sb("msg_sq", [P, 2, TQ, D])
    k.bank = [nc.alloc_psum_tensor(f"bank{i}", [P, 512], F32) for i in range(8)]
    k.gather_tab = nc.dram_tensor("gather_tab", [N, D], F32).ap()
    k.p2_tab = nc.dram_tensor("p2_tab", [NPAD, NS * D], BF16).ap()
    k.edge_tab = nc.dram_tensor("edge_tab", [KS, EP], BF16).ap()
    k.rel_tab = nc.dram_tensor("rel_tab", [NQ, QE], BF16).ap()
    k.base_tab = nc.dram_tensor("base_tab", [2, QB], F32).ap()


def end_phase(nc, sems):
    nc.all_engine_barrier()
    for s in sems:
        nc.gpsimd.sem_clear(s)
    nc.all_engine_barrier()


def named(nc, k, *names):
    for n in names:
        if n not in k.sems:
            k.sems[n] = nc.alloc_semaphore(n)
    return [k.sems[n] for n in names]


def linker(eng, sem):
    n = [0]

    def link(ins):
        n[0] += 1
        ins.then_inc(sem, 1)
        eng.wait_ge(sem, n[0])
    return link


def load_phase(nc, k, a):
    sems = named(nc, k, "cleared", "loaded", "pool_link", "dve_link", "parts", "wparts", "stored",
                 "weights_loaded")
    cleared, loaded, pool_link, dve_link, parts, wparts, stored, weights_loaded = sems
    FW = DE * EP // P
    raw = k.aggT[:, 0:FW]
    part = k.gathered[:, :, :].rearrange("p t d -> p (t d)").bitcast(BF16)[:, 0:NS * FW].rearrange("p (s w) -> p s w", s=NS)
    wraw = k.aff_msg[0:DE, 0:D]
    wpart = k.p2w[0:DE, 0:2, :].rearrange("p a b -> p (a b)")
    zeros = k.drow[0:W, 0, 0:NS * D]

    with nc.Block() as block:
        @block.gpsimd
        def _(pool):
            link = linker(pool, pool_link)
            for t in (k.w12, k.w_node, k.w3, k.w3e):
                pool.memset(t[:, :], 0.0)
            pool.memset(k.w_gcn[:, :, :], 0.0)
            link(pool.memset(zeros, 0.0))
            pool.sem_inc(cleared, 1)
            link(pool.memset(k.ident[:, :], 0.0))
            link(pool.affine_select(out=k.ident[:, :], in_=k.ident[:, :], compare_op=ALU.not_equal, fill=1.0,
                               base=0, pattern=[[-1, P]], channel_multiplier=1))
            link(pool.iota(k.iota[:, :], [[1, W]], 0, 0, allow_small_or_imprecise_dtypes=True))
            for r in range(P // W):
                link(pool.iota(k.node_of_row[r * W:(r + 1) * W, :], [[0, 1]], 0, 1, allow_small_or_imprecise_dtypes=True))
            link(pool.memset(k.ones[:, :], 1.0))
            link(pool.memset(k.eps[:, :], EPS))
            link(pool.memset(k.sq_sum[:, :], 0.0))
            for t in (k.hT, k.sumT, k.nodeT):
                link(pool.memset(t[:, :, :], 0.0))
            link(pool.memset(k.aff_lhs[:, :, :], 0.0))
            link(pool.memset(k.aff_node[:, :], 0.0))
            link(pool.memset(k.edgeT[:, :, :], 0.0))
            link(pool.memset(k.nfT[D:P, :], 0.0))
            link(pool.memset(k.msg[:, :, :, :], 1.0))
            link(pool.memset(k.edgeT[D:D + 1, :, :], 1.0))
            link(pool.memset(k.nfT[D:D + 1, :], 1.0))

        @block.sync
        def _(sp):
            n = 0
            for dst, src in ((raw, a["edge_attr_4"]), (wraw, a["L0_gnn_W_edge"])):
                sp.dma_start(dst, src).then_inc(loaded, 16)
                n += 1
            loads = [(k.xs[:, :, :], a["x"].rearrange("(p b) d -> p b d", b=NB)),
                     (k.src_cols[:, :], a["src"]),
                     (k.aggT[:, DE * EP // P:DE * EP // P + NT], a["edge_weight"]),
                     (k.b_msg_row[D:D + 1, :], a["L0_gnn_b_msg"].unsqueeze(0))]
            for i, name in enumerate(COLUMNS):
                loads.append((k.cols[:, i:i + 1], a[name].unsqueeze(1)))
            for i, name in enumerate(("L1_gnn_b1", "L1_gnn_b2")):
                loads.append((k.b_gcn[:, i, :], a[name].unsqueeze(0).broadcast_to([NPART, D])))
            for dst, src in loads:
                sp.dma_start(dst, src).then_inc(loaded, 16)
                n += 1
            sp.wait_ge(cleared, 1)
            wm = a["L0_gnn_W_msg"]
            for dst, src in ((k.w12[0:D, 0:D], wm[0:D, :]), (k.w12[0:D, D:2 * D], wm[D:2 * D, :]),
                             (k.w3[0:D, :], wm[2 * D:3 * D, :]), (k.w_node[0:D, :], a["L0_gnn_W_node"]),
                             (k.w_gcn[0:D, 0, :], a["L1_gnn_W1"]), (k.w_gcn[0:D, 1, :], a["L1_gnn_W2"]),
                             (k.p2_tab[N:NPAD, :], zeros)):
                sp.dma_start(dst, src).then_inc(weights_loaded, 16)
            sp.wait_ge(parts, 1)
            m = 0
            for i in range(NS):
                for j in range(NS):
                    r = (i * NS + j) * DE
                    rows = k.edge_tab[r:r + DE, :].rearrange("c (w f) -> (c w) f", f=FW)
                    sp.dma_start(rows, part[:, i, :]).then_inc(stored, 16)
                    m += 1
            sp.wait_ge(wparts, 1)
            for i in range(NS):
                for j in range(NS):
                    r = (i * NS + j) * DE
                    sp.dma_start(k.w_edge_stack[r:r + DE, :], wpart[:, j * D:(j + 1) * D]).then_inc(stored, 16)
                    m += 1
            sp.wait_ge(loaded, 16 * n)
            sp.wait_ge(weights_loaded, 16 * 7)
            sp.wait_ge(stored, 16 * m)

        @block.vector
        def _(dve):
            link = linker(dve, dve_link)
            dve.wait_ge(loaded, 32 + 16 * (len(COLUMNS) + 6))
            for s in range(NS):
                link(dve.tensor_copy(part[:, s, :], raw))
                if s < NS - 1:
                    link(dve.tensor_tensor(raw, raw, part[:, s, :], ALU.subtract))
            dve.sem_inc(parts, 1)
            link(dve.tensor_copy(k.edge_cols[:, :, 1], k.aggT[:, FW:FW + NT]))
            for s in range(NS):
                link(dve.tensor_copy(wpart[:, s * D:(s + 1) * D], wraw))
                if s < NS - 1:
                    link(dve.tensor_tensor(wraw, wraw, wpart[:, s * D:(s + 1) * D], ALU.subtract))
            dve.sem_inc(wparts, 1)
    end_phase(nc, sems)


COLUMNS = ("L0_gnn_b_node", "L0_gnn_g_node", "L0_gnn_beta_node", "L0_gnn_b_edge", "L0_gnn_g_edge",
           "L0_gnn_beta_edge", "L0_gnn_g_msg", "L0_gnn_beta_msg")


def col(k, name):
    i = COLUMNS.index(name)
    return k.cols[:, i:i + 1]


def window_phase(nc, k, a):
    sems = named(nc, k, "loaded", "dve_link", "base_ready", "base_stored", "base_back", "span_ready", "span_turned")
    loaded, link_sem, base_ready, base_stored, base_back, span_ready, span_turned = sems
    dst_q = k.aggT[0:QB, 0:2 * QE].bitcast(I32).rearrange("p (b e) -> p b e", b=2)
    dst_p = k.aggT[:, 2 * QE:2 * QE + NT].bitcast(I32)
    spans = k.aggT[0:QB, 2 * QE + NT:2 * QE + NT + 2 * QE].rearrange("p (b e) -> p b e", b=2)
    span_row = k.bank[0][0:1, 0:QB]
    with nc.Block() as block:
        @block.sync
        def _(sp):
            sp.dma_start(dst_q, a["dst"].rearrange("(b q e) -> q b e", b=2, e=QE)).then_inc(loaded, 16)
            sp.dma_start(dst_p, a["dst_cols"]).then_inc(loaded, 16)
            sp.wait_ge(base_ready, 1)
            for b in range(2):
                sp.dma_start(k.base_tab[b].unsqueeze(1), k.base_q[:, b:b + 1]).then_inc(base_stored, 16)
            sp.wait_ge(base_stored, 32)
            sp.dma_start(k.base_all[:, :], k.base_tab.rearrange("b q -> (b q)").unsqueeze(0).broadcast_to([P, NQ]))\
              .then_inc(base_back, 16)

        @block.tensor
        def _(pe):
            pe.wait_ge(span_ready, 1)
            pe.transpose(span_row, k.small[0:QB, 0, 0:1], k.ident[0:QB, 0:QB]).then_inc(span_turned, 1)

        @block.vector
        def _(dve):
            link = linker(dve, link_sem)
            dve.wait_ge(loaded, 32)
            link(dve.tensor_copy(k.rel_rows[:, :, :], dst_q))
            link(dve.tensor_reduce(k.base_q[:, :], k.rel_rows[:, :, :], AX.X, ALU.min))
            dve.sem_inc(base_ready, 1)
            link(dve.tensor_tensor(k.rel_rows[:, :, :], k.rel_rows[:, :, :],
                                   k.base_q[:, :].unsqueeze(2).broadcast_to([QB, 2, QE]), ALU.subtract))
            link(dve.scalar_tensor_tensor(spans, k.rel_rows[:, :, :], FAR / 2, k.rel_rows[:, :, :], ALU.is_lt, ALU.mult))
            link(dve.tensor_reduce(k.small[0:QB, 0, 0:1], spans, AX.XY, ALU.max))
            dve.sem_inc(span_ready, 1)
            link(dve.tensor_copy(k.rel_cols[:, :, :].rearrange("p q j -> p (q j)"), dst_p))
            dve.wait_ge(base_back, 16)
            link(dve.tensor_tensor(k.rel_cols[:, :, :], k.rel_cols[:, :, :],
                                   k.base_all[:, :].unsqueeze(2).broadcast_to([P, NQ, TQ]), ALU.subtract))
            dve.wait_ge(span_turned, 1)
            link(dve.tensor_reduce(k.small[0:1, 0, 1:2], span_row, AX.X, ALU.max))
            link(dve.tensor_scalar(k.flag[:, :], k.small[0:1, 0, 1:2], float(W), None, ALU.is_ge))
    end_phase(nc, sems)


def place_windows(nc, k, move):
    sems = named(nc, k, "dve_link", "clipped", "stored")
    link_sem, clipped, stored = sems
    with nc.Block() as block:
        @block.vector
        def _(dve):
            link = linker(dve, link_sem)
            if move:
                link(dve.tensor_scalar(k.rel_rows[:, :, :], k.rel_rows[:, :, :], float(-move), None, ALU.add))
                link(dve.tensor_scalar(k.rel_cols[:, :, :], k.rel_cols[:, :, :], float(-move), None, ALU.add))
                link(dve.tensor_scalar(k.base_all[:, :], k.base_all[:, :], float(move), None, ALU.add))
            link(dve.tensor_scalar(k.rel_clip[:, :, :], k.rel_rows[:, :, :], CLIP, -1.0, ALU.min, ALU.max))
            dve.sem_inc(clipped, 1)
            link(dve.tensor_scalar(k.base_int[:, :], k.base_all[0:1, :], float(N), None, ALU.min))
            rel = k.rel_cols[:, :, :].rearrange("p q j -> p (q j)")
            inside = k.edge_cols[:, :, 0]
            link(dve.tensor_scalar(inside, rel, 0.0, None, ALU.is_ge))
            link(dve.scalar_tensor_tensor(inside, rel, float(W), inside, ALU.is_lt, ALU.mult))

        @block.sync
        def _(sp):
            sp.wait_ge(clipped, 1)
            sp.dma_start(k.rel_tab.rearrange("(b q) e -> q b e", b=2), k.rel_clip[:, :, :]).then_inc(stored, 16)
            sp.wait_ge(stored, 16)
    end_phase(nc, sems)


def edge_stats_phase(nc, k):
    sems = named(nc, k, "rows_landed0", "rows_landed1", "product_done", "relu_done", "stats_done", "dve_link",
                 "var_ready", "root_done", "shift_ready", "shift_done")
    landed = sems[0:2]
    product_done, relu_done, stats_done, link_sem, var_ready, root_done, shift_ready, shift_done = sems[2:]
    NI, CI = NCH // 2, 2
    QI = CI * QC
    with nc.Block() as block:
        @block.sync
        def _(sp):
            with sp.Fori(0, NI) as it:
                for c in range(CI):
                    sp.wait_ge(product_done, nth(it * QI + (c - 2) * QC + QC - 1))
                    sp.dma_start(k.estack[:, c, :], k.edge_tab[:, ds((it * CI + c) * QC * QE, QC * QE)])\
                      .then_inc(landed[c], 16)

        @block.tensor
        def _(pe):
            pe.sem_inc(product_done, CREDIT)
            with pe.Fori(0, NI) as it:
                for q in range(QI):
                    n = it * QI + q
                    if q % QC == 0:
                        pe.wait_ge(landed[q // QC], it * 16 + 16)
                    pe.wait_ge(relu_done, nth(n - 2))
                    pe.matmul(k.bank[q % 2][0:D, :], k.w_edge_stack[:, :],
                              k.estack[:, q // QC, (q % QC) * QE:(q % QC + 1) * QE], start=True, stop=True)\
                      .then_inc(product_done, 1)
            pe.wait_ge(shift_ready, 1)
            pe.matmul(k.bank[2][:, 0:D], k.aff_lhs[:, 0, :], k.w3[0:D, :], start=True, stop=True).then_inc(shift_done, 1)

        @block.scalar
        def _(act):
            act.sem_inc(relu_done, CREDIT)
            with act.Fori(0, NI) as it:
                for q in range(QI):
                    n = it * QI + q
                    act.wait_ge(product_done, nth(n))
                    act.wait_ge(stats_done, nth(n - 2))
                    act.activation(k.edgeT[0:D, q % 2, :], k.bank[q % 2][0:D, :], ACT.Relu,
                                   bias=col(k, "L0_gnn_b_edge")).then_inc(relu_done, 1)
            act.wait_ge(var_ready, 1)
            act.activation(k.aff[:, 2:3], k.aff[:, 1:2], ACT.Sqrt, bias=k.eps[0:D, :]).then_inc(root_done, 1)

        @block.vector
        def _(dve):
            dve.sem_inc(stats_done, CREDIT)
            with dve.Fori(0, NI) as it:
                for q in range(QI):
                    n = it * QI + q
                    dve.wait_ge(relu_done, nth(n))
                    dve.bn_stats(k.edge_stats[:, ds(n, 1), :].rearrange("p a b -> p (a b)"), k.edgeT[0:D, q % 2, :])\
                       .then_inc(stats_done, 1)
            link = linker(dve, link_sem)
            dve.wait_ge(stats_done, nth(NQ - 1))
            link(dve.bn_stats(k.edge_stats[:, NQ - 1, :], k.edgeT[0:D, (NQ - 1) % 2, 0:LASTV]))
            link(dve.bn_aggr(k.aff[:, 0:2], k.edge_stats[:, :, :].rearrange("p a b -> p (a b)")))
            dve.sem_inc(var_ready, 1)
            dve.wait_ge(root_done, 1)
            affine(dve, link, k, 0, "edge")
            link(dve.tensor_scalar(k.w3e[0:D, :], k.w3[0:D, :], k.aff[:, 4:5], None, ALU.mult))
            link(dve.tensor_copy(k.aff_lhs[:, 0, D:D + 1], k.aff[:, 5:6]))
            dve.sem_inc(shift_ready, 1)
            dve.wait_ge(shift_done, 1)
            link(dve.tensor_tensor(k.w3e[D:D + 1, :], k.bank[2][D:D + 1, 0:D], k.b_msg_row[D:D + 1, :], ALU.add))
    end_phase(nc, sems)


def affine(dve, link, k, o, what):
    c = k.aff
    link(dve.reciprocal(c[:, o + 3:o + 4], c[:, o + 2:o + 3]))
    link(dve.tensor_tensor(c[:, o + 4:o + 5], c[:, o + 3:o + 4], col(k, f"L0_gnn_g_{what}"), ALU.mult))
    link(dve.tensor_tensor(c[:, o + 5:o + 6], c[:, o:o + 1], c[:, o + 4:o + 5], ALU.mult))
    link(dve.tensor_tensor(c[:, o + 5:o + 6], col(k, f"L0_gnn_beta_{what}"), c[:, o + 5:o + 6], ALU.subtract))


def layernorm_stats(dve, link, k, root_wait, var_inc):
    st = k.stats[:, :, :]
    m0, m1, v0, v1 = st[:, :, 1], st[:, :, 4], st[:, :, 2], st[:, :, 5]
    mean, half, var = k.small[:, 0, :], k.small[:, 1, :], k.small[:, 2, :]
    link(dve.tensor_tensor(mean, m0, m1, ALU.add))
    link(dve.tensor_tensor(half, m0, m1, ALU.subtract))
    link(dve.tensor_tensor(half, half, half, ALU.mult))
    link(dve.tensor_tensor(var, v0, v1, ALU.add))
    link(dve.tensor_scalar(half, half, 0.25, None, ALU.mult))
    link(dve.scalar_tensor_tensor(var, var, 1.0 / D, half, ALU.mult, ALU.add))
    dve.sem_inc(var_inc, 1)
    dve.wait_ge(root_wait, 1)
    link(dve.reciprocal(k.rstd[:, :], k.small[:, 3, :]))
    link(dve.scalar_tensor_tensor(k.shift[:, :], mean, -0.5, k.rstd[:, :], ALU.mult, ALU.mult))


def table_phase(nc, k):
    sems = named(nc, k, "dve_link", "var_ready", "root_done", "norm_ready", "h_done", "turned", "hT_done",
                 "products_done", "copied", "nf_done", "split_done", "stored0", "stored1", "affine_root",
                 "node_var", "act_link", "stats_done")
    (link_sem, var_ready, root_done, norm_ready, h_done, turned, hT_done, products_done, copied, nf_done,
     split_done, stored0, stored1, affine_root, node_var, act_link, stats_done) = sems
    stored = (stored0, stored1)
    TI = 2 * HB
    p2_stage = k.gathered[0:NPART, :, :].rearrange("p t d -> p (t d)").bitcast(BF16)[:, 0:TI * NS * D]\
        .rearrange("p (t s d) -> p t s d", t=TI, s=NS)
    rest = k.pre[0:NPART, :, 0, :]
    NG = 500
    groups = [(i, min(i + NG, N)) for i in range(0, N, NG)]
    tab = k.gather_tab.rearrange("(p b) d -> p b d", b=NB)
    p2 = k.p2_tab[0:N, :].rearrange("(p b) d -> p b d", b=NB)

    def tiles(n):
        return k.xs[:, ds(n, 1), :].rearrange("p a d -> p (a d)")

    with nc.Block() as block:
        @block.vector
        def _(dve):
            link = linker(dve, link_sem)
            for b in range(NB):
                ins = dve.bn_stats(k.stats[:, b, :], k.xs[:, b, :])
            link(ins)
            layernorm_stats(dve, link, k, root_done, var_ready)
            dve.sem_inc(norm_ready, 1)
            dve.sem_inc(split_done, CREDIT)
            dve.sem_inc(hT_done, CREDIT)
            with dve.Fori(0, NIB) as it:
                for t in range(TI):
                    n = it * TI + t
                    dve.wait_ge(turned, nth(n))
                    dve.wait_ge(products_done, nth(n - 2))
                    dve.tensor_copy(k.hT[0:D, t % 2, :], k.bank[t % 2][0:D, 0:NPART]).then_inc(hT_done, 1)
                    dve.wait_ge(products_done, nth(n))
                    prod = k.bank[6 + t % 2][0:NPART, 0:D]
                    rst = rest[:, t % 2, :]
                    st = p2_stage[:, t, :, :]
                    linkw = lambda ins, m: (ins.then_inc(stats_done, 1), dve.wait_ge(stats_done, n * 5 + m))
                    linkw(dve.tensor_copy(st[:, 0, :], prod), 1)
                    linkw(dve.tensor_tensor(rst, prod, st[:, 0, :], ALU.subtract), 2)
                    linkw(dve.tensor_copy(st[:, 2, :], rst), 3)
                    linkw(dve.tensor_tensor(rst, rst, st[:, 2, :], ALU.subtract), 4)
                    linkw(dve.tensor_copy(st[:, 1, :], rst), 5)
                    dve.sem_inc(split_done, 1)
                for half in range(2):
                    dve.wait_ge(stored[half], it * 32 + 32)
            dve.wait_ge(nf_done, nth(NB - 1))
            for i, (lo, hi) in enumerate(groups):
                ins = dve.bn_stats(k.edge_stats[:, i, :], k.nfT[0:D, lo:hi])
            link(ins)
            link(dve.bn_aggr(k.aff[:, 8:10], k.edge_stats[:, 0:len(groups), :].rearrange("p a b -> p (a b)")))
            dve.sem_inc(node_var, 1)
            dve.wait_ge(affine_root, 1)
            affine(dve, link, k, 8, "node")

        @block.scalar
        def _(act):
            act.wait_ge(var_ready, 1)
            act.activation(k.small[:, 3, :], k.small[:, 2, :], ACT.Sqrt, bias=k.eps[0:NPART, :]).then_inc(root_done, 1)
            act.wait_ge(norm_ready, 1)
            act.sem_inc(h_done, CREDIT)
            act.sem_inc(copied, CREDIT)
            act.sem_inc(nf_done, CREDIT)
            with act.Fori(0, NIB) as it:
                for t in range(TI):
                    n = it * TI + t
                    act.wait_ge(turned, nth(n - 2))
                    act.activation(k.h[:, t % 2, :], tiles(n), ACT.Relu,
                                   bias=k.shift[:, ds(n, 1)], scale=k.rstd[:, ds(n, 1)]).then_inc(h_done, 1)
                    act.wait_ge(products_done, nth(n))
                    act.copy(k.table[:, ds(n, 1), :].rearrange("p a d -> p (a d)"), k.bank[2 + t % 2][0:NPART, 0:D])\
                       .then_inc(copied, 1)
                    act.activation(k.nfT[0:D, ds(n * NPART, NPART)], k.bank[4 + t % 2][0:D, 0:NPART], ACT.Relu,
                                   bias=col(k, "L0_gnn_b_node")).then_inc(nf_done, 1)
            act.wait_ge(node_var, 1)
            act.activation(k.aff[:, 10:11], k.aff[:, 9:10], ACT.Sqrt, bias=k.eps[0:D, :]).then_inc(affine_root, 1)

        @block.tensor
        def _(pe):
            pe.sem_inc(turned, CREDIT)
            pe.sem_inc(products_done, CREDIT)
            with pe.Fori(0, NIB) as it:
                for t in range(TI):
                    n = it * TI + t
                    pe.wait_ge(h_done, nth(n))
                    pe.wait_ge(hT_done, nth(n - 2))
                    pe.transpose(k.bank[t % 2][0:D, 0:NPART], k.h[:, t % 2, :], k.ident[0:NPART, 0:NPART])\
                      .then_inc(turned, 1)
                    pe.wait_ge(hT_done, nth(n))
                    pe.wait_ge(copied, nth(n - 2))
                    pe.wait_ge(split_done, nth(n - 2))
                    pe.matmul(k.bank[2 + t % 2][0:NPART, 0:D], k.hT[:, t % 2, :], k.w12[:, 0:D], start=True, stop=True)
                    pe.matmul(k.bank[6 + t % 2][0:NPART, 0:D], k.hT[:, t % 2, :], k.w12[:, D:2 * D],
                              start=True, stop=True)
                    pe.wait_ge(nf_done, nth(n - 2))
                    pe.matmul(k.bank[4 + t % 2][0:D, 0:NPART], k.w_node[:, :], k.hT[:, t % 2, :], start=True, stop=True)\
                      .then_inc(products_done, 1)

        @block.sync
        def _(sp):
            with sp.Fori(0, NIB) as it:
                for half in range(2):
                    n = it * TI + half * HB
                    sp.wait_ge(split_done, nth(n + HB - 1))
                    sp.wait_ge(copied, nth(n + HB - 1))
                    sp.dma_start(p2[:, ds(n, HB), :], p2_stage[:, half * HB:half * HB + HB, :, :]
                                 .rearrange("p t s d -> p t (s d)")).then_inc(stored[half], 16)
                    sp.dma_start(tab[:, ds(n, HB), :], k.table[:, ds(n, HB), :]).then_inc(stored[half], 16)
            sp.wait_ge(stored0, NIB * 32)
            sp.wait_ge(stored1, NIB * 32)
    end_phase(nc, sems)


def clear_sums(nc, k):
    sems = named(nc, k, "cleared")
    with nc.Block() as block:
        @block.vector
        def _(dve):
            dve.memset(k.aggT[:, :], 0.0).then_inc(sems[0], 1)
            dve.wait_ge(sems[0], 1)
    end_phase(nc, sems)


def gather_rows(pool, k, ring, staged, used, turns):
    with pool.Fori(0, NIT) as it:
        for c in range(RC):
            pool.wait_ge(staged, it * RC + c + 1)
            pool.wait_ge(used, nth(it * QR + c * QC + QC - 1 - QR))
            pool.sem_inc(turns, 1)
            for t in range(c * QC * TQ, (c + 1) * QC * TQ):
                pool.indirect_dma_start(k.gathered[:, t, :], None, k.gather_tab,
                                        bass.IndirectOffsetOnAxis(ap=k.src_stage[:, t:t + 1], axis=0))\
                    .then_inc(ring[c], 16)
    for c in range(RC):
        pool.wait_ge(ring[c], NIT * 16 * QC * TQ)


def stage_first(act, k, staged):
    CT = QC * TQ
    for c in range(RC):
        act.copy(k.src_stage[:, c * CT:(c + 1) * CT], k.src_cols[:, c * CT:(c + 1) * CT]).then_inc(staged, 1)


def stage_next(act, k, it, c, ring, staged):
    CT = QC * TQ
    act.wait_ge(ring[c], it * (16 * CT) + 16 * CT)
    act.copy(k.src_stage[:, c * CT:(c + 1) * CT], k.src_cols[:, ds((it + 1) * TR + c * CT, CT)]).then_inc(staged, 1)


def window_bases(eng, k, it, c):
    return [eng.value_load(k.base_int[0:1, ds(it * QR + c * QC + q, 1)], min_val=0, max_val=N) for q in range(QC)]


def message_pass(nc, k, ring):
    sems = named(nc, k, "staged", "turns", "add_done", "edge_product", "edge_relu",
                 "onehotT_done", "onehot_done", "pre_done", "relu_done", "square_done", "seg_done", "sum_done",
                 "rows_landed0", "rows_landed1", "est_landed0", "est_landed1", "p2_landed0", "p2_landed1")
    (staged, turns, add_done, edge_product, edge_relu, onehotT_done, onehot_done, pre_done, relu_done, square_done,
     seg_done, sum_done) = sems[0:12]
    rows_landed, est_landed, p2_landed = sems[12:14], sems[14:16], sems[16:18]
    CT = QC * TQ

    with nc.Block() as block:
        @block.gpsimd
        def _(pool):
            gather_rows(pool, k, ring, staged, add_done, turns)

        @block.sync
        def _(sp):
            with sp.Fori(0, NIT) as it:
                for c in range(RC):
                    last = it * QR + (c - 2) * QC + QC - 1
                    i = it * RC + c
                    sp.wait_ge(edge_product, nth(last))
                    sp.dma_start(k.estack[:, c % 2, :], k.edge_tab[:, ds(i * QC * QE, QC * QE)])\
                      .then_inc(est_landed[c % 2], 16)
                    sp.wait_ge(onehotT_done, nth(last))
                    sp.dma_start(k.drow[:, c % 2, :], k.rel_tab[ds(i * QC, QC), :].rearrange("q e -> (q e)")
                                 .unsqueeze(0).broadcast_to([P, QC * QE])).then_inc(rows_landed[c % 2], 16)
                    bases = window_bases(sp, k, it, c)
                    sp.wait_ge(pre_done, nth(last))
                    for q in range(QC):
                        slot = (c % 2) * QC + q
                        sp.dma_start(k.p2w[0:W, slot, :], k.p2_tab[ds(bases[q], W), 0:2 * D]).then_inc(p2_landed[c % 2], 16)
                        sp.dma_start(k.p2w[W:P, slot, 0:D], k.p2_tab[ds(bases[q], W), 2 * D:3 * D])\
                          .then_inc(p2_landed[c % 2], 16)

        @block.tensor
        def _(pe):
            for s in (edge_product, pre_done, seg_done):
                pe.sem_inc(s, CREDIT)

            def edge(it, q):
                if q % QC == 0:
                    pe.wait_ge(est_landed[q // QC % 2], it * (16 * RC // 2) + 16 * (q // QC // 2 + 1))
                pe.wait_ge(edge_relu, nth(it * QR + q - 2))
                pe.matmul(k.bank[q % 2][0:D, :], k.w_edge_stack[:, :],
                          k.estack[:, q // QC % 2, (q % QC) * QE:(q % QC + 1) * QE], start=True, stop=True)\
                  .then_inc(edge_product, 1)

            def message(it, q):
                n = it * QR + q
                c = q // QC
                if q % QC == 0:
                    pe.wait_ge(p2_landed[c % 2], it * (32 * QC * RC // 2) + 32 * QC * (c // 2 + 1))
                pe.wait_ge(edge_relu, nth(n))
                pe.wait_ge(onehotT_done, nth(n))
                pe.wait_ge(add_done, nth(n - 2))
                slot = (c % 2) * QC + q % QC
                for j in range(TQ):
                    out = k.bank[2 + q % 2][:, j * D:(j + 1) * D]
                    e = slice(j * P, (j + 1) * P)
                    pe.matmul(out, k.onehotT[:, q % 2, e], k.p2w[:, slot, 0:D], start=True, stop=False)
                    pe.matmul(out, k.onehotT[0:W, q % 2, e], k.p2w[0:W, slot, D:2 * D], start=False, stop=False)
                    ins = pe.matmul(out, k.edgeT[:, q % 2, e], k.w3e[:, :], start=False, stop=True)
                ins.then_inc(pre_done, 1)

            def sums(it, q):
                n = it * QR + q
                pe.wait_ge(square_done, nth(n))
                pe.wait_ge(onehot_done, nth(n))
                pe.wait_ge(sum_done, nth(n - 2))
                for j in range(TQ):
                    pe.matmul(k.bank[4 + q % 2][0:D + 2, 0:W], k.msg[:, q % 2, j, 0:D + 2], k.onehot[:, q % 2, j, :],
                              start=(j == 0), stop=(j == TQ - 1))
                for j in range(TQ):
                    ins = pe.matmul(k.bank[6 + q % 2][0:1, 0:D], k.msg[:, q % 2, j, D:D + 1],
                                    k.msg_sq[:, q % 2, j, :], start=(j == 0), stop=(j == TQ - 1))
                ins.then_inc(seg_done, 1)

            with pe.Fori(0, NIT) as it:
                edge(it, 0)
                for q in range(QR):
                    if q + 1 < QR:
                        edge(it, q + 1)
                    message(it, q)
                    if q >= 1:
                        sums(it, q - 1)
                sums(it, QR - 1)

        @block.scalar
        def _(act):
            for s in (edge_relu, relu_done, square_done):
                act.sem_inc(s, CREDIT)
            stage_first(act, k, staged)

            def edge(it, q):
                n = it * QR + q
                act.wait_ge(edge_product, nth(n))
                act.wait_ge(pre_done, nth(n - 2))
                act.activation(k.edgeT[0:D, q % 2, :], k.bank[q % 2][0:D, :], ACT.Relu,
                               bias=col(k, "L0_gnn_b_edge")).then_inc(edge_relu, 1)

            with act.Fori(0, NIT) as it:
                edge(it, 0)
                for q in range(QR):
                    n = it * QR + q
                    if q + 1 < QR:
                        edge(it, q + 1)
                    if q % QC == 0:
                        stage_next(act, k, it, q // QC, ring, staged)
                    act.wait_ge(add_done, nth(n))
                    act.wait_ge(seg_done, nth(n - 2))
                    act.activation(k.msg[:, q % 2, :, 0:D], k.pre[:, q % 2, :, :], ACT.Relu).then_inc(relu_done, 1)
                    act.wait_ge(relu_done, nth(n))
                    act.activation(k.msg_sq[:, q % 2, :, :], k.msg[:, q % 2, :, 0:D], ACT.Square)\
                       .then_inc(square_done, 1)

        @block.vector
        def _(dve):
            dve.sem_inc(sum_done, CREDIT)
            for s in (add_done, onehotT_done, onehot_done):
                dve.sem_inc(s, CREDIT)

            def onehots(it, q):
                n = it * QR + q
                c = q // QC
                if q % QC == 0:
                    dve.wait_ge(rows_landed[c % 2], it * (16 * RC // 2) + 16 * (c // 2 + 1))
                dve.wait_ge(pre_done, nth(n - 2))
                dve.tensor_scalar(k.onehotT[:, q % 2, :], k.drow[:, c % 2, (q % QC) * QE:(q % QC + 1) * QE],
                                  k.node_of_row[:, :], None, ALU.is_equal).then_inc(onehotT_done, 1)
                dve.wait_ge(seg_done, nth(n - 2))
                dve.tensor_copy(k.msg[:, q % 2, :, D:D + 2], k.edge_cols[:, ds(n * TQ, TQ), :])
                dve.tensor_tensor(k.onehot[:, q % 2, :, :], k.iota[:, :].unsqueeze(1).broadcast_to([P, TQ, W]),
                                  k.rel_cols[:, ds(n, 1), :].rearrange("p a j -> p (a j)").unsqueeze(2)
                                  .broadcast_to([P, TQ, W]), ALU.is_equal).then_inc(onehot_done, 1)

            def add_sums(it, q, base):
                n = it * QR + q
                dve.wait_ge(seg_done, nth(n))
                dve.wait_ge(sum_done, nth(n - 1))
                window = k.aggT[0:D + 2, ds(base, W)]
                dve.tensor_tensor(window, window, k.bank[4 + q % 2][0:D + 2, 0:W], ALU.add)
                dve.tensor_tensor(k.sq_sum[:, :], k.sq_sum[:, :], k.bank[6 + q % 2][0:1, 0:D], ALU.add)\
                   .then_inc(sum_done, 1)

            with dve.Fori(0, NIT) as it:
                onehots(it, 0)
                for q in range(QR):
                    n = it * QR + q
                    if q + 1 < QR:
                        onehots(it, q + 1)
                    if q % QC == 0:
                        dve.wait_ge(ring[q // QC], it * (16 * CT) + 16 * CT)
                    dve.wait_ge(pre_done, nth(n))
                    dve.wait_ge(relu_done, nth(n - 2))
                    dve.tensor_tensor(k.pre[:, q % 2, :, :], k.gathered[:, q * TQ:(q + 1) * TQ, :],
                                      k.bank[2 + q % 2][:, 0:TQ * D].rearrange("p (j d) -> p j d", j=TQ), ALU.add)\
                       .then_inc(add_done, 1)
                    if q >= 1:
                        if (q - 1) % QC == 0:
                            bases = window_bases(dve, k, it, (q - 1) // QC)
                        add_sums(it, q - 1, bases[(q - 1) % QC])
                add_sums(it, QR - 1, bases[QC - 1])
    end_phase(nc, sems)


def gcn_pass(nc, k, ring):
    sems = named(nc, k, "staged", "turns", "onehot_done", "seg_done", "sum_done",
                 "pick_done")
    staged, turns, onehot_done, seg_done, sum_done, pick_done = sems
    CT = QC * TQ
    with nc.Block() as block:
        @block.gpsimd
        def _(pool):
            gather_rows(pool, k, ring, staged, seg_done, turns)

        @block.scalar
        def _(act):
            stage_first(act, k, staged)
            with act.Fori(0, NIT) as it:
                for c in range(RC):
                    stage_next(act, k, it, c, ring, staged)

        @block.tensor
        def _(pe):
            pe.sem_inc(seg_done, CREDIT)
            with pe.Fori(0, NIT) as it:
                for q in range(QR):
                    n = it * QR + q
                    if q % QC == 0:
                        pe.wait_ge(ring[q // QC], it * (16 * CT) + 16 * CT)
                    pe.wait_ge(onehot_done, nth(n))
                    pe.wait_ge(sum_done, nth(n - 2))
                    for j in range(TQ):
                        ins = pe.matmul(k.bank[q % 2][0:D, 0:W], k.gathered[:, q * TQ + j, :], k.onehot[:, q % 2, j, :],
                                        start=(j == 0), stop=(j == TQ - 1))
                    ins.then_inc(seg_done, 1)

        @block.vector
        def _(dve):
            for s in (sum_done, onehot_done, pick_done):
                dve.sem_inc(s, CREDIT)

            def weights(it, q):
                n = it * QR + q
                dve.wait_ge(seg_done, nth(n - 2))
                hot = k.onehot[:, q % 2, :, :]
                dve.tensor_tensor(hot, k.iota[:, :].unsqueeze(1).broadcast_to([P, TQ, W]),
                                  k.rel_cols[:, ds(n, 1), :].rearrange("p a j -> p (a j)").unsqueeze(2)
                                  .broadcast_to([P, TQ, W]), ALU.is_equal).then_inc(pick_done, 1)
                dve.wait_ge(pick_done, nth(n))
                dve.tensor_tensor(hot, hot, k.edge_cols[:, ds(n * TQ, TQ), 1:2].broadcast_to([P, TQ, W]), ALU.mult)\
                   .then_inc(onehot_done, 1)

            def add_sums(it, q, base):
                n = it * QR + q
                dve.wait_ge(seg_done, nth(n))
                dve.wait_ge(sum_done, nth(n - 1))
                window = k.aggT[0:D, ds(base, W)]
                dve.tensor_tensor(window, window, k.bank[q % 2][0:D, 0:W], ALU.add).then_inc(sum_done, 1)

            with dve.Fori(0, NIT) as it:
                weights(it, 0)
                for q in range(QR):
                    if q + 1 < QR:
                        weights(it, q + 1)
                    if q % QC == 0:
                        bases = window_bases(dve, k, it, q // QC)
                    add_sums(it, q, bases[q % QC])
    end_phase(nc, sems)


def restart_ring(nc, ring):
    nc.all_engine_barrier()
    nc.gpsimd.dma_reset(range(ring[0].num, ring[-1].num + 1))
    for s in ring:
        nc.gpsimd.sem_clear(s)
    nc.all_engine_barrier()


def all_windows(nc, k, name, run):
    ring = [nc.alloc_semaphore(f"{name}_landed{c}") for c in range(RC)]
    run(nc, k, ring)
    wide = nc.values_load(k.flag[0:1, 0:1], min_val=0, max_val=1)
    with nc.If(wide > 0):
        with nc.Fori(1, ROUNDS):
            restart_ring(nc, ring)
            place_windows(nc, k, W)
            run(nc, k, ring)
        place_windows(nc, k, -W * (ROUNDS - 1))


def copy_sums(pool, k, by_tile, rows, read, copied, turns):
    pool.sem_inc(copied, CREDIT)
    with pool.Fori(0, NIB) as it:
        for t in range(2 * HB):
            n = it * 2 * HB + t
            pool.wait_ge(read, nth(n - 2))
            pool.sem_inc(turns, 1)
            pool.tensor_copy(k.sumT[0:rows, t % 2, :], by_tile[0:rows, ds(n, 1), :].rearrange("k a p -> k (a p)"))\
                .then_inc(copied, 1)


def message_norm_phase(nc, k):
    sems = named(nc, k, "dve_link", "square_turned", "var_ready", "root_done", "maps_ready", "maps_done", "sum_product",
                 "added", "deg_ready", "deg_root", "sum_copied", "node_copied", "turns")
    (link_sem, square_turned, var_ready, root_done, maps_ready, maps_done, sum_product, added, deg_ready,
     deg_root, sum_copied, node_copied, turns) = sems
    by_tile = k.aggT[:, 0:N].rearrange("k (p b) -> k b p", b=NB)
    c = k.aff
    TI = 2 * HB
    with nc.Block() as block:
        @block.tensor
        def _(pe):
            pe.matmul(k.bank[0][0:D, 0:1], k.sq_sum[0:1, :], k.ones[0:1, 0:1], start=True, stop=True)\
              .then_inc(square_turned, 1)
            pe.wait_ge(maps_ready, 1)
            for i in range(2):
                ins = pe.matmul(k.bank[1][:, i * D:(i + 1) * D], k.aff_lhs[:, i, :], k.ident[0:D, 0:D],
                                start=True, stop=True)
            ins.then_inc(maps_done, 1)
            pe.sem_inc(sum_product, CREDIT)
            pe.wait_ge(maps_ready, 2)
            with pe.Fori(0, NIB) as it:
                for t in range(TI):
                    n = it * TI + t
                    pe.wait_ge(added, nth(n - 2))
                    out = k.bank[2 + t % 2][0:NPART, 0:D + 1]
                    pe.wait_ge(sum_copied, nth(n))
                    pe.matmul(out, k.sumT[:, t % 2, :], k.aff_msg[:, :], start=True, stop=False)
                    pe.wait_ge(node_copied, nth(n))
                    pe.matmul(out, k.nodeT[:, t % 2, :], k.aff_node[:, :], start=False, stop=True)\
                      .then_inc(sum_product, 1)

        @block.gpsimd
        def _(pool):
            copy_sums(pool, k, by_tile, D + 2, sum_product, sum_copied, turns)

        @block.scalar
        def _(act):
            act.wait_ge(var_ready, 1)
            act.activation(c[:, 18:19], c[:, 17:18], ACT.Sqrt, bias=k.eps[0:D, :]).then_inc(root_done, 1)
            act.sem_inc(node_copied, CREDIT)
            with act.Fori(0, NIB) as it:
                for t in range(TI):
                    n = it * TI + t
                    act.wait_ge(sum_product, nth(n - 2))
                    act.copy(k.nodeT[0:D + 1, t % 2, :], k.nfT[0:D + 1, ds(n * NPART, NPART)]).then_inc(node_copied, 1)
            act.wait_ge(deg_ready, 1)
            act.activation(k.small[:, 1, :], k.small[:, 0, :], ACT.Sqrt).then_inc(deg_root, 1)

        @block.vector
        def _(dve):
            link = linker(dve, link_sem)
            link(dve.tensor_reduce(c[:, 16:17], k.aggT[0:D, 0:N], AX.X, ALU.add))
            link(dve.tensor_scalar(c[:, 16:17], c[:, 16:17], 1.0 / E, None, ALU.mult))
            link(dve.tensor_tensor(c[:, 22:23], c[:, 16:17], c[:, 16:17], ALU.mult))
            dve.wait_ge(square_turned, 1)
            link(dve.scalar_tensor_tensor(c[:, 17:18], k.bank[0][0:D, 0:1], 1.0 / E, c[:, 22:23], ALU.mult, ALU.subtract))
            link(dve.tensor_scalar(c[:, 17:18], c[:, 17:18], 0.0, None, ALU.max))
            dve.sem_inc(var_ready, 1)
            dve.wait_ge(root_done, 1)
            affine(dve, link, k, 16, "msg")
            for i, o in ((0, 16), (1, 8)):
                dve.tensor_scalar(k.aff_lhs[:, i, 0:D], k.ident[0:D, 0:D], c[:, o + 4:o + 5], None, ALU.mult)
                link(dve.tensor_copy(k.aff_lhs[:, i, D:D + 1], c[:, o + 5:o + 6]))
            dve.sem_inc(maps_ready, 1)
            dve.wait_ge(maps_done, 1)
            dve.tensor_copy(k.aff_msg[:, 0:D], k.bank[1][:, 0:D])
            dve.tensor_copy(k.aff_msg[:, D:D + 1], k.ident[:, D + 1:D + 2])
            link(dve.tensor_copy(k.aff_node[:, 0:D], k.bank[1][:, D:2 * D]))
            dve.sem_inc(maps_ready, 1)
            dve.sem_inc(added, CREDIT)
            with dve.Fori(0, NIB) as it:
                for t in range(TI):
                    n = it * TI + t
                    dve.wait_ge(sum_product, nth(n))
                    xt = k.xs[:, ds(n, 1), :].rearrange("p a d -> p (a d)")
                    dve.tensor_scalar(k.small[:, 0, ds(n, 1)], k.bank[2 + t % 2][0:NPART, D:D + 1], 1.0, None, ALU.add)
                    dve.tensor_tensor(xt, xt, k.bank[2 + t % 2][0:NPART, 0:D], ALU.add).then_inc(added, 1)
            dve.wait_ge(added, nth(NB - 1))
            link(dve.tensor_scalar(k.small[:, 2, :], k.small[:, 0, :], 0.0, None, ALU.is_gt))
            link(dve.tensor_scalar(k.small[:, 0, :], k.small[:, 0, :], 1e-30, None, ALU.max))
            dve.sem_inc(deg_ready, 1)
            dve.wait_ge(deg_root, 1)
            link(dve.reciprocal(k.dinv[:, :], k.small[:, 1, :]))
            link(dve.tensor_tensor(k.dinv[:, :], k.dinv[:, :], k.small[:, 2, :], ALU.mult))
    end_phase(nc, sems)


def gcn_table_phase(nc, k, layer):
    sems = named(nc, k, "dve_link", "var_ready", "root_done", "norm_ready", "h_done", "turned", "hT_done",
                 "products_done", "scaled", "stored0", "stored1", "sum_turned", "added", "mixed", "cleared",
                 "sum_copied", "turns")
    (link_sem, var_ready, root_done, norm_ready, h_done, turned, hT_done, products_done, scaled, stored0, stored1,
     sum_turned, added, mixed, cleared, sum_copied, turns) = sems
    stored = (stored0, stored1)
    TI = 2 * HB
    tab = k.gather_tab.rearrange("(p b) d -> p b d", b=NB)
    by_tile = k.aggT[:, 0:N].rearrange("k (p b) -> k b p", b=NB)
    with nc.Block() as block:
        @block.vector
        def _(dve):
            link = linker(dve, link_sem)
            if layer == 0:
                for b in range(NB):
                    ins = dve.bn_stats(k.stats[:, b, :], k.xs[:, b, :])
                link(ins)
                layernorm_stats(dve, link, k, root_done, var_ready)
                dve.sem_inc(norm_ready, 1)
            for s in (hT_done, added, mixed):
                dve.sem_inc(s, CREDIT)
            with dve.Fori(0, NIB) as it:
                for t in range(TI):
                    n = it * TI + t
                    if layer:
                        dve.wait_ge(sum_turned, nth(n))
                        dve.wait_ge(h_done, nth(n - 2))
                        mix(dve, k, n, t, layer - 1, added, mixed)
                    dve.wait_ge(turned, nth(n))
                    dve.wait_ge(products_done, nth(n - 2))
                    dve.tensor_copy(k.hT[0:D, t % 2, :], k.bank[t % 2][0:D, 0:NPART]).then_inc(hT_done, 1)

        @block.scalar
        def _(act):
            if layer == 0:
                act.wait_ge(var_ready, 1)
                act.activation(k.small[:, 3, :], k.small[:, 2, :], ACT.Sqrt, bias=k.eps[0:NPART, :])\
                   .then_inc(root_done, 1)
                act.wait_ge(norm_ready, 1)
            act.sem_inc(h_done, CREDIT)
            act.sem_inc(scaled, CREDIT)
            with act.Fori(0, NIB) as it:
                for t in range(TI):
                    n = it * TI + t
                    act.wait_ge(turned, nth(n - 2))
                    if layer:
                        act.wait_ge(mixed, nth(n))
                        act.activation(k.h[:, t % 2, :], k.pre[0:NPART, t % 2, 0, :], ACT.Relu).then_inc(h_done, 1)
                    else:
                        act.activation(k.h[:, t % 2, :], k.xs[:, ds(n, 1), :].rearrange("p a d -> p (a d)"), ACT.Relu,
                                       bias=k.shift[:, ds(n, 1)], scale=k.rstd[:, ds(n, 1)]).then_inc(h_done, 1)
                    act.wait_ge(products_done, nth(n))
                    act.activation(k.table[:, ds(n, 1), :].rearrange("p a d -> p (a d)"), k.bank[2 + t % 2][0:NPART, 0:D],
                                   ACT.Copy, scale=k.dinv[:, ds(n, 1)]).then_inc(scaled, 1)

        @block.tensor
        def _(pe):
            for s in (turned, products_done, sum_turned):
                pe.sem_inc(s, CREDIT)
            with pe.Fori(0, NIB) as it:
                for t in range(TI):
                    n = it * TI + t
                    if layer:
                        pe.wait_ge(added, nth(n - 2))
                        pe.wait_ge(sum_copied, nth(n))
                        pe.transpose(k.bank[4 + t % 2][0:NPART, 0:D], k.sumT[0:D, t % 2, :], k.ident[0:D, 0:D])\
                          .then_inc(sum_turned, 1)
                    pe.wait_ge(h_done, nth(n))
                    pe.wait_ge(hT_done, nth(n - 2))
                    pe.transpose(k.bank[t % 2][0:D, 0:NPART], k.h[:, t % 2, :], k.ident[0:NPART, 0:NPART])\
                      .then_inc(turned, 1)
                    pe.wait_ge(hT_done, nth(n))
                    pe.wait_ge(scaled, nth(n - 2))
                    pe.matmul(k.bank[2 + t % 2][0:NPART, 0:D], k.hT[:, t % 2, :], k.w_gcn[:, layer, :],
                              start=True, stop=True).then_inc(products_done, 1)

        @block.gpsimd
        def _(pool):
            if layer:
                copy_sums(pool, k, by_tile, D, sum_turned, sum_copied, turns)
                pool.wait_ge(sum_copied, nth(NB - 1))
            pool.memset(k.aggT[:, :], 0.0).then_inc(cleared, 1)
            pool.wait_ge(cleared, 1)

        @block.sync
        def _(sp):
            with sp.Fori(0, NIB) as it:
                for half in range(2):
                    n = it * TI + half * HB
                    sp.wait_ge(scaled, nth(n + HB - 1))
                    sp.dma_start(tab[:, ds(n, HB), :], k.table[:, ds(n, HB), :]).then_inc(stored[half], 16)
            sp.wait_ge(stored0, NIB * 16)
            sp.wait_ge(stored1, NIB * 16)
    end_phase(nc, sems)


def mix(dve, k, n, t, layer, added, mixed):
    u = k.pre[0:NPART, t % 2, 0, :]
    dve.tensor_tensor(u, k.bank[4 + t % 2][0:NPART, 0:D], k.table[:, ds(n, 1), :].rearrange("p a d -> p (a d)"),
                      ALU.add).then_inc(added, 1)
    dve.wait_ge(added, nth(n))
    dve.scalar_tensor_tensor(u, u, k.dinv[:, ds(n, 1)], k.b_gcn[:, layer, :], ALU.mult, ALU.add).then_inc(mixed, 1)


def output_phase(nc, k, out):
    sems = named(nc, k, "sum_turned", "added", "mixed", "h_done", "out_done", "stored0", "stored1", "sum_copied",
                 "turns")
    sum_turned, added, mixed, h_done, out_done, stored0, stored1, sum_copied, turns = sems
    stored = (stored0, stored1)
    TI = 2 * HB
    by_tile = k.aggT[:, 0:N].rearrange("k (p b) -> k b p", b=NB)
    rows = out.rearrange("(p b) d -> p b d", b=NB)
    with nc.Block() as block:
        @block.tensor
        def _(pe):
            pe.sem_inc(sum_turned, CREDIT)
            with pe.Fori(0, NIB) as it:
                for t in range(TI):
                    n = it * TI + t
                    pe.wait_ge(added, nth(n - 2))
                    pe.wait_ge(sum_copied, nth(n))
                    pe.transpose(k.bank[4 + t % 2][0:NPART, 0:D], k.sumT[0:D, t % 2, :], k.ident[0:D, 0:D])\
                      .then_inc(sum_turned, 1)

        @block.gpsimd
        def _(pool):
            copy_sums(pool, k, by_tile, D, sum_turned, sum_copied, turns)

        @block.vector
        def _(dve):
            for s in (added, mixed, out_done):
                dve.sem_inc(s, CREDIT)
            with dve.Fori(0, NIB) as it:
                for t in range(TI):
                    n = it * TI + t
                    dve.wait_ge(sum_turned, nth(n))
                    dve.wait_ge(h_done, nth(n - 2))
                    mix(dve, k, n, t, 1, added, mixed)
                    dve.wait_ge(h_done, nth(n))
                    xt = k.xs[:, ds(n, 1), :].rearrange("p a d -> p (a d)")
                    dve.tensor_tensor(xt, xt, k.h[:, t % 2, :], ALU.add).then_inc(out_done, 1)

        @block.scalar
        def _(act):
            act.sem_inc(h_done, CREDIT)
            with act.Fori(0, NIB) as it:
                for t in range(TI):
                    n = it * TI + t
                    act.wait_ge(mixed, nth(n))
                    act.wait_ge(out_done, nth(n - 2))
                    act.activation(k.h[:, t % 2, :], k.pre[0:NPART, t % 2, 0, :], ACT.Relu).then_inc(h_done, 1)

        @block.sync
        def _(sp):
            with sp.Fori(0, NIB) as it:
                for half in range(2):
                    n = it * TI + half * HB
                    sp.wait_ge(out_done, nth(n + HB - 1))
                    sp.dma_start(rows[:, ds(n, HB), :], k.xs[:, ds(n, HB), :]).then_inc(stored[half], 16)
            sp.wait_ge(stored0, NIB * 16)
            sp.wait_ge(stored1, NIB * 16)


def gnn_kernel(nc, a, out):
    k = Kernel()
    k.sems = {}
    allocate(nc, k)
    load_phase(nc, k, a)
    window_phase(nc, k, a)
    place_windows(nc, k, 0)
    table_phase(nc, k)
    edge_stats_phase(nc, k)
    clear_sums(nc, k)
    all_windows(nc, k, "message", message_pass)
    message_norm_phase(nc, k)
    gcn_table_phase(nc, k, 0)
    all_windows(nc, k, "first", gcn_pass)
    gcn_table_phase(nc, k, 1)
    all_windows(nc, k, "second", gcn_pass)
    output_phase(nc, k, out)


def laid_out(inputs):
    a = {n: np.ascontiguousarray(v) for n, v in inputs.items()}

    def padded(v, fill, n=EP):
        return np.concatenate([v, np.full((n - v.shape[0],) + v.shape[1:], fill, v.dtype)])

    dst = padded(a["dst"], int(FAR))
    a["dst"] = dst
    a["dst_cols"] = np.ascontiguousarray(dst.reshape(NT, P).T)
    a["src"] = np.ascontiguousarray(padded(a["src"], 0, NCOL * P).reshape(NCOL, P).T)
    a["edge_weight"] = np.ascontiguousarray(padded(a["edge_weight"], 0).reshape(NT, P).T)
    a["edge_attr_4"] = np.ascontiguousarray(padded(a["edge_attr_4"], 0).T).reshape(P, DE * EP // P)
    return a


def kernel(**inputs):
    import concourse.bacc as bacc
    from concourse.bass_utils import run_bass_kernel_spmd

    nc = bacc.Bacc("TRN2", target_bir_lowering=False, num_devices=1)
    arrays, args = {}, {}
    for name, v in laid_out(inputs).items():
        arrays[f"in_{name}"] = v
        args[name] = nc.dram_tensor(f"in_{name}", v.shape, mybir.dt.from_np(v.dtype), kind="ExternalInput").ap()
    out = nc.dram_tensor("out", (N, D), F32, kind="ExternalOutput").ap()
    gnn_kernel(nc, args, out)
    r = run_bass_kernel_spmd(nc, [arrays], core_ids=[0])
    return r.results[0]["out"]
```

```python
import numpy as np
import concourse.bass as bass
from concourse import mybir

ALU = mybir.AluOpType
ACT = mybir.ActivationFunctionType
AX = mybir.AxisListType
F32 = mybir.dt.float32
BF16 = mybir.dt.bfloat16
I32 = mybir.dt.int32
ds = bass.ds

N, D, E, DE = 6250, 96, 106250, 4
EPS = 1e-5
P = 128

TQ, QC, RC = 4, 4, 4
QE = TQ * P
NCH = -(-E // (QE * QC * RC)) * RC
NQ = NCH * QC
NT = NQ * TQ
EP = NT * P
NIT = NCH // RC
QR = QC * RC
TR = QR * TQ
CT = QC * TQ
LASTV = E - (NQ - 1) * QE
QB = NQ // 2
NCOL = NT + TR

W = 64
ROUNDS = -(-N // W)
FAR = float(1 << 20)
CLIP = 200.0

NB, NPART = 50, 125
HB = 5
NIB = NB // (2 * HB)
HALVES = ((0, 3), (3, HB))
NPAD = N + W

NS = 3
KS = NS * NS * DE
CREDIT = QR


def nth(n):
    return n + 1 + CREDIT


class Kernel:
    pass


def allocate(nc, k):
    def sb(name, shape, dt=F32):
        return nc.alloc_sbuf_tensor(name, shape, dt)

    k.ident = sb("ident", [P, P])
    k.iota = sb("iota", [P, W])
    k.node_of_row = sb("node_of_row", [P, 1])
    k.ones = sb("ones", [P, 1])
    k.eps = sb("eps", [P, 1])
    k.zeros = sb("zeros", [W, NS * D], BF16)
    k.xs = sb("xs", [NPART, NB, D])
    k.nfT = sb("nfT", [P, N])
    k.aggT = sb("aggT", [P, NPAD])
    k.tables = sb("tables", [NPART, NB, 2, D])
    k.gathered = sb("gathered", [P, TR, D])
    k.src_cols = sb("src_cols", [P, NCOL], I32)
    k.src_stage = sb("src_stage", [P, TR], I32)
    k.edge_cols = sb("edge_cols", [P, NT, 2])
    k.rel_cols = sb("rel_cols", [P, NQ, TQ])
    k.rel_rows = sb("rel_rows", [QB, 2, QE])
    k.rel_clip = sb("rel_clip", [QB, 2, QE], BF16)
    k.base_q = sb("base_q", [QB, 2])
    k.base_all = sb("base_all", [P, NQ])
    k.base_int = sb("base_int", [1, NQ], I32)
    k.span = sb("span", [QB, 2])
    k.flag = sb("flag", [1, 1], I32)
    k.w12 = sb("w12", [P, 2 * D])
    k.w_node = sb("w_node", [P, D])
    k.w3 = sb("w3", [P, D])
    k.w3e = sb("w3e", [P, D])
    k.w_gcn = sb("w_gcn", [P, 2, D])
    k.w_edge = sb("w_edge", [DE, D])
    k.w_edge_parts = sb("w_edge_parts", [DE, NS, D], BF16)
    k.w_edge_stack = sb("w_edge_stack", [KS, D], BF16)
    k.cols = sb("cols", [D, 16])
    k.b_gcn = sb("b_gcn", [NPART, 2, D])
    k.b_msg_row = sb("b_msg_row", [P, D])
    k.sq_sum = sb("sq_sum", [1, D])
    k.dinv = sb("dinv", [NPART, NB])
    k.rstd = sb("rstd", [NPART, NB])
    k.shift = sb("shift", [NPART, NB])
    k.stats = sb("stats", [NPART, NB, 6])
    k.small = sb("small", [NPART, 4, NB])
    k.deg = sb("deg", [NPART, 3, NB])
    k.edge_stats = sb("edge_stats", [D, NQ, 6])
    k.node_stats = sb("node_stats", [D, 2 * NIB * 2, 6])
    k.aff = sb("aff", [D, 24])
    k.aff_lhs = sb("aff_lhs", [D, 2, P])
    k.aff_msg = sb("aff_msg", [P, D + 1])
    k.aff_node = sb("aff_node", [P, D + 1])
    ring = k.gathered[:, :, :].rearrange("p t d -> p (t d)")
    hT_at = TR * D - 2 * HB * NPART
    k.hT = ring[:, hT_at:].rearrange("p (a b c) -> p a b c", a=2, b=HB)
    k.h = ring[0:NPART, hT_at - 2 * HB * D:hT_at].rearrange("p (a b c) -> p a b c", a=2, b=HB)

    FW = DE * EP // P
    work = sb("work", [P, 9232])
    k.edge_raw = work[:, 0:FW]
    k.edge_parts = work[:, FW:FW + NS * FW // 2].bitcast(BF16).rearrange("p (s w) -> p s w", s=NS)
    at = [0]

    def view(shape, dt=F32, parts=P):
        words = int(np.prod(shape)) // (1 if dt == F32 else 2)
        v = work[0:parts, at[0]:at[0] + words]
        at[0] += words
        letters = "abcd"[:len(shape)]
        sizes = {x: n for x, n in zip(letters, shape)}
        return (v if dt == F32 else v.bitcast(dt)).rearrange(f"p ({' '.join(letters)}) -> p {' '.join(letters)}", **sizes)

    k.estack = view([2, QC * QE], BF16, KS)
    k.edgeT = view([2, QE])
    passes_at = at[0]
    k.drow = view([2, QC * QE], BF16)
    k.p2w = view([2 * QC, 2 * D], BF16)
    k.onehotT = view([2, QE], BF16)
    k.onehot = view([2, TQ, W])
    k.pre = view([2, TQ, D])
    k.msg = view([2, TQ, D + 2])
    k.msg_sq = view([2, TQ, D])
    k.edgeT_more = work[:, at[0] - 2 * QE:at[0]].rearrange("p (a e) -> p a e", a=2)
    at[0] = passes_at
    k.p2_room = view([2, NB // XL * NS * D], BF16, NPART)
    at[0] = 0
    k.sumT = view([2, HB, NPART])
    k.nodeT = view([2, HB, NPART])
    k.mix_room = view([2, HB, D], parts=NPART)

    k.bank = [nc.alloc_psum_tensor(f"bank{i}", [P, 512], F32) for i in range(8)]
    k.gather_tab = nc.dram_tensor("gather_tab", [N, D], F32).ap()
    k.p2_tab = nc.dram_tensor("p2_tab", [NPAD, NS * D], BF16).ap()
    k.edge_tab = nc.dram_tensor("edge_tab", [NS * DE, EP], BF16).ap()
    k.rel_tab = nc.dram_tensor("rel_tab", [NQ, QE], BF16).ap()
    k.base_tab = nc.dram_tensor("base_tab", [2, QB], F32).ap()


def end_phase(nc, sems):
    nc.all_engine_barrier()
    for s in sems:
        nc.gpsimd.sem_clear(s)
    nc.all_engine_barrier()


def named(nc, k, *names):
    for n in names:
        if n not in k.sems:
            k.sems[n] = nc.alloc_semaphore(n)
    return [k.sems[n] for n in names]


def linker(eng, sem):
    n = [0]

    def link(ins):
        n[0] += 1
        ins.then_inc(sem, 1)
        eng.wait_ge(sem, n[0])
    return link


COLUMNS = ("L0_gnn_b_node", "L0_gnn_g_node", "L0_gnn_beta_node", "L0_gnn_b_edge", "L0_gnn_g_edge",
           "L0_gnn_beta_edge", "L0_gnn_g_msg", "L0_gnn_beta_msg")


def col(k, name):
    i = COLUMNS.index(name)
    return k.cols[:, i:i + 1]


def clip_windows(dve, link, k, clipped):
    link(dve.tensor_scalar(k.rel_clip[:, :, :], k.rel_rows[:, :, :], CLIP, -1.0, ALU.min, ALU.max))
    dve.sem_inc(clipped, 1)
    link(dve.tensor_scalar(k.base_int[:, :], k.base_all[0:1, :], float(N), None, ALU.min))
    rel = k.rel_cols[:, :, :].rearrange("p q j -> p (q j)")
    inside = k.edge_cols[:, :, 0]
    link(dve.tensor_scalar(inside, rel, 0.0, None, ALU.is_ge))
    link(dve.scalar_tensor_tensor(inside, rel, float(W), inside, ALU.is_lt, ALU.mult))


def move_windows(nc, k, move):
    sems = named(nc, k, "move_link", "move_clipped", "move_stored")
    link_sem, clipped, stored = sems
    with nc.Block() as block:
        @block.vector
        def _(dve):
            link = linker(dve, link_sem)
            link(dve.tensor_scalar(k.rel_rows[:, :, :], k.rel_rows[:, :, :], float(-move), None, ALU.add))
            link(dve.tensor_scalar(k.rel_cols[:, :, :], k.rel_cols[:, :, :], float(-move), None, ALU.add))
            link(dve.tensor_scalar(k.base_all[:, :], k.base_all[:, :], float(move), None, ALU.add))
            clip_windows(dve, link, k, clipped)

        @block.sync
        def _(sp):
            sp.wait_ge(clipped, 1)
            sp.dma_start(k.rel_tab.rearrange("(b q) e -> q b e", b=2), k.rel_clip[:, :, :]).then_inc(stored, 16)
            sp.wait_ge(stored, 16)
    end_phase(nc, sems)


def affine(dve, link, k, o, what):
    c = k.aff
    link(dve.reciprocal(c[:, o + 3:o + 4], c[:, o + 2:o + 3]))
    link(dve.tensor_tensor(c[:, o + 4:o + 5], c[:, o + 3:o + 4], col(k, f"L0_gnn_g_{what}"), ALU.mult))
    link(dve.tensor_tensor(c[:, o + 5:o + 6], c[:, o:o + 1], c[:, o + 4:o + 5], ALU.mult))
    link(dve.tensor_tensor(c[:, o + 5:o + 6], col(k, f"L0_gnn_beta_{what}"), c[:, o + 5:o + 6], ALU.subtract))


def layernorm_sums(dve, link, k):
    st = k.stats[:, :, :]
    m0, m1, v0, v1 = st[:, :, 1], st[:, :, 4], st[:, :, 2], st[:, :, 5]
    mean, half, var = k.small[:, 0, :], k.small[:, 1, :], k.small[:, 2, :]
    dve.tensor_tensor(mean, m0, m1, ALU.add)
    dve.tensor_tensor(var, v0, v1, ALU.add)
    link(dve.tensor_tensor(half, m0, m1, ALU.subtract))
    link(dve.scalar_tensor_tensor(half, half, 0.25, half, ALU.mult, ALU.mult))
    link(dve.scalar_tensor_tensor(var, var, 1.0 / D, half, ALU.mult, ALU.add))


def layernorm_map(dve, link, k):
    link(dve.reciprocal(k.rstd[:, :], k.small[:, 3, :]))
    link(dve.scalar_tensor_tensor(k.shift[:, :], k.small[:, 0, :], -0.5, k.rstd[:, :], ALU.mult, ALU.mult))


def tile_of(t, n):
    return t[:, ds(n, 1), :].rearrange("p a d -> p (a d)")


def half_turns(eng, step):
    with eng.Fori(0, NIB - 1) as it:
        for half in range(2):
            step(it * 2 + half, half, True)
    for half in range(2):
        step((NIB - 1) * 2 + half, half, False)


def normal_rows(act, k, g, half, turned, h_done):
    act.wait_ge(turned, nth(g - 2))
    for t in range(HB):
        n = g * HB + t
        ins = act.activation(k.h[:, half, t, :], tile_of(k.xs, n), ACT.Relu,
                             bias=k.shift[:, ds(n, 1)], scale=k.rstd[:, ds(n, 1)])
    ins.then_inc(h_done, 1)


def turn_rows(pe, k, bank, g, half, h_done, hT_done, turned):
    pe.wait_ge(h_done, nth(g))
    pe.wait_ge(hT_done, nth(g - 1))
    for i, (lo, hi) in enumerate(HALVES):
        for t in range(lo, hi):
            ins = pe.transpose(k.bank[bank + i][0:D, (t - lo) * NPART:(t - lo + 1) * NPART], k.h[:, half, t, :],
                               k.ident[0:NPART, 0:NPART])
    ins.then_inc(turned, 1)


def columns_out(dve, k, bank, g, half, turned, products_done, hT_done):
    dve.wait_ge(turned, nth(g))
    dve.wait_ge(products_done, nth(g - 2))
    for i, (lo, hi) in enumerate(HALVES):
        ins = dve.tensor_copy(k.hT[0:D, half, lo:hi, :].rearrange("p t n -> p (t n)"),
                              k.bank[bank + i][0:D, 0:(hi - lo) * NPART])
    ins.then_inc(hT_done, 1)


XL = 5
SB = 4


def first_phase(nc, k, a, ring):
    names = ("cleared", "consts_ready", "sums_cleared", "pool_link", "dve_link", "dst_landed", "src_landed",
             "edge_landed", "early_landed", "weights_landed", "base_ready", "base_stored", "base_back", "span_ready",
             "span_turned", "clipped", "rel_stored", "var_ready", "root_done", "norm_ready", "h_done", "turned",
             "hT_done", "w12_done", "products_done", "copied", "nf_done", "tab_stored0", "tab_stored1", "edge_part", "edge_rest",
             "parts_stored", "stack_ready", "flag_done", "rows_landed_a", "rows_landed_b", "edge_mm", "edge_act", "edge_stat",
             "edge_var", "edge_root", "shift_ready", "shift_done", "w3e_ready", "buffers_ready",
             "p2_link", "cols_ready")
    sems = named(nc, k, *names)
    (cleared, consts_ready, sums_cleared, pool_link, dve_link, dst_landed, src_landed,
     edge_landed, early_landed, weights_landed, base_ready, base_stored, base_back, span_ready,
     span_turned, clipped, rel_stored, var_ready, root_done, norm_ready, h_done, turned,
     hT_done, w12_done, products_done, copied, nf_done, tab_stored0, tab_stored1, edge_part, edge_rest,
     parts_stored, stack_ready, flag_done, rows_landed_a, rows_landed_b, edge_mm, edge_act, edge_stat,
     edge_var, edge_root, shift_ready, shift_done, w3e_ready, buffers_ready,
     p2_link, cols_ready) = sems
    p2_stored = [nc.alloc_semaphore(f"p2_stored{i}") for i in range(2)]
    x_landed = named(nc, k, *[f"x_landed{i}" for i in range(XL)])
    landed, tab_stored = (rows_landed_a, rows_landed_b), (tab_stored0, tab_stored1)
    message = MessagePass(nc, k, ring)

    NI, CI = NCH // 2, 2
    QI = CI * QC
    FW = DE * EP // P
    room = k.gathered[:, :, :].rearrange("p t d -> p (t d)")
    dst_q = room[0:QB, 0:2 * QE].bitcast(I32).rearrange("p (b e) -> p b e", b=2)
    spans = room[0:QB, 2 * QE:4 * QE].rearrange("p (b e) -> p b e", b=2)
    dst_p = room[:, 4 * QE:4 * QE + NT].bitcast(I32)
    weight_p = room[:, 4 * QE + NT:4 * QE + 2 * NT]
    span_row = k.bank[5][0:1, 0:QB]
    tab = k.gather_tab.rearrange("(p b) d -> p b d", b=NB)
    p2 = k.p2_tab[0:N, :].rearrange("(p b) d -> p b d", b=NB)
    XB = NB // XL

    with nc.Block() as block:
        @block.sync
        def _(sp):
            sp.dma_start(dst_q, a["dst"].rearrange("(b q e) -> q b e", b=2, e=QE)).then_inc(dst_landed, 16)
            sp.dma_start(dst_p, a["dst_cols"]).then_inc(dst_landed, 16)
            sp.dma_start(weight_p, a["edge_weight"]).then_inc(dst_landed, 16)
            sp.dma_start(k.edge_raw, a["edge_attr_4"]).then_inc(edge_landed, 16)
            sp.dma_start(k.w_edge[:, :], a["L0_gnn_W_edge"]).then_inc(edge_landed, 16)
            xr = a["x"].rearrange("(p b) d -> p b d", b=NB)
            for i in range(XL):
                sp.dma_start(k.xs[:, i * XB:(i + 1) * XB, :], xr[:, i * XB:(i + 1) * XB, :]).then_inc(x_landed[i], 16)
            sp.wait_ge(cleared, 1)
            wm = a["L0_gnn_W_msg"]
            early = [(k.w12[0:D, 0:D], wm[0:D, :]), (k.w12[0:D, D:2 * D], wm[D:2 * D, :]),
                     (k.w_node[0:D, :], a["L0_gnn_W_node"])]
            early += [(k.cols[:, i:i + 1], a[name].unsqueeze(1)) for i, name in enumerate(COLUMNS)]
            for dst, src in early:
                sp.dma_start(dst, src).then_inc(early_landed, 16)
            sp.dma_start(k.src_cols[:, :], a["src"]).then_inc(src_landed, 16)
            for b in range(2):
                sp.wait_ge(base_ready, 1)
                sp.dma_start(k.base_tab[b].unsqueeze(1), k.base_q[:, b:b + 1]).then_inc(base_stored, 16)
            sp.wait_ge(base_stored, 32)
            sp.dma_start(k.base_all[:, :], k.base_tab.rearrange("b q -> (b q)").unsqueeze(0).broadcast_to([P, NQ]))\
              .then_inc(base_back, 16)
            late = [(k.b_msg_row[D:D + 1, :], a["L0_gnn_b_msg"].unsqueeze(0)),
                    (k.w3[0:D, :], wm[2 * D:3 * D, :]), (k.w_gcn[0:D, 0, :], a["L1_gnn_W1"]),
                    (k.w_gcn[0:D, 1, :], a["L1_gnn_W2"]), (k.p2_tab[N:NPAD, :], k.zeros[:, :])]
            late += [(k.b_gcn[:, i, :], a[name].unsqueeze(0).broadcast_to([NPART, D]))
                     for i, name in enumerate(("L1_gnn_b1", "L1_gnn_b2"))]
            for dst, src in late:
                sp.dma_start(dst, src).then_inc(weights_landed, 16)
            for i in range(NS):
                sp.wait_ge(edge_part, i + 1)
                rows = k.edge_tab[i * DE:(i + 1) * DE, :].rearrange("c (w f) -> (c w) f", f=FW)
                sp.dma_start(rows, k.edge_parts[:, i, :]).then_inc(parts_stored, 16)
                for j in range(NS):
                    r = (i * NS + j) * DE
                    sp.dma_start(k.w_edge_stack[r:r + DE, :], k.w_edge_parts[:, i, :]).then_inc(stack_ready, 16)
            with sp.Fori(0, NIB) as it:
                for half in range(2):
                    g = it * 2 + half
                    sp.wait_ge(copied, nth(g))
                    sp.dma_start(tab[:, ds(g * HB, HB), :], k.tables[:, ds(g * HB, HB), 0, :])\
                        .then_inc(tab_stored[half], 16)
            sp.wait_ge(clipped, 1)
            sp.dma_start(k.rel_tab.rearrange("(b q) e -> q b e", b=2), k.rel_clip[:, :, :]).then_inc(rel_stored, 16)
            sp.wait_ge(parts_stored, 16 * NS)
            with sp.Fori(0, NI) as it:
                for c in range(CI):
                    sp.wait_ge(edge_mm, nth(it * QI + (c - 2) * QC + QC - 1))
                    load_stack(sp, k, c, it * CI + c).then_inc(landed[c], 16)
            for i in range(2):
                sp.wait_ge(p2_stored[i], 16 * len(range(i, XL, 2)))
            sp.wait_ge(weights_landed, 16 * len(late))
            sp.wait_ge(rel_stored, 16)
            message.sync(sp)

        @block.gpsimd
        def _(pool):
            link = linker(pool, pool_link)
            for t in (k.w12, k.w_node, k.w3, k.w3e):
                pool.memset(t[:, :], 0.0)
            pool.memset(k.w_gcn[:, :, :], 0.0)
            link(pool.memset(k.zeros[:, :], 0.0))
            pool.sem_inc(cleared, 1)
            pool.memset(k.eps[:, :], EPS)
            link(pool.memset(k.ident[:, :], 0.0))
            link(pool.affine_select(out=k.ident[:, :], in_=k.ident[:, :], compare_op=ALU.not_equal, fill=1.0,
                                    base=0, pattern=[[-1, P]], channel_multiplier=1))
            pool.sem_inc(consts_ready, 1)
            pool.wait_ge(dst_landed, 48)
            pool.tensor_copy(k.rel_cols[:, :, :].rearrange("p q j -> p (q j)"), dst_p).then_inc(cols_ready, 1)
            pool.tensor_copy(k.edge_cols[:, :, 1], weight_p).then_inc(cols_ready, 1)
            link(pool.iota(k.iota[:, :], [[1, W]], 0, 0, allow_small_or_imprecise_dtypes=True))
            for r in range(P // W):
                link(pool.iota(k.node_of_row[r * W:(r + 1) * W, :], [[0, 1]], 0, 1, allow_small_or_imprecise_dtypes=True))
            for t in (k.ones[:, :],):
                link(pool.memset(t, 1.0))
            for t in (k.sq_sum[:, :], k.aff_lhs[:, :, :], k.aff_node[:, :], k.nfT[D:P, :]):
                link(pool.memset(t, 0.0))
            link(pool.memset(k.nfT[D:D + 1, :], 1.0))
            link(pool.memset(k.aggT[:, :], 0.0))
            pool.sem_inc(sums_cleared, 1)
            for i in range(NS - 1):
                pool.wait_ge(edge_part, i + 1)
                pool.tensor_tensor(k.w_edge[:, :], k.w_edge[:, :], k.w_edge_parts[:, i, :], ALU.subtract)\
                    .then_inc(edge_rest, 1)
                pool.tensor_tensor(k.edge_raw, k.edge_raw, k.edge_parts[:, i, :], ALU.subtract).then_inc(edge_rest, 1)
            pool.wait_ge(edge_rest, 2 * (NS - 1))
            edge_parts(k, pool.tensor_copy, NS - 1).then_inc(edge_part, 1)
            for s in tab_stored:
                pool.wait_ge(s, 16 * NIB)
            pool.wait_ge(products_done, nth(2 * NIB - 1))

            def target_parts():
                plink = linker(pool, p2_link)
                pool.wait_ge(copied, nth(2 * NIB - 1))
                pool.wait_ge(parts_stored, 16 * NS)
                for i in range(XL):
                    if i >= 2:
                        pool.wait_ge(p2_stored[i % 2], 16 * (i // 2))
                    piece = p2_piece(k, i % 2)
                    rest = k.tables[:, i * XB:(i + 1) * XB, 1, :]
                    for s, at in ((0, 0), (1, 2), (2, 1)):
                        plink(pool.tensor_copy(piece[:, :, at, :], rest))
                        if s < NS - 1:
                            plink(pool.tensor_tensor(rest, rest, piece[:, :, at, :], ALU.subtract))
                    pool.dma_start(p2[:, i * XB:(i + 1) * XB, :], piece.rearrange("p t s d -> p t (s d)"))\
                        .then_inc(p2_stored[i % 2], 16)

            message.gpsimd(pool, target_parts)

        @block.tensor
        def _(pe):
            for s in (turned, w12_done, products_done):
                pe.sem_inc(s, CREDIT)
            pe.wait_ge(consts_ready, 1)
            pe.wait_ge(span_ready, 1)
            pe.transpose(span_row, k.span[:, 0:1], k.ident[0:QB, 0:QB]).then_inc(span_turned, 1)
            pe.wait_ge(early_landed, 16 * (3 + len(COLUMNS)))

            def turn(g, half):
                turn_rows(pe, k, 0, g, half, h_done, hT_done, turned)

            def products(g, half, more):
                if more or half == 0:
                    turn(g + 1, 1 - half)
                pe.wait_ge(hT_done, nth(g))
                pe.wait_ge(copied, nth(g - 1))
                for t in range(HB):
                    ins = pe.matmul(k.bank[2 + t // 2][0:NPART, (t % 2) * 2 * D:(t % 2 + 1) * 2 * D],
                                    k.hT[:, half, t, :], k.w12[:, :], start=True, stop=True)
                ins.then_inc(w12_done, 1)
                pe.wait_ge(nf_done, nth(g - 1))
                for i, (lo, hi) in enumerate(HALVES):
                    ins = pe.matmul(k.bank[6 + i][0:D, 0:(hi - lo) * NPART], k.w_node[:, :],
                                    k.hT[:, half, lo:hi, :].rearrange("p t n -> p (t n)"), start=True, stop=True)
                ins.then_inc(products_done, 1)

            turn(0, 0)
            half_turns(pe, products)
            pe.sem_inc(edge_mm, CREDIT)
            pe.wait_ge(stack_ready, 16 * NS * NS)
            pe.wait_ge(hT_done, nth(2 * NIB - 1))
            pe.wait_ge(copied, nth(2 * NIB - 1))
            with pe.Fori(0, NI) as it:
                for q in range(QI):
                    n = it * QI + q
                    if q % QC == 0:
                        pe.wait_ge(landed[q // QC], it * 16 + 16)
                    pe.wait_ge(edge_act, nth(n - SB))
                    pe.matmul(k.bank[q % SB][0:D, :], k.w_edge_stack[:, :],
                              k.estack[:, q // QC, (q % QC) * QE:(q % QC + 1) * QE], start=True, stop=True)\
                      .then_inc(edge_mm, 1)
            pe.wait_ge(shift_ready, 1)
            pe.matmul(k.bank[2][:, 0:D], k.aff_lhs[:, 0, :], k.w3[0:D, :], start=True, stop=True).then_inc(shift_done, 1)
            pe.wait_ge(w3e_ready, 1)
            pe.wait_ge(flag_done, 1)
            pe.wait_ge(nf_done, nth(2 * NIB - 1))
            message.tensor(pe)

        @block.scalar
        def _(act):
            act.wait_ge(src_landed, 16)
            message.stage_first(act)
            for s in (h_done, copied):
                act.sem_inc(s, CREDIT)
            act.wait_ge(edge_landed, 32)
            edge_parts(k, act.copy, 0).then_inc(edge_part, 1)
            act.wait_ge(var_ready, 1)
            act.wait_ge(consts_ready, 1)
            act.activation(k.small[:, 3, :], k.small[:, 2, :], ACT.Sqrt, bias=k.eps[0:NPART, :]).then_inc(root_done, 1)
            act.wait_ge(norm_ready, 1)

            def copy_out(g, half, more):
                if more:
                    normal_rows(act, k, g + 2, half, turned, h_done)
                act.wait_ge(w12_done, nth(g))
                for b in range(-(-HB // 2)):
                    tiles = min(2, HB - 2 * b)
                    ins = act.copy(k.tables[:, ds(g * HB + 2 * b, tiles), :, :].rearrange("p a s d -> p (a s d)"),
                                   k.bank[2 + b][0:NPART, 0:tiles * 2 * D])
                ins.then_inc(copied, 1)

            for half in range(2):
                normal_rows(act, k, half, half, turned, h_done)
            half_turns(act, copy_out)
            act.sem_inc(edge_act, CREDIT)
            with act.Fori(0, NI) as it:
                for q in range(QI):
                    n = it * QI + q
                    act.wait_ge(edge_mm, nth(n))
                    act.wait_ge(edge_stat, nth(n - SB))
                    act.activation(edge_buffer(k, q), k.bank[q % SB][0:D, :], ACT.Relu,
                                   bias=col(k, "L0_gnn_b_edge")).then_inc(edge_act, 1)
            act.wait_ge(edge_var, 1)
            act.activation(k.aff[:, 2:3], k.aff[:, 1:2], ACT.Sqrt, bias=k.eps[0:D, :]).then_inc(edge_root, 1)
            act.wait_ge(buffers_ready, 1)
            message.scalar(act)

        @block.vector
        def _(dve):
            link = linker(dve, dve_link)
            message.credit(dve)
            dve.memset(k.hT[D:P, :, :, :], 0.0).then_inc(hT_done, CREDIT)
            dve.wait_ge(dst_landed, 48)
            link(dve.tensor_copy(k.rel_rows[:, :, :], dst_q))
            link(dve.tensor_reduce(k.base_q[:, :], k.rel_rows[:, :, :], AX.X, ALU.min))
            dve.sem_inc(base_ready, 1)
            link(dve.tensor_tensor(k.rel_rows[:, :, :], k.rel_rows[:, :, :],
                                   k.base_q[:, :].unsqueeze(2).broadcast_to([QB, 2, QE]), ALU.subtract))
            link(dve.scalar_tensor_tensor(spans, k.rel_rows[:, :, :], FAR / 2, k.rel_rows[:, :, :], ALU.is_lt, ALU.mult))
            link(dve.tensor_reduce(k.span[:, 0:1], spans, AX.XY, ALU.max))
            dve.sem_inc(span_ready, 1)
            for b in range(NB):
                if b % XB == 0:
                    dve.wait_ge(x_landed[b // XB], 16)
                ins = dve.bn_stats(k.stats[:, b, :], k.xs[:, b, :])
            link(ins)
            layernorm_sums(dve, link, k)
            dve.sem_inc(var_ready, 1)
            dve.wait_ge(root_done, 1)
            layernorm_map(dve, link, k)
            dve.sem_inc(norm_ready, 1)
            dve.sem_inc(nf_done, CREDIT)
            dve.wait_ge(early_landed, 16 * (3 + len(COLUMNS)))
            dve.wait_ge(consts_ready, 1)

            def nodes(g, half, more):
                if more or half == 0:
                    columns_out(dve, k, 0, g + 1, 1 - half, turned, products_done, hT_done)
                dve.wait_ge(products_done, nth(g))
                for i, (lo, hi) in enumerate(HALVES):
                    w = (hi - lo) * NPART
                    ins = dve.tensor_scalar(k.nfT[0:D, ds((g * HB + lo) * NPART, w)], k.bank[6 + i][0:D, 0:w],
                                            col(k, "L0_gnn_b_node"), 0.0, ALU.add, ALU.max)
                ins.then_inc(nf_done, 1)
                dve.wait_ge(nf_done, nth(g))
                for i, (lo, hi) in enumerate(HALVES):
                    dve.bn_stats(tile_of(k.node_stats, g * 2 + i),
                                 k.nfT[0:D, ds((g * HB + lo) * NPART, (hi - lo) * NPART)])

            columns_out(dve, k, 0, 0, 0, turned, products_done, hT_done)
            dve.wait_ge(edge_rest, 2)
            edge_parts(k, dve.tensor_copy, 1).then_inc(edge_part, 1)
            half_turns(dve, nodes)
            dve.wait_ge(base_back, 16)
            dve.wait_ge(cols_ready, 2)
            link(dve.tensor_tensor(k.rel_cols[:, :, :], k.rel_cols[:, :, :],
                                   k.base_all[:, :].unsqueeze(2).broadcast_to([P, NQ, TQ]), ALU.subtract))
            clip_windows(dve, link, k, clipped)
            dve.wait_ge(span_turned, 1)
            link(dve.tensor_reduce(k.span[0:1, 1:2], span_row, AX.X, ALU.max))
            link(dve.tensor_scalar(k.flag[:, :], k.span[0:1, 1:2], float(W), None, ALU.is_ge))
            dve.sem_inc(flag_done, 1)
            dve.wait_ge(parts_stored, 16 * NS)
            link(dve.memset(k.edgeT[D:P, :, :], 0.0))
            link(dve.memset(k.edgeT[D:D + 1, :, :], 1.0))
            dve.sem_inc(edge_stat, CREDIT)
            with dve.Fori(0, NI) as it:
                for q in range(QI):
                    n = it * QI + q
                    dve.wait_ge(edge_act, nth(n))
                    dve.bn_stats(tile_of(k.edge_stats, n), edge_buffer(k, q)).then_inc(edge_stat, 1)
            dve.wait_ge(edge_stat, nth(NQ - 1))
            link(dve.bn_stats(k.edge_stats[:, NQ - 1, :], edge_buffer(k, NQ - 1)[:, 0:LASTV]))
            dve.sem_inc(buffers_ready, 1)
            link(dve.bn_aggr(k.aff[:, 0:2], k.edge_stats[:, :, :].rearrange("p a b -> p (a b)")))
            dve.sem_inc(edge_var, 1)
            dve.wait_ge(edge_root, 1)
            affine(dve, link, k, 0, "edge")
            dve.wait_ge(sums_cleared, 1)
            dve.wait_ge(weights_landed, 16 * 7)
            link(dve.tensor_copy(k.aff_lhs[:, 0, D:D + 1], k.aff[:, 5:6]))
            dve.sem_inc(shift_ready, 1)
            link(dve.tensor_scalar(k.w3e[0:D, :], k.w3[0:D, :], k.aff[:, 4:5], None, ALU.mult))
            dve.wait_ge(shift_done, 1)
            link(dve.tensor_tensor(k.w3e[D:D + 1, :], k.bank[2][D:D + 1, 0:D], k.b_msg_row[D:D + 1, :], ALU.add))
            dve.sem_inc(w3e_ready, 1)
            message.vector(dve)
    end_phase(nc, sems + x_landed + message.sems)


def load_stack(sp, k, room, chunk):
    return sp.dma_start(k.estack[:, room, :], k.edge_tab[:, ds(chunk * QC * QE, QC * QE)].unsqueeze(0)
                        .broadcast_to([NS, NS * DE, QC * QE]))


def edge_parts(k, copy, i):
    copy(k.w_edge_parts[:, i, :], k.w_edge[:, :])
    return copy(k.edge_parts[:, i, :], k.edge_raw)


def edge_buffer(k, q):
    return (k.edgeT if q % SB < 2 else k.edgeT_more)[0:D, q % 2, :]


def p2_piece(k, i):
    return k.p2_room[:, i, :].rearrange("p (t s d) -> p t s d", t=NB // XL, s=NS)


def gather_rows(pool, k, ring, staged, used, turns, first_turn_then=None):
    def turn(it):
        for c in range(RC):
            pool.wait_ge(staged, it * RC + c + 1)
            pool.wait_ge(used, nth(it * QR + c * QC + QC - 1 - QR))
            pool.sem_inc(turns, 1)
            for t in range(c * CT, (c + 1) * CT):
                pool.indirect_dma_start(k.gathered[:, t, :], None, k.gather_tab,
                                        bass.IndirectOffsetOnAxis(ap=k.src_stage[:, t:t + 1], axis=0))\
                    .then_inc(ring[c], 16)

    if first_turn_then:
        turn(0)
        first_turn_then()
    with pool.Fori(1 if first_turn_then else 0, NIT) as it:
        turn(it)
    for c in range(RC):
        pool.wait_ge(ring[c], NIT * 16 * QC * TQ)


def stage_first(act, k, staged):
    for c in range(RC):
        act.copy(k.src_stage[:, c * CT:(c + 1) * CT], k.src_cols[:, c * CT:(c + 1) * CT]).then_inc(staged, 1)


def stage_next(act, k, it, c, ring, staged):
    act.wait_ge(ring[c], it * (16 * CT) + 16 * CT)
    act.copy(k.src_stage[:, c * CT:(c + 1) * CT], k.src_cols[:, ds((it + 1) * TR + c * CT, CT)]).then_inc(staged, 1)


def window_bases(eng, k, it, c):
    return [eng.value_load(k.base_int[0:1, ds(it * QR + c * QC + q, 1)], min_val=0, max_val=N) for q in range(QC)]


class MessagePass:

    def __init__(self, nc, k, ring):
        self.k, self.ring = k, ring
        self.sems = named(nc, k, "staged", "turns", "add_done", "edge_product", "edge_relu",
                          "onehotT_done", "onehot_done", "pre_done", "relu_done", "square_done", "seg_done", "sum_done",
                 "rows_landed0", "rows_landed1", "est_landed0", "est_landed1", "p2_landed0", "p2_landed1")
        (self.staged, self.turns, self.add_done, self.edge_product, self.edge_relu, self.onehotT_done,
         self.onehot_done, self.pre_done, self.relu_done, self.square_done, self.seg_done, self.sum_done) = self.sems[0:12]
        self.rows_landed, self.est_landed, self.p2_landed = self.sems[12:14], self.sems[14:16], self.sems[16:18]

    def gpsimd(self, pool, first_turn_then=None):
        gather_rows(pool, self.k, self.ring, self.staged, self.add_done, self.turns, first_turn_then)

    def sync(self, sp):
        k, ring = self.k, self.ring
        with sp.Fori(0, NIT) as it:
            for c in range(RC):
                last = it * QR + (c - 2) * QC + QC - 1
                i = it * RC + c
                sp.wait_ge(self.edge_product, nth(last))
                load_stack(sp, k, c % 2, i).then_inc(self.est_landed[c % 2], 16)
                sp.wait_ge(self.onehotT_done, nth(last))
                sp.dma_start(k.drow[:, c % 2, :], k.rel_tab[ds(i * QC, QC), :].rearrange("q e -> (q e)")
                             .unsqueeze(0).broadcast_to([P, QC * QE])).then_inc(self.rows_landed[c % 2], 16)
                bases = window_bases(sp, k, it, c)
                sp.wait_ge(self.pre_done, nth(last))
                for q in range(QC):
                    slot = (c % 2) * QC + q
                    sp.dma_start(k.p2w[0:W, slot, :], k.p2_tab[ds(bases[q], W), 0:2 * D]).then_inc(self.p2_landed[c % 2], 16)
                    sp.dma_start(k.p2w[W:P, slot, 0:D], k.p2_tab[ds(bases[q], W), 2 * D:3 * D])\
                      .then_inc(self.p2_landed[c % 2], 16)

    def tensor(self, pe):
        k, ring = self.k, self.ring
        for s in (self.edge_product, self.pre_done, self.seg_done):
            pe.sem_inc(s, CREDIT)

        def edge(it, q):
            if q % QC == 0:
                pe.wait_ge(self.est_landed[q // QC % 2], it * (16 * RC // 2) + 16 * (q // QC // 2 + 1))
            pe.wait_ge(self.edge_relu, nth(it * QR + q - 2))
            pe.matmul(k.bank[q % 2][0:D, :], k.w_edge_stack[:, :],
                      k.estack[:, q // QC % 2, (q % QC) * QE:(q % QC + 1) * QE], start=True, stop=True)\
              .then_inc(self.edge_product, 1)

        def message(it, q):
            n = it * QR + q
            c = q // QC
            if q % QC == 0:
                pe.wait_ge(self.p2_landed[c % 2], it * (32 * QC * RC // 2) + 32 * QC * (c // 2 + 1))
            pe.wait_ge(self.edge_relu, nth(n))
            pe.wait_ge(self.onehotT_done, nth(n))
            pe.wait_ge(self.add_done, nth(n - 2))
            slot = (c % 2) * QC + q % QC
            for j in range(TQ):
                out = k.bank[2 + q % 2][:, j * D:(j + 1) * D]
                e = slice(j * P, (j + 1) * P)
                pe.matmul(out, k.onehotT[:, q % 2, e], k.p2w[:, slot, 0:D], start=True, stop=False)
                pe.matmul(out, k.onehotT[0:W, q % 2, e], k.p2w[0:W, slot, D:2 * D], start=False, stop=False)
                ins = pe.matmul(out, k.edgeT[:, q % 2, e], k.w3e[:, :], start=False, stop=True)
            ins.then_inc(self.pre_done, 1)

        def sums(it, q):
            n = it * QR + q
            pe.wait_ge(self.square_done, nth(n))
            pe.wait_ge(self.onehot_done, nth(n))
            pe.wait_ge(self.sum_done, nth(n - 2))
            for j in range(TQ):
                pe.matmul(k.bank[4 + q % 2][0:D + 2, 0:W], k.msg[:, q % 2, j, 0:D + 2], k.onehot[:, q % 2, j, :],
                          start=(j == 0), stop=(j == TQ - 1))
            for j in range(TQ):
                ins = pe.matmul(k.bank[6 + q % 2][0:1, 0:D], k.msg[:, q % 2, j, D:D + 1],
                                k.msg_sq[:, q % 2, j, :], start=(j == 0), stop=(j == TQ - 1))
            ins.then_inc(self.seg_done, 1)

        with pe.Fori(0, NIT) as it:
            edge(it, 0)
            for q in range(QR):
                if q + 1 < QR:
                    edge(it, q + 1)
                message(it, q)
                if q >= 1:
                    sums(it, q - 1)
            sums(it, QR - 1)

    def stage_first(self, act):
        stage_first(act, self.k, self.staged)

    def scalar(self, act):
        k, ring = self.k, self.ring
        for s in (self.edge_relu, self.relu_done, self.square_done):
            act.sem_inc(s, CREDIT)

        def edge(it, q):
            n = it * QR + q
            act.wait_ge(self.edge_product, nth(n))
            act.wait_ge(self.pre_done, nth(n - 2))
            act.activation(k.edgeT[0:D, q % 2, :], k.bank[q % 2][0:D, :], ACT.Relu,
                           bias=col(k, "L0_gnn_b_edge")).then_inc(self.edge_relu, 1)

        with act.Fori(0, NIT) as it:
            edge(it, 0)
            for q in range(QR):
                n = it * QR + q
                if q + 1 < QR:
                    edge(it, q + 1)
                if q % QC == 0:
                    stage_next(act, k, it, q // QC, ring, self.staged)
                act.wait_ge(self.add_done, nth(n))
                act.wait_ge(self.seg_done, nth(n - 2))
                act.activation(k.msg[:, q % 2, :, 0:D], k.pre[:, q % 2, :, :], ACT.Relu).then_inc(self.relu_done, 1)
                act.wait_ge(self.relu_done, nth(n))
                act.activation(k.msg_sq[:, q % 2, :, :], k.msg[:, q % 2, :, 0:D], ACT.Square)\
                   .then_inc(self.square_done, 1)

    def credit(self, dve):
        for s in (self.add_done, self.onehotT_done, self.onehot_done, self.sum_done):
            dve.sem_inc(s, CREDIT)

    def vector(self, dve):
        k, ring = self.k, self.ring

        def onehots(it, q):
            n = it * QR + q
            c = q // QC
            if q % QC == 0:
                dve.wait_ge(self.rows_landed[c % 2], it * (16 * RC // 2) + 16 * (c // 2 + 1))
            dve.wait_ge(self.pre_done, nth(n - 2))
            dve.tensor_scalar(k.onehotT[:, q % 2, :], k.drow[:, c % 2, (q % QC) * QE:(q % QC + 1) * QE],
                              k.node_of_row[:, :], None, ALU.is_equal).then_inc(self.onehotT_done, 1)
            dve.wait_ge(self.seg_done, nth(n - 2))
            dve.tensor_copy(k.msg[:, q % 2, :, D:D + 2], k.edge_cols[:, ds(n * TQ, TQ), :])
            dve.tensor_tensor(k.onehot[:, q % 2, :, :], k.iota[:, :].unsqueeze(1).broadcast_to([P, TQ, W]),
                              k.rel_cols[:, ds(n, 1), :].rearrange("p a j -> p (a j)").unsqueeze(2)
                              .broadcast_to([P, TQ, W]), ALU.is_equal).then_inc(self.onehot_done, 1)

        def add_sums(it, q, base):
            n = it * QR + q
            dve.wait_ge(self.seg_done, nth(n))
            dve.wait_ge(self.sum_done, nth(n - 1))
            window = k.aggT[0:D + 2, ds(base, W)]
            dve.tensor_tensor(window, window, k.bank[4 + q % 2][0:D + 2, 0:W], ALU.add)
            dve.tensor_tensor(k.sq_sum[:, :], k.sq_sum[:, :], k.bank[6 + q % 2][0:1, 0:D], ALU.add)\
               .then_inc(self.sum_done, 1)

        with dve.Fori(0, NIT) as it:
            onehots(it, 0)
            for q in range(QR):
                n = it * QR + q
                if q + 1 < QR:
                    onehots(it, q + 1)
                if q % QC == 0:
                    dve.wait_ge(ring[q // QC], it * (16 * CT) + 16 * CT)
                dve.wait_ge(self.pre_done, nth(n))
                dve.wait_ge(self.relu_done, nth(n - 2))
                dve.tensor_tensor(k.pre[:, q % 2, :, :], k.gathered[:, q * TQ:(q + 1) * TQ, :],
                                  k.bank[2 + q % 2][:, 0:TQ * D].rearrange("p (j d) -> p j d", j=TQ), ALU.add)\
                   .then_inc(self.add_done, 1)
                if q >= 1:
                    if (q - 1) % QC == 0:
                        bases = window_bases(dve, k, it, (q - 1) // QC)
                    add_sums(it, q - 1, bases[(q - 1) % QC])
            add_sums(it, QR - 1, bases[QC - 1])


def message_pass(nc, k, ring):
    message = MessagePass(nc, k, ring)
    with nc.Block() as block:
        @block.gpsimd
        def _(pool):
            message.gpsimd(pool)

        @block.sync
        def _(sp):
            message.sync(sp)

        @block.tensor
        def _(pe):
            message.tensor(pe)

        @block.scalar
        def _(act):
            message.stage_first(act)
            message.scalar(act)

        @block.vector
        def _(dve):
            message.credit(dve)
            message.vector(dve)
    end_phase(nc, message.sems)


def gcn_pass(nc, k, ring):
    sems = named(nc, k, "staged", "turns", "onehot_done", "seg_done", "sum_done",
                 "pick_done")
    staged, turns, onehot_done, seg_done, sum_done, pick_done = sems
    with nc.Block() as block:
        @block.gpsimd
        def _(pool):
            gather_rows(pool, k, ring, staged, seg_done, turns)

        @block.scalar
        def _(act):
            stage_first(act, k, staged)
            with act.Fori(0, NIT) as it:
                for c in range(RC):
                    stage_next(act, k, it, c, ring, staged)

        @block.tensor
        def _(pe):
            pe.sem_inc(seg_done, CREDIT)
            with pe.Fori(0, NIT) as it:
                for q in range(QR):
                    n = it * QR + q
                    if q % QC == 0:
                        pe.wait_ge(ring[q // QC], it * (16 * CT) + 16 * CT)
                    pe.wait_ge(onehot_done, nth(n))
                    pe.wait_ge(sum_done, nth(n - 2))
                    for j in range(TQ):
                        ins = pe.matmul(k.bank[q % 2][0:D, 0:W], k.gathered[:, q * TQ + j, :], k.onehot[:, q % 2, j, :],
                                        start=(j == 0), stop=(j == TQ - 1))
                    ins.then_inc(seg_done, 1)

        @block.vector
        def _(dve):
            for s in (sum_done, onehot_done, pick_done):
                dve.sem_inc(s, CREDIT)

            def weights(it, q):
                n = it * QR + q
                dve.wait_ge(seg_done, nth(n - 2))
                hot = k.onehot[:, q % 2, :, :]
                dve.tensor_tensor(hot, k.iota[:, :].unsqueeze(1).broadcast_to([P, TQ, W]),
                                  k.rel_cols[:, ds(n, 1), :].rearrange("p a j -> p (a j)").unsqueeze(2)
                                  .broadcast_to([P, TQ, W]), ALU.is_equal).then_inc(pick_done, 1)
                dve.wait_ge(pick_done, nth(n))
                dve.tensor_tensor(hot, hot, k.edge_cols[:, ds(n * TQ, TQ), 1:2].broadcast_to([P, TQ, W]), ALU.mult)\
                   .then_inc(onehot_done, 1)

            def add_sums(it, q, base):
                n = it * QR + q
                dve.wait_ge(seg_done, nth(n))
                dve.wait_ge(sum_done, nth(n - 1))
                window = k.aggT[0:D, ds(base, W)]
                dve.tensor_tensor(window, window, k.bank[q % 2][0:D, 0:W], ALU.add).then_inc(sum_done, 1)

            with dve.Fori(0, NIT) as it:
                weights(it, 0)
                for q in range(QR):
                    if q + 1 < QR:
                        weights(it, q + 1)
                    if q % QC == 0:
                        bases = window_bases(dve, k, it, q // QC)
                    add_sums(it, q, bases[q % QC])
    end_phase(nc, sems)


def restart_ring(nc, ring):
    nc.all_engine_barrier()
    nc.gpsimd.dma_reset(range(ring[0].num, ring[-1].num + 1))
    for s in ring:
        nc.gpsimd.sem_clear(s)
    nc.all_engine_barrier()


def further_windows(nc, k, ring, run):
    wide = nc.values_load(k.flag[0:1, 0:1], min_val=0, max_val=1)
    with nc.If(wide > 0):
        with nc.Fori(1, ROUNDS):
            restart_ring(nc, ring)
            move_windows(nc, k, W)
            run(nc, k, ring)
        move_windows(nc, k, -W * (ROUNDS - 1))


def copy_sums(act, k, g, half, read, copied):
    by_tile = k.aggT[:, 0:N].rearrange("k (p b) -> k b p", b=NB)
    act.wait_ge(read, nth(g - 2))
    act.copy(k.sumT[:, half, :, :], by_tile[:, ds(g * HB, HB), :]).then_inc(copied, 1)


def clear_sums(pool, k, copied, cleared):
    pool.wait_ge(copied, nth(2 * NIB - 1))
    pool.memset(k.aggT[0:D, :], 0.0).then_inc(cleared, 1)
    pool.wait_ge(cleared, 1)


def between_phase(nc, k):
    sems = named(nc, k, "dve_link", "square_turned", "var_ready", "root_done", "maps_ready", "maps_done", "sum_product",
                 "added", "deg_ready", "deg_root", "sum_copied", "node_copied", "norm_ready", "cleared")
    (link_sem, square_turned, var_ready, root_done, maps_ready, maps_done, sum_product, added, deg_ready,
     deg_root, sum_copied, node_copied, norm_ready, cleared) = sems
    table = TableProduct(nc, k, 0)
    c = k.aff
    with nc.Block() as block:
        @block.gpsimd
        def _(pool):
            clear_sums(pool, k, sum_copied, cleared)

        @block.tensor
        def _(pe):
            pe.matmul(k.bank[0][0:D, 0:1], k.sq_sum[0:1, :], k.ones[0:1, 0:1], start=True, stop=True)\
              .then_inc(square_turned, 1)
            pe.wait_ge(maps_ready, 1)
            for i in range(2):
                ins = pe.matmul(k.bank[1][:, i * D:(i + 1) * D], k.aff_lhs[:, i, :], k.ident[0:D, 0:D],
                                start=True, stop=True)
            ins.then_inc(maps_done, 1)
            pe.sem_inc(sum_product, CREDIT)
            pe.wait_ge(maps_ready, 2)
            with pe.Fori(0, NIB) as it:
                for half in range(2):
                    g = it * 2 + half
                    pe.wait_ge(added, nth(g - 2))
                    pe.wait_ge(sum_copied, nth(g))
                    pe.wait_ge(node_copied, nth(g))
                    for t in range(HB):
                        out = k.bank[2 + half][0:NPART, t * (D + 1):(t + 1) * (D + 1)]
                        pe.matmul(out, k.sumT[:, half, t, :], k.aff_msg[:, :], start=True, stop=False)
                        ins = pe.matmul(out, k.nodeT[:, half, t, :], k.aff_node[:, :], start=False, stop=True)
                    ins.then_inc(sum_product, 1)
            table.credit_tensor(pe)

            def step(g, half, more):
                if more or half == 0:
                    table.turn(pe, g + 1, 1 - half)
                table.products(pe, g, half)

            table.turn(pe, 0, 0)
            half_turns(pe, step)

        @block.scalar
        def _(act):
            act.sem_inc(node_copied, CREDIT)
            act.sem_inc(sum_copied, CREDIT)
            act.wait_ge(var_ready, 1)
            for o in (8, 16):
                ins = act.activation(c[:, o + 2:o + 3], c[:, o + 1:o + 2], ACT.Sqrt, bias=k.eps[0:D, :])
            ins.then_inc(root_done, 1)
            with act.Fori(0, NIB) as it:
                for half in range(2):
                    g = it * 2 + half
                    copy_sums(act, k, g, half, sum_product, sum_copied)
                    act.copy(k.nodeT[:, half, :, :].rearrange("p t n -> p (t n)"),
                             k.nfT[:, ds(g * HB * NPART, HB * NPART)]).then_inc(node_copied, 1)
            act.wait_ge(deg_ready, 1)
            act.activation(k.deg[:, 1, :], k.deg[:, 0, :], ACT.Sqrt)
            act.activation(k.small[:, 3, :], k.small[:, 2, :], ACT.Sqrt, bias=k.eps[0:NPART, :]).then_inc(deg_root, 1)
            act.wait_ge(norm_ready, 1)
            act.sem_inc(table.h_done, CREDIT)
            with act.Fori(0, NIB) as it:
                for half in range(2):
                    normal_rows(act, k, it * 2 + half, half, table.turned, table.h_done)

        @block.vector
        def _(dve):
            link = linker(dve, link_sem)
            dve.bn_aggr(c[:, 8:10], k.node_stats[:, :, :].rearrange("p a b -> p (a b)"))
            link(dve.tensor_reduce(c[:, 16:17], k.aggT[0:D, 0:N], AX.X, ALU.add))
            link(dve.tensor_scalar(c[:, 16:17], c[:, 16:17], 1.0 / E, None, ALU.mult))
            link(dve.tensor_tensor(c[:, 22:23], c[:, 16:17], c[:, 16:17], ALU.mult))
            dve.wait_ge(square_turned, 1)
            link(dve.scalar_tensor_tensor(c[:, 17:18], k.bank[0][0:D, 0:1], 1.0 / E, c[:, 22:23], ALU.mult, ALU.subtract))
            link(dve.tensor_scalar(c[:, 17:18], c[:, 17:18], 0.0, None, ALU.max))
            dve.sem_inc(var_ready, 1)
            dve.wait_ge(root_done, 1)
            affine(dve, link, k, 8, "node")
            affine(dve, link, k, 16, "msg")
            for i, o in ((0, 16), (1, 8)):
                dve.tensor_scalar(k.aff_lhs[:, i, 0:D], k.ident[0:D, 0:D], c[:, o + 4:o + 5], None, ALU.mult)
                link(dve.tensor_copy(k.aff_lhs[:, i, D:D + 1], c[:, o + 5:o + 6]))
            dve.sem_inc(maps_ready, 1)
            dve.wait_ge(maps_done, 1)
            dve.tensor_copy(k.aff_msg[:, 0:D], k.bank[1][:, 0:D])
            dve.tensor_copy(k.aff_msg[:, D:D + 1], k.ident[:, D + 1:D + 2])
            link(dve.tensor_copy(k.aff_node[:, 0:D], k.bank[1][:, D:2 * D]))
            dve.sem_inc(maps_ready, 1)
            dve.sem_inc(added, CREDIT)
            with dve.Fori(0, NIB) as it:
                for half in range(2):
                    g = it * 2 + half
                    dve.wait_ge(sum_product, nth(g))
                    got = k.bank[2 + half][0:NPART, 0:HB * (D + 1)].rearrange("p (t d) -> p t d", t=HB)
                    xt = k.xs[:, ds(g * HB, HB), :]
                    dve.tensor_scalar(k.deg[:, 0:1, ds(g * HB, HB)].rearrange("p a t -> p t a"), got[:, :, D:D + 1],
                                      1.0, None, ALU.add)
                    dve.tensor_tensor(xt, xt, got[:, :, 0:D], ALU.add).then_inc(added, 1)
                    dve.wait_ge(added, nth(g))
                    for t in range(HB):
                        dve.bn_stats(tile_of(k.stats, g * HB + t), tile_of(k.xs, g * HB + t))
            dve.wait_ge(added, nth(2 * NIB - 1))
            link(dve.tensor_scalar(k.deg[:, 2, :], k.deg[:, 0, :], 0.0, None, ALU.is_gt))
            link(dve.tensor_scalar(k.deg[:, 0, :], k.deg[:, 0, :], 1e-30, None, ALU.max))
            layernorm_sums(dve, link, k)
            dve.sem_inc(deg_ready, 1)
            dve.wait_ge(deg_root, 1)
            layernorm_map(dve, link, k)
            link(dve.reciprocal(k.dinv[:, :], k.deg[:, 1, :]))
            link(dve.tensor_tensor(k.dinv[:, :], k.dinv[:, :], k.deg[:, 2, :], ALU.mult))
            dve.sem_inc(norm_ready, 1)
            table.credit_vector(dve)

            def step(g, half, more):
                if more or half == 0:
                    table.columns(dve, g + 1, 1 - half)
                table.scale(dve, g, half)

            table.columns(dve, 0, 0)
            half_turns(dve, step)

        @block.sync
        def _(sp):
            table.sync(sp)
    end_phase(nc, sems + table.sems)


class TableProduct:

    def __init__(self, nc, k, layer):
        self.k, self.layer = k, layer
        self.sems = named(nc, k, "t_h_done", "t_turned", "t_hT_done", "t_products_done", "t_scaled", "t_stored0",
                          "t_stored1")
        self.h_done, self.turned, self.hT_done, self.products_done, self.scaled, stored0, stored1 = self.sems
        self.stored = (stored0, stored1)

    def credit_tensor(self, pe):
        for s in (self.turned, self.products_done):
            pe.sem_inc(s, CREDIT)

    def credit_vector(self, dve):
        dve.sem_inc(self.scaled, CREDIT)
        dve.memset(self.k.hT[D:P, :, :, :], 0.0).then_inc(self.hT_done, CREDIT)

    def turn(self, pe, g, half):
        turn_rows(pe, self.k, 4, g, half, self.h_done, self.hT_done, self.turned)

    def products(self, pe, g, half):
        k = self.k
        pe.wait_ge(self.hT_done, nth(g))
        pe.wait_ge(self.scaled, nth(g - 2))
        for t in range(HB):
            ins = pe.matmul(k.bank[6 + half][0:NPART, t * D:(t + 1) * D], k.hT[:, half, t, :],
                            k.w_gcn[:, self.layer, :], start=True, stop=True)
        ins.then_inc(self.products_done, 1)

    def columns(self, dve, g, half):
        columns_out(dve, self.k, 4, g, half, self.turned, self.products_done, self.hT_done)

    def scale(self, dve, g, half):
        k = self.k
        dve.wait_ge(self.products_done, nth(g))
        dve.tensor_tensor(k.tables[:, ds(g * HB, HB), 0, :],
                          k.bank[6 + half][0:NPART, 0:HB * D].rearrange("p (t d) -> p t d", t=HB),
                          by_node(k, g), ALU.mult).then_inc(self.scaled, 1)

    def sync(self, sp):
        k = self.k
        tab = k.gather_tab.rearrange("(p b) d -> p b d", b=NB)
        with sp.Fori(0, NIB) as it:
            for half in range(2):
                g = it * 2 + half
                sp.wait_ge(self.scaled, nth(g))
                sp.dma_start(tab[:, ds(g * HB, HB), :], k.tables[:, ds(g * HB, HB), 0, :])\
                    .then_inc(self.stored[half], 16)
        for s in self.stored:
            sp.wait_ge(s, NIB * 16)


def by_node(k, g):
    return k.dinv[:, ds(g * HB, HB)].unsqueeze(2).broadcast_to([NPART, HB, D])


def turn_sums(pe, k, g, half, copied, read, turned):
    pe.wait_ge(copied, nth(g))
    pe.wait_ge(read, nth(g - 2))
    for t in range(HB):
        ins = pe.transpose(k.bank[half][0:NPART, t * D:(t + 1) * D], k.sumT[0:D, half, t, :], k.ident[0:D, 0:D])
    ins.then_inc(turned, 1)


def mix_rows(dve, k, layer, g, half, turned, added, spread, mixed):
    u = k.mix_room[:, half, :, :]
    dve.wait_ge(turned, nth(g))
    dve.tensor_tensor(u, k.bank[half][0:NPART, 0:HB * D].rearrange("p (t d) -> p t d", t=HB),
                      k.tables[:, ds(g * HB, HB), 0, :], ALU.add).then_inc(added, 1)
    dve.wait_ge(added, nth(g))
    dve.tensor_tensor(u, u, by_node(k, g), ALU.mult).then_inc(spread, 1)
    dve.wait_ge(spread, nth(g))
    dve.tensor_tensor(u, u, k.b_gcn[:, layer, :].unsqueeze(1).broadcast_to([NPART, HB, D]), ALU.add)\
       .then_inc(mixed, 1)


def second_table_phase(nc, k):
    sems = named(nc, k, "sum_copied", "sum_turned", "added", "spread", "mixed", "cleared")
    sum_copied, sum_turned, added, spread, mixed, cleared = sems
    table = TableProduct(nc, k, 1)
    with nc.Block() as block:
        @block.gpsimd
        def _(pool):
            clear_sums(pool, k, sum_copied, cleared)

        @block.tensor
        def _(pe):
            pe.sem_inc(sum_turned, CREDIT)
            table.credit_tensor(pe)

            def step(g, half, more):
                if more:
                    turn_sums(pe, k, g + 2, half, sum_copied, added, sum_turned)
                if more or half == 0:
                    table.turn(pe, g + 1, 1 - half)
                table.products(pe, g, half)

            for half in range(2):
                turn_sums(pe, k, half, half, sum_copied, added, sum_turned)
            table.turn(pe, 0, 0)
            half_turns(pe, step)

        @block.scalar
        def _(act):
            for s in (sum_copied, table.h_done):
                act.sem_inc(s, CREDIT)

            def rows(g, half):
                act.wait_ge(mixed, nth(g))
                act.wait_ge(table.turned, nth(g - 2))
                act.activation(k.h[:, half, :, :], k.mix_room[:, half, :, :], ACT.Relu).then_inc(table.h_done, 1)

            def step(g, half, more):
                if more:
                    copy_sums(act, k, g + 2, half, sum_turned, sum_copied)
                if more or half == 0:
                    rows(g + 1, 1 - half)

            for half in range(2):
                copy_sums(act, k, half, half, sum_turned, sum_copied)
            rows(0, 0)
            half_turns(act, step)

        @block.vector
        def _(dve):
            for s in (added, spread, mixed):
                dve.sem_inc(s, CREDIT)
            table.credit_vector(dve)

            def mix(g, half):
                dve.wait_ge(table.h_done, nth(g - 2))
                mix_rows(dve, k, 0, g, half, sum_turned, added, spread, mixed)

            def step(g, half, more):
                if more:
                    mix(g + 2, half)
                if more or half == 0:
                    table.columns(dve, g + 1, 1 - half)
                table.scale(dve, g, half)

            for half in range(2):
                mix(half, half)
            table.columns(dve, 0, 0)
            half_turns(dve, step)

        @block.sync
        def _(sp):
            table.sync(sp)
    end_phase(nc, sems + table.sems)


def output_phase(nc, k, out):
    sems = named(nc, k, "sum_copied", "sum_turned", "added", "spread", "mixed", "out_done", "stored0", "stored1")
    sum_copied, sum_turned, added, spread, mixed, out_done, stored0, stored1 = sems
    stored = (stored0, stored1)
    rows = out.rearrange("(p b) d -> p b d", b=NB)
    with nc.Block() as block:
        @block.scalar
        def _(act):
            act.sem_inc(sum_copied, CREDIT)
            with act.Fori(0, NIB) as it:
                for half in range(2):
                    copy_sums(act, k, it * 2 + half, half, sum_turned, sum_copied)

        @block.tensor
        def _(pe):
            pe.sem_inc(sum_turned, CREDIT)
            with pe.Fori(0, NIB) as it:
                for half in range(2):
                    turn_sums(pe, k, it * 2 + half, half, sum_copied, added, sum_turned)

        @block.vector
        def _(dve):
            for s in (added, spread, mixed, out_done):
                dve.sem_inc(s, CREDIT)
            with dve.Fori(0, NIB) as it:
                for half in range(2):
                    g = it * 2 + half
                    dve.wait_ge(out_done, nth(g - 2))
                    mix_rows(dve, k, 1, g, half, sum_turned, added, spread, mixed)
                    dve.wait_ge(mixed, nth(g))
                    xt = k.xs[:, ds(g * HB, HB), :]
                    dve.scalar_tensor_tensor(xt, k.mix_room[:, half, :, :], 0.0, xt, ALU.max, ALU.add)\
                       .then_inc(out_done, 1)

        @block.sync
        def _(sp):
            with sp.Fori(0, NIB) as it:
                for half in range(2):
                    g = it * 2 + half
                    sp.wait_ge(out_done, nth(g))
                    sp.dma_start(rows[:, ds(g * HB, HB), :], k.xs[:, ds(g * HB, HB), :]).then_inc(stored[half], 16)
            sp.wait_ge(stored0, NIB * 16)
            sp.wait_ge(stored1, NIB * 16)


def gnn_kernel(nc, a, out):
    k = Kernel()
    k.sems = {}
    allocate(nc, k)
    rings = [[nc.alloc_semaphore(f"{name}_landed{c}") for c in range(RC)] for name in ("message", "first", "second")]
    first_phase(nc, k, a, rings[0])
    further_windows(nc, k, rings[0], message_pass)
    between_phase(nc, k)
    gcn_pass(nc, k, rings[1])
    further_windows(nc, k, rings[1], gcn_pass)
    second_table_phase(nc, k)
    gcn_pass(nc, k, rings[2])
    further_windows(nc, k, rings[2], gcn_pass)
    output_phase(nc, k, out)


def laid_out(inputs):
    a = {n: np.ascontiguousarray(v) for n, v in inputs.items()}

    def padded(v, fill, n=EP):
        return np.concatenate([v, np.full((n - v.shape[0],) + v.shape[1:], fill, v.dtype)])

    dst = padded(a["dst"], int(FAR))
    a["dst"] = dst
    a["dst_cols"] = np.ascontiguousarray(dst.reshape(NT, P).T)
    a["src"] = np.ascontiguousarray(padded(a["src"], 0, NCOL * P).reshape(NCOL, P).T)
    a["edge_weight"] = np.ascontiguousarray(padded(a["edge_weight"], 0).reshape(NT, P).T)
    a["edge_attr_4"] = np.ascontiguousarray(padded(a["edge_attr_4"], 0).T).reshape(P, DE * EP // P)
    return a


def kernel(**inputs):
    import concourse.bacc as bacc
    from concourse.bass_utils import run_bass_kernel_spmd

    nc = bacc.Bacc("TRN2", target_bir_lowering=False, num_devices=1)
    arrays, args = {}, {}
    for name, v in laid_out(inputs).items():
        arrays[f"in_{name}"] = v
        args[name] = nc.dram_tensor(f"in_{name}", v.shape, mybir.dt.from_np(v.dtype), kind="ExternalInput").ap()
    out = nc.dram_tensor("out", (N, D), F32, kind="ExternalOutput").ap()
    gnn_kernel(nc, args, out)
    r = run_bass_kernel_spmd(nc, [arrays], core_ids=[0])
    return r.results[0]["out"]
```

```python
import numpy as np
import concourse.bass as bass
from concourse import mybir

ALU = mybir.AluOpType
ACT = mybir.ActivationFunctionType
AX = mybir.AxisListType
F32 = mybir.dt.float32
BF16 = mybir.dt.bfloat16
I32 = mybir.dt.int32
ds = bass.ds

N, D, E, DE = 6250, 96, 106250, 4
EPS = 1e-5
P = 128

TQ, QC, RC = 4, 4, 4
QE = TQ * P
NCH = -(-E // (QE * QC * RC)) * RC
NQ = NCH * QC
NT = NQ * TQ
EP = NT * P
NIT = NCH // RC
GC = RC - 1
QR = QC * RC
TR = QR * TQ
CT = QC * TQ
LASTV = E - (NQ - 1) * QE
QB = NQ // 2
NCOL = NT + TR

W = 64
ROUNDS = -(-N // W)
FAR = float(1 << 20)
CLIP = 200.0

NB, NPART = 50, 125
HB = 5
NIB = NB // (2 * HB)
HALVES = ((0, 3), (3, HB))
NPAD = N + W

NS = 3
KS = NS * NS * DE
CREDIT = QR


def nth(n):
    return n + 1 + CREDIT


class Kernel:
    pass


def allocate(nc, k):
    def sb(name, shape, dt=F32):
        return nc.alloc_sbuf_tensor(name, shape, dt)

    k.ident = sb("ident", [P, P])
    k.iota = sb("iota", [P, W])
    k.node_of_row = sb("node_of_row", [P, 1])
    k.ones = sb("ones", [P, 1])
    k.eps = sb("eps", [P, 1])
    k.zeros = sb("zeros", [W, NS * D], BF16)
    k.xs = sb("xs", [NPART, NB, D])
    k.nfT = sb("nfT", [P, N])
    k.aggT = sb("aggT", [P, NPAD])
    k.tables = sb("tables", [NPART, NB, 2, D])
    k.gathered = sb("gathered", [P, TR, D])
    k.src_cols = sb("src_cols", [P, NCOL], I32)
    k.src_stage = sb("src_stage", [P, TR], I32)
    k.edge_cols = sb("edge_cols", [P, NT, 2])
    k.rel_cols = sb("rel_cols", [P, NQ, TQ])
    k.rel_rows = sb("rel_rows", [QB, 2, QE])
    k.rel_clip = sb("rel_clip", [QB, 2, QE], BF16)
    k.base_q = sb("base_q", [QB, 2])
    k.base_all = sb("base_all", [P, NQ])
    k.base_int = sb("base_int", [1, NQ], I32)
    k.span = sb("span", [QB, 2])
    k.flag = sb("flag", [1, 1], I32)
    k.w12 = sb("w12", [P, 2 * D])
    k.w_node = sb("w_node", [P, D])
    k.w3 = sb("w3", [P, D])
    k.w3e = sb("w3e", [P, D])
    k.w_gcn = sb("w_gcn", [P, 2, D])
    k.w_edge = sb("w_edge", [DE, D])
    k.w_edge_parts = sb("w_edge_parts", [DE, NS, D], BF16)
    k.w_edge_stack = sb("w_edge_stack", [KS, D], BF16)
    k.cols = sb("cols", [D, 16])
    k.b_gcn = sb("b_gcn", [NPART, 2, D])
    k.b_msg_row = sb("b_msg_row", [P, D])
    k.sq_sum = sb("sq_sum", [1, D])
    k.dinv = sb("dinv", [NPART, NB])
    k.rstd = sb("rstd", [NPART, NB])
    k.shift = sb("shift", [NPART, NB])
    k.stats = sb("stats", [NPART, NB, 6])
    k.small = sb("small", [NPART, 4, NB])
    k.deg = sb("deg", [NPART, 3, NB])
    k.edge_stats = sb("edge_stats", [D, NQ, 6])
    k.node_stats = sb("node_stats", [D, 2 * NIB * 2, 6])
    k.aff = sb("aff", [D, 24])
    k.aff_lhs = sb("aff_lhs", [D, 2, P])
    k.aff_msg = sb("aff_msg", [P, D + 1])
    k.aff_node = sb("aff_node", [P, D + 1])
    ring = k.gathered[:, :, :].rearrange("p t d -> p (t d)")
    hT_at = TR * D - 2 * HB * NPART
    k.hT = ring[:, hT_at:].rearrange("p (a b c) -> p a b c", a=2, b=HB)
    k.h = ring[0:NPART, hT_at - 2 * HB * D:hT_at].rearrange("p (a b c) -> p a b c", a=2, b=HB)

    FW = DE * EP // P
    work = sb("work", [P, 9232])
    k.edge_raw = work[:, 0:FW]
    k.edge_parts = work[:, FW:FW + NS * FW // 2].bitcast(BF16).rearrange("p (s w) -> p s w", s=NS)
    at = [0]

    def view(shape, dt=F32, parts=P):
        words = int(np.prod(shape)) // (1 if dt == F32 else 2)
        v = work[0:parts, at[0]:at[0] + words]
        at[0] += words
        letters = "abcd"[:len(shape)]
        sizes = {x: n for x, n in zip(letters, shape)}
        return (v if dt == F32 else v.bitcast(dt)).rearrange(f"p ({' '.join(letters)}) -> p {' '.join(letters)}", **sizes)

    k.estack = view([2, QC * QE], BF16, KS)
    k.edgeT = view([2, QE])
    passes_at = at[0]
    k.drow = view([2, QC * QE], BF16)
    k.p2w = view([2 * QC, 2 * D], BF16)
    k.onehotT = view([2, QE], BF16)
    k.onehot = view([2, TQ, W])
    k.pre = view([2, TQ, D])
    k.msg = view([2, TQ, D + 2])
    k.msg_sq = view([2, TQ, D])
    k.edgeT_more = work[:, at[0] - 2 * QE:at[0]].rearrange("p (a e) -> p a e", a=2)
    at[0] = passes_at
    k.p2_room = view([2, NB // XL * NS * D], BF16, NPART)
    at[0] = 0
    k.sumT = view([2, HB, NPART])
    k.nodeT = view([2, HB, NPART])
    k.mix_room = view([2, HB, D], parts=NPART)

    k.bank = [nc.alloc_psum_tensor(f"bank{i}", [P, 512], F32) for i in range(8)]
    k.gather_tab = nc.dram_tensor("gather_tab", [N, D], F32).ap()
    k.stash_tab = nc.dram_tensor("stash_tab", [P, NIT, CT * D], F32).ap()
    k.p2_tab = nc.dram_tensor("p2_tab", [NPAD, NS * D], BF16).ap()
    k.edge_tab = nc.dram_tensor("edge_tab", [NS * DE, EP], BF16).ap()
    k.rel_tab = nc.dram_tensor("rel_tab", [NQ, QE], BF16).ap()
    k.base_tab = nc.dram_tensor("base_tab", [2, QB], F32).ap()


def end_phase(nc, sems):
    nc.all_engine_barrier()
    for s in sems:
        nc.gpsimd.sem_clear(s)
    nc.all_engine_barrier()


def named(nc, k, *names):
    for n in names:
        if n not in k.sems:
            k.sems[n] = nc.alloc_semaphore(n)
    return [k.sems[n] for n in names]


def linker(eng, sem):
    n = [0]

    def link(ins):
        n[0] += 1
        ins.then_inc(sem, 1)
        eng.wait_ge(sem, n[0])
    return link


COLUMNS = ("L0_gnn_b_node", "L0_gnn_g_node", "L0_gnn_beta_node", "L0_gnn_b_edge", "L0_gnn_g_edge",
           "L0_gnn_beta_edge", "L0_gnn_g_msg", "L0_gnn_beta_msg")


def col(k, name):
    i = COLUMNS.index(name)
    return k.cols[:, i:i + 1]


def clip_windows(dve, link, k, clipped):
    link(dve.tensor_scalar(k.rel_clip[:, :, :], k.rel_rows[:, :, :], CLIP, -1.0, ALU.min, ALU.max))
    dve.sem_inc(clipped, 1)
    link(dve.tensor_scalar(k.base_int[:, :], k.base_all[0:1, :], float(N), None, ALU.min))
    rel = k.rel_cols[:, :, :].rearrange("p q j -> p (q j)")
    inside = k.edge_cols[:, :, 0]
    link(dve.tensor_scalar(inside, rel, 0.0, None, ALU.is_ge))
    link(dve.scalar_tensor_tensor(inside, rel, float(W), inside, ALU.is_lt, ALU.mult))


def move_windows(nc, k, move):
    sems = named(nc, k, "move_link", "move_clipped", "move_stored")
    link_sem, clipped, stored = sems
    with nc.Block() as block:
        @block.vector
        def _(dve):
            link = linker(dve, link_sem)
            link(dve.tensor_scalar(k.rel_rows[:, :, :], k.rel_rows[:, :, :], float(-move), None, ALU.add))
            link(dve.tensor_scalar(k.rel_cols[:, :, :], k.rel_cols[:, :, :], float(-move), None, ALU.add))
            link(dve.tensor_scalar(k.base_all[:, :], k.base_all[:, :], float(move), None, ALU.add))
            clip_windows(dve, link, k, clipped)

        @block.sync
        def _(sp):
            sp.wait_ge(clipped, 1)
            sp.dma_start(k.rel_tab.rearrange("(b q) e -> q b e", b=2), k.rel_clip[:, :, :]).then_inc(stored, 16)
            sp.wait_ge(stored, 16)
    end_phase(nc, sems)


def affine(dve, link, k, o, what):
    c = k.aff
    link(dve.reciprocal(c[:, o + 3:o + 4], c[:, o + 2:o + 3]))
    link(dve.tensor_tensor(c[:, o + 4:o + 5], c[:, o + 3:o + 4], col(k, f"L0_gnn_g_{what}"), ALU.mult))
    link(dve.tensor_tensor(c[:, o + 5:o + 6], c[:, o:o + 1], c[:, o + 4:o + 5], ALU.mult))
    link(dve.tensor_tensor(c[:, o + 5:o + 6], col(k, f"L0_gnn_beta_{what}"), c[:, o + 5:o + 6], ALU.subtract))


def layernorm_sums(dve, link, k):
    st = k.stats[:, :, :]
    m0, m1, v0, v1 = st[:, :, 1], st[:, :, 4], st[:, :, 2], st[:, :, 5]
    mean, half, var = k.small[:, 0, :], k.small[:, 1, :], k.small[:, 2, :]
    dve.tensor_tensor(mean, m0, m1, ALU.add)
    dve.tensor_tensor(var, v0, v1, ALU.add)
    link(dve.tensor_tensor(half, m0, m1, ALU.subtract))
    link(dve.scalar_tensor_tensor(half, half, 0.25, half, ALU.mult, ALU.mult))
    link(dve.scalar_tensor_tensor(var, var, 1.0 / D, half, ALU.mult, ALU.add))


def layernorm_map(dve, link, k):
    link(dve.reciprocal(k.rstd[:, :], k.small[:, 3, :]))
    link(dve.scalar_tensor_tensor(k.shift[:, :], k.small[:, 0, :], -0.5, k.rstd[:, :], ALU.mult, ALU.mult))


def tile_of(t, n):
    return t[:, ds(n, 1), :].rearrange("p a d -> p (a d)")


def half_turns(eng, step):
    with eng.Fori(0, NIB - 1) as it:
        for half in range(2):
            step(it * 2 + half, half, True)
    for half in range(2):
        step((NIB - 1) * 2 + half, half, False)


def normal_rows(act, k, g, half, turned, h_done):
    act.wait_ge(turned, nth(g - 2))
    for t in range(HB):
        n = g * HB + t
        ins = act.activation(k.h[:, half, t, :], tile_of(k.xs, n), ACT.Relu,
                             bias=k.shift[:, ds(n, 1)], scale=k.rstd[:, ds(n, 1)])
    ins.then_inc(h_done, 1)


def turn_rows(pe, k, bank, g, half, h_done, hT_done, turned):
    pe.wait_ge(h_done, nth(g))
    pe.wait_ge(hT_done, nth(g - 1))
    for i, (lo, hi) in enumerate(HALVES):
        for t in range(lo, hi):
            ins = pe.transpose(k.bank[bank + i][0:D, (t - lo) * NPART:(t - lo + 1) * NPART], k.h[:, half, t, :],
                               k.ident[0:NPART, 0:NPART])
    ins.then_inc(turned, 1)


def columns_out(dve, k, bank, g, half, turned, products_done, hT_done):
    dve.wait_ge(turned, nth(g))
    dve.wait_ge(products_done, nth(g - 2))
    for i, (lo, hi) in enumerate(HALVES):
        ins = dve.tensor_copy(k.hT[0:D, half, lo:hi, :].rearrange("p t n -> p (t n)"),
                              k.bank[bank + i][0:D, 0:(hi - lo) * NPART])
    ins.then_inc(hT_done, 1)


def tile_of_turn(x, g, t):
    return x[:, :, :].rearrange("p (g t) d -> p g t d", t=HB)[:, ds(g, 1), t, :].rearrange("p a d -> p (a d)")


XL = 5
SB = 4


def first_phase(nc, k, a, ring):
    names = ("cleared", "consts_ready", "sums_cleared", "pool_link", "dve_link", "dst_landed", "src_landed",
             "edge_landed", "early_landed", "weights_landed", "base_ready", "base_stored", "base_back", "span_ready",
             "span_turned", "clipped", "rel_stored", "var_ready", "root_done", "norm_ready", "h_done", "turned",
             "hT_done", "w12_done", "products_done", "copied", "nf_done", "tab_stored0", "tab_stored1",
             "edge_part", "edge_rest",
             "parts_stored", "stack_ready", "flag_done", "stack_landed0", "stack_landed1", "edge_mm", "edge_act",
             "edge_stat", "edge_var", "edge_root", "shift_ready", "shift_done", "w3e_ready", "buffers_ready",
             "p2_part", "p2_rest", "p2_stored0", "p2_stored1", "cols_ready", "stash_turns", "stash_staged")
    sems = named(nc, k, *names)
    (cleared, consts_ready, sums_cleared, pool_link, dve_link, dst_landed, src_landed,
     edge_landed, early_landed, weights_landed, base_ready, base_stored, base_back, span_ready,
     span_turned, clipped, rel_stored, var_ready, root_done, norm_ready, h_done, turned,
     hT_done, w12_done, products_done, copied, nf_done, tab_stored0, tab_stored1, edge_part, edge_rest,
     parts_stored, stack_ready, flag_done, stack_landed0, stack_landed1, edge_mm, edge_act, edge_stat,
     edge_var, edge_root, shift_ready, shift_done, w3e_ready, buffers_ready,
     p2_part, p2_rest, p2_stored0, p2_stored1, cols_ready, stash_turns, stash_staged) = sems
    p2_stored = (p2_stored0, p2_stored1)
    x_landed = named(nc, k, *[f"x_landed{i}" for i in range(XL)])
    landed, tab_stored = (stack_landed0, stack_landed1), (tab_stored0, tab_stored1)
    message = MessagePass(nc, k, ring)
    stash_landed, k.stash_saved = ({c: nc.alloc_semaphore(f"stash_{name}{c}") for c in range(1, RC)}
                                   for name in ("landed", "saved"))

    NI, CI = NCH // 2, 2
    QI = CI * QC
    FW = DE * EP // P
    room = k.gathered[:, :, :].rearrange("p t d -> p (t d)")
    dst_q = room[0:QB, 0:2 * QE].bitcast(I32).rearrange("p (b e) -> p b e", b=2)
    spans = room[0:QB, 2 * QE:4 * QE].rearrange("p (b e) -> p b e", b=2)
    dst_p = room[:, 4 * QE:4 * QE + NT].bitcast(I32)
    weight_p = room[:, 4 * QE + NT:4 * QE + 2 * NT]
    span_row = k.bank[5][0:1, 0:QB]
    tab = k.gather_tab.rearrange("(p b) d -> p b d", b=NB)
    p2 = k.p2_tab[0:N, :].rearrange("(p b) d -> p b d", b=NB)
    XB = NB // XL

    with nc.Block() as block:
        @block.sync
        def _(sp):
            sp.dma_start(dst_q, a["dst"].rearrange("(b q e) -> q b e", b=2, e=QE)).then_inc(dst_landed, 16)
            sp.dma_start(dst_p, a["dst_cols"]).then_inc(dst_landed, 16)
            sp.dma_start(weight_p, a["edge_weight"]).then_inc(dst_landed, 16)
            xr = a["x"].rearrange("(p b) d -> p b d", b=NB)
            for i in range(XL):
                sp.dma_start(k.xs[:, i * XB:(i + 1) * XB, :], xr[:, i * XB:(i + 1) * XB, :]).then_inc(x_landed[i], 16)
            sp.dma_start(k.edge_raw, a["edge_attr_4"]).then_inc(edge_landed, 16)
            sp.dma_start(k.w_edge[:, :], a["L0_gnn_W_edge"]).then_inc(edge_landed, 16)
            sp.wait_ge(cleared, 1)
            wm = a["L0_gnn_W_msg"]
            early = [(k.w12[0:D, 0:D], wm[0:D, :]), (k.w12[0:D, D:2 * D], wm[D:2 * D, :]),
                     (k.w_node[0:D, :], a["L0_gnn_W_node"])]
            early += [(k.cols[:, i:i + 1], a[name].unsqueeze(1)) for i, name in enumerate(COLUMNS)]
            for dst, src in early:
                sp.dma_start(dst, src).then_inc(early_landed, 16)
            sp.dma_start(k.src_cols[:, :], a["src"]).then_inc(src_landed, 16)
            for b in range(2):
                sp.wait_ge(base_ready, 1)
                sp.dma_start(k.base_tab[b].unsqueeze(1), k.base_q[:, b:b + 1]).then_inc(base_stored, 16)
            sp.wait_ge(base_stored, 32)
            sp.dma_start(k.base_all[:, :], k.base_tab.rearrange("b q -> (b q)").unsqueeze(0).broadcast_to([P, NQ]))\
              .then_inc(base_back, 16)
            late = [(k.b_msg_row[D:D + 1, :], a["L0_gnn_b_msg"].unsqueeze(0)),
                    (k.w3[0:D, :], wm[2 * D:3 * D, :]), (k.w_gcn[0:D, 0, :], a["L1_gnn_W1"]),
                    (k.w_gcn[0:D, 1, :], a["L1_gnn_W2"]), (k.p2_tab[N:NPAD, :], k.zeros[:, :])]
            late += [(k.b_gcn[:, i, :], a[name].unsqueeze(0).broadcast_to([NPART, D]))
                     for i, name in enumerate(("L1_gnn_b1", "L1_gnn_b2"))]
            for dst, src in late:
                sp.dma_start(dst, src).then_inc(weights_landed, 16)
            def store_part(i):
                sp.wait_ge(edge_part, i + 1)
                rows = k.edge_tab[i * DE:(i + 1) * DE, :].rearrange("c (w f) -> (c w) f", f=FW)
                sp.dma_start(rows, k.edge_parts[:, i, :]).then_inc(parts_stored, 16)
                for j in range(NS):
                    r = (i * NS + j) * DE
                    sp.dma_start(k.w_edge_stack[r:r + DE, :], k.w_edge_parts[:, i, :]).then_inc(stack_ready, 16)

            store_part(0)
            with sp.Fori(0, NIB) as it:
                for half in range(2):
                    g = it * 2 + half
                    sp.wait_ge(copied, nth(g))
                    sp.dma_start(tab[:, ds(g * HB, HB), :], k.tables[:, ds(g * HB, HB), 0, :])\
                        .then_inc(tab_stored[half], 16)
            for i in range(1, NS):
                store_part(i)
            for i in range(XL):
                sp.wait_ge(p2_part, NS * (i + 1))
                sp.dma_start(p2[:, i * XB:(i + 1) * XB, :], p2_piece(k, i % 2).rearrange("p t s d -> p t (s d)"))\
                    .then_inc(p2_stored[i % 2], 16)
            sp.wait_ge(clipped, 1)
            sp.dma_start(k.rel_tab.rearrange("(b q) e -> q b e", b=2), k.rel_clip[:, :, :]).then_inc(rel_stored, 16)
            sp.wait_ge(parts_stored, 16 * NS)
            with sp.Fori(0, NI) as it:
                for c in range(CI):
                    sp.wait_ge(edge_mm, nth(it * QI + (c - 2) * QC + QC - 1))
                    load_stack(sp, k, c, it * CI + c).then_inc(landed[c], 16)
            for i in range(2):
                sp.wait_ge(p2_stored[i], 16 * len(range(i, XL, 2)))
            sp.wait_ge(weights_landed, 16 * len(late))
            sp.wait_ge(rel_stored, 16)
            message.sync(sp)

        @block.gpsimd
        def _(pool):
            link = linker(pool, pool_link)
            for t in (k.w12, k.w_node, k.w3, k.w3e):
                pool.memset(t[:, :], 0.0)
            pool.memset(k.w_gcn[:, :, :], 0.0)
            link(pool.memset(k.zeros[:, :], 0.0))
            pool.sem_inc(cleared, 1)
            pool.memset(k.eps[:, :], EPS)
            link(pool.memset(k.ident[:, :], 0.0))
            link(pool.affine_select(out=k.ident[:, :], in_=k.ident[:, :], compare_op=ALU.not_equal, fill=1.0,
                                    base=0, pattern=[[-1, P]], channel_multiplier=1))
            pool.sem_inc(consts_ready, 1)
            pool.wait_ge(dst_landed, 48)
            pool.tensor_copy(k.rel_cols[:, :, :].rearrange("p q j -> p (q j)"), dst_p).then_inc(cols_ready, 1)
            pool.tensor_copy(k.edge_cols[:, :, 1], weight_p).then_inc(cols_ready, 1)
            link(pool.iota(k.iota[:, :], [[1, W]], 0, 0, allow_small_or_imprecise_dtypes=True))
            for r in range(P // W):
                link(pool.iota(k.node_of_row[r * W:(r + 1) * W, :], [[0, 1]], 0, 1, allow_small_or_imprecise_dtypes=True))
            for t in (k.ones[:, :],):
                link(pool.memset(t, 1.0))
            for t in (k.sq_sum[:, :], k.aff_lhs[:, :, :], k.aff_node[:, :], k.nfT[D:P, :]):
                link(pool.memset(t, 0.0))
            link(pool.memset(k.nfT[D:D + 1, :], 1.0))
            link(pool.memset(k.aggT[:, :], 0.0))
            pool.sem_inc(sums_cleared, 1)
            for i in range(NS - 1):
                pool.wait_ge(edge_part, i + 1)
                pool.tensor_tensor(k.w_edge[:, :], k.w_edge[:, :], k.w_edge_parts[:, i, :], ALU.subtract)\
                    .then_inc(edge_rest, 1)
                pool.tensor_tensor(k.edge_raw, k.edge_raw, k.edge_parts[:, i, :], ALU.subtract).then_inc(edge_rest, 1)
                pool.wait_ge(edge_rest, 2 * (i + 1))
                edge_parts(k, pool.tensor_copy, i + 1).then_inc(edge_part, 1)
            pool.wait_ge(src_landed, 16)
            for s in tab_stored:
                pool.wait_ge(s, 16 * NIB)
            pool.wait_ge(products_done, nth(2 * NIB - 1))
            stash_rows(pool, k, stash_landed, k.stash_saved, stash_staged, stash_turns)
            for c in range(1, RC):
                pool.tensor_copy(k.src_stage[:, c * CT:(c + 1) * CT], k.src_cols[:, c * CT:(c + 1) * CT])\
                    .then_inc(message.staged, 1)
            pool.wait_ge(message.staged, GC)
            message.gpsimd(pool)

        @block.tensor
        def _(pe):
            for s in (turned, w12_done, products_done):
                pe.sem_inc(s, CREDIT)
            pe.wait_ge(consts_ready, 1)
            pe.wait_ge(span_ready, 1)
            pe.transpose(span_row, k.span[:, 0:1], k.ident[0:QB, 0:QB]).then_inc(span_turned, 1)
            pe.wait_ge(early_landed, 16 * (3 + len(COLUMNS)))

            def turn(g, half):
                turn_rows(pe, k, 0, g, half, h_done, hT_done, turned)

            def products(g, half, more):
                if more or half == 0:
                    turn(g + 1, 1 - half)
                pe.wait_ge(hT_done, nth(g))
                pe.wait_ge(copied, nth(g - 1))
                for t in range(HB):
                    ins = pe.matmul(k.bank[2 + t // 2][0:NPART, (t % 2) * 2 * D:(t % 2 + 1) * 2 * D],
                                    k.hT[:, half, t, :], k.w12[:, :], start=True, stop=True)
                ins.then_inc(w12_done, 1)
                pe.wait_ge(nf_done, nth(g - 1))
                for i, (lo, hi) in enumerate(HALVES):
                    ins = pe.matmul(k.bank[6 + i][0:D, 0:(hi - lo) * NPART], k.w_node[:, :],
                                    k.hT[:, half, lo:hi, :].rearrange("p t n -> p (t n)"), start=True, stop=True)
                ins.then_inc(products_done, 1)

            turn(0, 0)
            half_turns(pe, products)
            pe.sem_inc(edge_mm, CREDIT)
            pe.wait_ge(stack_ready, 16 * NS * NS)
            pe.wait_ge(hT_done, nth(2 * NIB - 1))
            pe.wait_ge(copied, nth(2 * NIB - 1))
            with pe.Fori(0, NI) as it:
                for q in range(QI):
                    n = it * QI + q
                    if q % QC == 0:
                        pe.wait_ge(landed[q // QC], it * 16 + 16)
                    pe.wait_ge(edge_act, nth(n - SB))
                    pe.matmul(k.bank[q % SB][0:D, :], k.w_edge_stack[:, :],
                              k.estack[:, q // QC, (q % QC) * QE:(q % QC + 1) * QE], start=True, stop=True)\
                      .then_inc(edge_mm, 1)
            pe.wait_ge(shift_ready, 1)
            pe.matmul(k.bank[2][:, 0:D], k.aff_lhs[:, 0, :], k.w3[0:D, :], start=True, stop=True).then_inc(shift_done, 1)
            pe.wait_ge(w3e_ready, 1)
            pe.wait_ge(flag_done, 1)
            pe.wait_ge(nf_done, nth(2 * NIB - 1))
            message.tensor(pe)

        @block.scalar
        def _(act):
            for s in (h_done, copied):
                act.sem_inc(s, CREDIT)
            act.wait_ge(var_ready, 1)
            act.wait_ge(consts_ready, 1)
            act.activation(k.small[:, 3, :], k.small[:, 2, :], ACT.Sqrt, bias=k.eps[0:NPART, :]).then_inc(root_done, 1)
            act.wait_ge(norm_ready, 1)

            def copy_out(g, half, more):
                if more:
                    normal_rows(act, k, g + 2, half, turned, h_done)
                act.wait_ge(w12_done, nth(g))
                for b in range(-(-HB // 2)):
                    tiles = min(2, HB - 2 * b)
                    ins = act.copy(k.tables[:, ds(g * HB + 2 * b, tiles), :, :].rearrange("p a s d -> p (a s d)"),
                                   k.bank[2 + b][0:NPART, 0:tiles * 2 * D])
                ins.then_inc(copied, 1)

            for half in range(2):
                normal_rows(act, k, half, half, turned, h_done)
            act.wait_ge(edge_landed, 32)
            edge_parts(k, act.copy, 0).then_inc(edge_part, 1)
            half_turns(act, copy_out)
            act.wait_ge(copied, nth(2 * NIB - 1))
            act.wait_ge(parts_stored, 16 * NS)
            for i in range(XL):
                if i >= 2:
                    act.wait_ge(p2_stored[i % 2], 16 * (i // 2))
                for s, at in enumerate((0, 2, 1)):
                    if s:
                        act.wait_ge(p2_rest, (NS - 1) * i + s)
                    act.copy(p2_piece(k, i % 2)[:, :, at, :], k.tables[:, i * XB:(i + 1) * XB, 1, :])\
                       .then_inc(p2_part, 1)
            act.sem_inc(edge_act, CREDIT)
            with act.Fori(0, NI) as it:
                for q in range(QI):
                    n = it * QI + q
                    act.wait_ge(edge_mm, nth(n))
                    act.wait_ge(edge_stat, nth(n - SB))
                    act.activation(edge_buffer(k, q), k.bank[q % SB][0:D, :], ACT.Relu,
                                   bias=col(k, "L0_gnn_b_edge")).then_inc(edge_act, 1)
            act.wait_ge(edge_var, 1)
            act.activation(k.aff[:, 2:3], k.aff[:, 1:2], ACT.Sqrt, bias=k.eps[0:D, :]).then_inc(edge_root, 1)
            act.wait_ge(buffers_ready, 1)
            message.scalar(act)

        @block.vector
        def _(dve):
            link = linker(dve, dve_link)
            message.credit(dve)
            dve.memset(k.hT[D:P, :, :, :], 0.0).then_inc(hT_done, CREDIT)
            dve.wait_ge(dst_landed, 48)
            link(dve.tensor_copy(k.rel_rows[:, :, :], dst_q))
            link(dve.tensor_reduce(k.base_q[:, :], k.rel_rows[:, :, :], AX.X, ALU.min))
            dve.sem_inc(base_ready, 1)
            link(dve.tensor_tensor(k.rel_rows[:, :, :], k.rel_rows[:, :, :],
                                   k.base_q[:, :].unsqueeze(2).broadcast_to([QB, 2, QE]), ALU.subtract))
            link(dve.scalar_tensor_tensor(spans, k.rel_rows[:, :, :], FAR / 2, k.rel_rows[:, :, :], ALU.is_lt, ALU.mult))
            link(dve.tensor_reduce(k.span[:, 0:1], spans, AX.XY, ALU.max))
            dve.sem_inc(span_ready, 1)
            for b in range(NB):
                if b % XB == 0:
                    dve.wait_ge(x_landed[b // XB], 16)
                ins = dve.bn_stats(k.stats[:, b, :], k.xs[:, b, :])
            link(ins)
            layernorm_sums(dve, link, k)
            dve.sem_inc(var_ready, 1)
            dve.wait_ge(root_done, 1)
            layernorm_map(dve, link, k)
            dve.sem_inc(norm_ready, 1)
            dve.sem_inc(nf_done, CREDIT)
            dve.wait_ge(early_landed, 16 * (3 + len(COLUMNS)))
            dve.wait_ge(consts_ready, 1)

            def nodes(g, half, more):
                if more or half == 0:
                    columns_out(dve, k, 0, g + 1, 1 - half, turned, products_done, hT_done)
                dve.wait_ge(products_done, nth(g))
                for i, (lo, hi) in enumerate(HALVES):
                    w = (hi - lo) * NPART
                    ins = dve.tensor_scalar(k.nfT[0:D, ds((g * HB + lo) * NPART, w)], k.bank[6 + i][0:D, 0:w],
                                            col(k, "L0_gnn_b_node"), 0.0, ALU.add, ALU.max)
                ins.then_inc(nf_done, 1)
                dve.wait_ge(nf_done, nth(g))
                for i, (lo, hi) in enumerate(HALVES):
                    dve.bn_stats(tile_of(k.node_stats, g * 2 + i),
                                 k.nfT[0:D, ds((g * HB + lo) * NPART, (hi - lo) * NPART)])

            columns_out(dve, k, 0, 0, 0, turned, products_done, hT_done)
            half_turns(dve, nodes)
            for i in range(XL):
                rest = k.tables[:, i * XB:(i + 1) * XB, 1, :]
                for s, at in ((0, 0), (1, 2)):
                    dve.wait_ge(p2_part, NS * i + s + 1)
                    dve.tensor_tensor(rest, rest, p2_piece(k, i % 2)[:, :, at, :], ALU.subtract).then_inc(p2_rest, 1)
            dve.wait_ge(base_back, 16)
            dve.wait_ge(cols_ready, 2)
            link(dve.tensor_tensor(k.rel_cols[:, :, :], k.rel_cols[:, :, :],
                                   k.base_all[:, :].unsqueeze(2).broadcast_to([P, NQ, TQ]), ALU.subtract))
            clip_windows(dve, link, k, clipped)
            dve.wait_ge(span_turned, 1)
            link(dve.tensor_reduce(k.span[0:1, 1:2], span_row, AX.X, ALU.max))
            link(dve.tensor_scalar(k.flag[:, :], k.span[0:1, 1:2], float(W), None, ALU.is_ge))
            dve.sem_inc(flag_done, 1)
            dve.wait_ge(parts_stored, 16 * NS)
            link(dve.memset(k.edgeT[D:P, :, :], 0.0))
            link(dve.memset(k.edgeT[D:D + 1, :, :], 1.0))
            dve.sem_inc(edge_stat, CREDIT)
            with dve.Fori(0, NI) as it:
                for q in range(QI):
                    n = it * QI + q
                    dve.wait_ge(edge_act, nth(n))
                    dve.bn_stats(tile_of(k.edge_stats, n), edge_buffer(k, q)).then_inc(edge_stat, 1)
            dve.wait_ge(edge_stat, nth(NQ - 1))
            link(dve.bn_stats(k.edge_stats[:, NQ - 1, :], edge_buffer(k, NQ - 1)[:, 0:LASTV]))
            dve.sem_inc(buffers_ready, 1)
            link(dve.bn_aggr(k.aff[:, 0:2], k.edge_stats[:, :, :].rearrange("p a b -> p (a b)")))
            dve.sem_inc(edge_var, 1)
            dve.wait_ge(edge_root, 1)
            affine(dve, link, k, 0, "edge")
            dve.wait_ge(sums_cleared, 1)
            dve.wait_ge(weights_landed, 16 * 7)
            link(dve.tensor_copy(k.aff_lhs[:, 0, D:D + 1], k.aff[:, 5:6]))
            dve.sem_inc(shift_ready, 1)
            link(dve.tensor_scalar(k.w3e[0:D, :], k.w3[0:D, :], k.aff[:, 4:5], None, ALU.mult))
            dve.wait_ge(shift_done, 1)
            link(dve.tensor_tensor(k.w3e[D:D + 1, :], k.bank[2][D:D + 1, 0:D], k.b_msg_row[D:D + 1, :], ALU.add))
            dve.sem_inc(w3e_ready, 1)
            message.vector(dve)
    end_phase(nc, sems + x_landed + message.sems)


def load_stack(sp, k, room, chunk):
    return sp.dma_start(k.estack[:, room, :], k.edge_tab[:, ds(chunk * QC * QE, QC * QE)].unsqueeze(0)
                        .broadcast_to([NS, NS * DE, QC * QE]))


def edge_parts(k, copy, i):
    copy(k.w_edge_parts[:, i, :], k.w_edge[:, :])
    return copy(k.edge_parts[:, i, :], k.edge_raw)


def edge_buffer(k, q):
    return (k.edgeT if q % SB < 2 else k.edgeT_more)[0:D, q % 2, :]


def p2_piece(k, i):
    return k.p2_room[:, i, :].rearrange("p (t s d) -> p t s d", t=NB // XL, s=NS)


def gather_tiles(pool, k, c, landed):
    for t in range(c * CT, (c + 1) * CT):
        pool.indirect_dma_start(k.gathered[:, t, :], None, k.gather_tab,
                                bass.IndirectOffsetOnAxis(ap=k.src_stage[:, t:t + 1], axis=0)).then_inc(landed[c], 16)


def stash_place(n):
    return 1 + (n - NIT) % GC


def stash_uses(c):
    return sum(stash_place(n) == c for n in range(NIT))


def stash_rows(pool, k, landed, saved, staged, turns):
    def gather(n, i):
        c = stash_place(i)
        pool.tensor_copy(k.src_stage[:, c * CT:(c + 1) * CT], k.src_cols[:, ds(n * TR, CT)]).then_inc(staged, 1)
        pool.wait_ge(staged, n + 1)
        pool.sem_inc(turns, 1)
        gather_tiles(pool, k, c, landed)

    def save(n, i, times):
        c = stash_place(i)
        pool.wait_ge(landed[c], times * (16 * CT))
        pool.sem_inc(turns, 1)
        pool.dma_start(k.stash_tab[:, ds(n, 1), :].rearrange("p a w -> p (a w)"),
                       k.gathered[:, c * CT:(c + 1) * CT, :].rearrange("p t d -> p (t d)")).then_inc(saved[c], 16)

    for i in range(GC):
        gather(i, i)
        if i >= 1:
            save(i - 1, i - 1, 1)
    with pool.Fori(1, NIT // GC) as it:
        for i in range(GC):
            pool.wait_ge(saved[stash_place(i)], it * 16)
            pool.sem_inc(turns, 1)
            gather(it * GC + i, i)
            save(it * GC + i - 1, (i - 1) % GC, it + 1 if i else it)
    for n in range(NIT - NIT % GC, NIT):
        pool.wait_ge(saved[stash_place(n)], n // GC * 16)
        gather(n, n)
        save(n - 1, n - 1, (n - 1) // GC + 1)
    save(NIT - 1, NIT - 1, (NIT - 1) // GC + 1)
    for c in range(1, RC):
        pool.wait_ge(saved[c], stash_uses(c) * 16)


def gather_rows(pool, k, ring, staged, used, turns, first):
    with pool.Fori(0, NIT) as it:
        for c in range(first, RC):
            pool.wait_ge(staged, it * (RC - first) + c - first + 1)
            pool.wait_ge(used, nth(it * QR + c * QC + QC - 1 - QR))
            pool.sem_inc(turns, 1)
            gather_tiles(pool, k, c, ring)
    for c in range(first, RC):
        pool.wait_ge(ring[c], NIT * 16 * CT)


def stage_first(act, k, staged, first):
    for c in range(first, RC):
        act.copy(k.src_stage[:, c * CT:(c + 1) * CT], k.src_cols[:, c * CT:(c + 1) * CT]).then_inc(staged, 1)


def stage_next(act, k, it, c, ring, staged):
    act.wait_ge(ring[c], it * (16 * CT) + 16 * CT)
    act.copy(k.src_stage[:, c * CT:(c + 1) * CT], k.src_cols[:, ds((it + 1) * TR + c * CT, CT)]).then_inc(staged, 1)


def window_base(eng, k, n):
    return eng.value_load(k.base_int[0:1, ds(n, 1)], min_val=0, max_val=N)


def turns_of_quads(eng, step):
    with eng.Fori(0, NIT - 1) as it:
        step(it, False)
    step(NIT - 1, True)


class MessagePass:

    def __init__(self, nc, k, ring):
        self.k, self.ring = k, ring
        self.sems = named(nc, k, "staged", "turns", "add_done", "edge_product", "edge_relu",
                          "onehotT_done", "onehot_done", "pre_done", "relu_done", "square_done", "seg_done", "sum_done",
                 "rows_landed0", "rows_landed1", "est_landed0", "est_landed1", "p2_landed0", "p2_landed1",
                          "reloaded")
        (self.staged, self.turns, self.add_done, self.edge_product, self.edge_relu, self.onehotT_done,
         self.onehot_done, self.pre_done, self.relu_done, self.square_done, self.seg_done, self.sum_done) = self.sems[0:12]
        self.rows_landed, self.est_landed, self.p2_landed = self.sems[12:14], self.sems[14:16], self.sems[16:18]
        self.reloaded = self.sems[18]

    def gpsimd(self, pool):
        gather_rows(pool, self.k, self.ring, self.staged, self.add_done, self.turns, 1)

    def sync(self, sp):
        k = self.k
        with sp.Fori(0, NIT) as it:
            for c in range(RC):
                last = it * QR + (c - 2) * QC + QC - 1
                i = it * RC + c
                sp.wait_ge(self.edge_product, nth(last))
                load_stack(sp, k, c % 2, i).then_inc(self.est_landed[c % 2], 16)
                sp.wait_ge(self.onehotT_done, nth(last))
                sp.dma_start(k.drow[:, c % 2, :], k.rel_tab[ds(i * QC, QC), :].rearrange("q e -> (q e)")
                             .unsqueeze(0).broadcast_to([P, QC * QE])).then_inc(self.rows_landed[c % 2], 16)
                if c == 0:
                    sp.wait_ge(k.stash_saved[stash_place(0)], 16)
                    sp.wait_ge(self.add_done, nth(it * QR + QC - 1 - QR))
                    sp.dma_start(k.gathered[:, 0:CT, :].rearrange("p t d -> p (t d)"),
                                 k.stash_tab[:, ds(it, 1), :].rearrange("p a w -> p (a w)")).then_inc(self.reloaded, 16)
                if c == 1:
                    for s in range(1, RC):
                        sp.wait_ge(k.stash_saved[s], stash_uses(s) * 16)
                bases = [window_base(sp, k, it * QR + c * QC + q) for q in range(QC)]
                sp.wait_ge(self.pre_done, nth(last))
                for q in range(QC):
                    slot = (c % 2) * QC + q
                    sp.dma_start(k.p2w[0:W, slot, :], k.p2_tab[ds(bases[q], W), 0:2 * D]).then_inc(self.p2_landed[c % 2], 16)
                    sp.dma_start(k.p2w[W:P, slot, 0:D], k.p2_tab[ds(bases[q], W), 2 * D:3 * D])\
                      .then_inc(self.p2_landed[c % 2], 16)

    def tensor(self, pe):
        k = self.k
        for s in (self.edge_product, self.pre_done, self.seg_done):
            pe.sem_inc(s, CREDIT)

        def edge(it, q):
            it, q = it + q // QR, q % QR
            if q % QC == 0:
                pe.wait_ge(self.est_landed[q // QC % 2], it * (16 * RC // 2) + 16 * (q // QC // 2 + 1))
            pe.wait_ge(self.edge_relu, nth(it * QR + q - 2))
            pe.matmul(k.bank[q % 2][0:D, :], k.w_edge_stack[:, :],
                      k.estack[:, q // QC % 2, (q % QC) * QE:(q % QC + 1) * QE], start=True, stop=True)\
              .then_inc(self.edge_product, 1)

        def message(it, q):
            it, q = it + q // QR, q % QR
            n = it * QR + q
            c = q // QC
            if q % QC == 0:
                pe.wait_ge(self.p2_landed[c % 2], it * (32 * QC * RC // 2) + 32 * QC * (c // 2 + 1))
            pe.wait_ge(self.edge_relu, nth(n))
            pe.wait_ge(self.onehotT_done, nth(n))
            pe.wait_ge(self.add_done, nth(n - 2))
            slot = (c % 2) * QC + q % QC
            for j in range(TQ):
                out = k.bank[2 + q % 2][:, j * D:(j + 1) * D]
                e = slice(j * P, (j + 1) * P)
                pe.matmul(out, k.onehotT[:, q % 2, e], k.p2w[:, slot, 0:D], start=True, stop=False)
                pe.matmul(out, k.onehotT[0:W, q % 2, e], k.p2w[0:W, slot, D:2 * D], start=False, stop=False)
                ins = pe.matmul(out, k.edgeT[:, q % 2, e], k.w3e[:, :], start=False, stop=True)
            ins.then_inc(self.pre_done, 1)

        def sums(it, q):
            n = it * QR + q
            pe.wait_ge(self.square_done, nth(n))
            pe.wait_ge(self.onehot_done, nth(n))
            pe.wait_ge(self.sum_done, nth(n - 2))
            for j in range(TQ):
                pe.matmul(k.bank[4 + q % 2][0:D + 2, 0:W], k.msg[:, q % 2, j, 0:D + 2], k.onehot[:, q % 2, j, :],
                          start=(j == 0), stop=(j == TQ - 1))
            for j in range(TQ):
                ins = pe.matmul(k.bank[6 + q % 2][0:1, 0:D], k.msg[:, q % 2, j, D:D + 1],
                                k.msg_sq[:, q % 2, j, :], start=(j == 0), stop=(j == TQ - 1))
            ins.then_inc(self.seg_done, 1)

        def turn(it, last):
            for q in range(1, QR if last else QR + 1):
                if not last or q + 1 < QR:
                    edge(it, q + 1)
                message(it, q)
                sums(it, q - 1)
            if last:
                sums(it, QR - 1)

        edge(0, 0)
        edge(0, 1)
        message(0, 0)
        turns_of_quads(pe, turn)

    def stage_first(self, act):
        stage_first(act, self.k, self.staged, 1)

    def scalar(self, act):
        k, ring = self.k, self.ring
        for s in (self.edge_relu, self.relu_done, self.square_done):
            act.sem_inc(s, CREDIT)

        def edge(it, q):
            it, q = it + q // QR, q % QR
            n = it * QR + q
            act.wait_ge(self.edge_product, nth(n))
            act.wait_ge(self.pre_done, nth(n - 2))
            act.activation(k.edgeT[0:D, q % 2, :], k.bank[q % 2][0:D, :], ACT.Relu,
                           bias=col(k, "L0_gnn_b_edge")).then_inc(self.edge_relu, 1)

        def turn(it, last):
            for q in range(QR):
                n = it * QR + q
                if not last or q + 1 < QR:
                    edge(it, q + 1)
                if q % QC == 0 and q // QC >= 1:
                    stage_next(act, k, it, q // QC, ring, self.staged)
                act.wait_ge(self.add_done, nth(n))
                act.wait_ge(self.seg_done, nth(n - 2))
                act.activation(k.msg[:, q % 2, :, 0:D], k.pre[:, q % 2, :, :], ACT.Relu).then_inc(self.relu_done, 1)
                act.wait_ge(self.relu_done, nth(n))
                act.activation(k.msg_sq[:, q % 2, :, :], k.msg[:, q % 2, :, 0:D], ACT.Square)\
                   .then_inc(self.square_done, 1)

        edge(0, 0)
        turns_of_quads(act, turn)

    def credit(self, dve):
        for s in (self.add_done, self.onehotT_done, self.onehot_done, self.sum_done):
            dve.sem_inc(s, CREDIT)

    def vector(self, dve):
        k, ring = self.k, self.ring

        def targets_by_node(it, q):
            it, q = it + q // QR, q % QR
            n = it * QR + q
            c = q // QC
            if q % QC == 0:
                dve.wait_ge(self.rows_landed[c % 2], it * (16 * RC // 2) + 16 * (c // 2 + 1))
            dve.wait_ge(self.pre_done, nth(n - 2))
            dve.tensor_scalar(k.onehotT[:, q % 2, :], k.drow[:, c % 2, (q % QC) * QE:(q % QC + 1) * QE],
                              k.node_of_row[:, :], None, ALU.is_equal).then_inc(self.onehotT_done, 1)

        def targets_by_edge(it, q):
            it, q = it + q // QR, q % QR
            n = it * QR + q
            dve.wait_ge(self.seg_done, nth(n - 2))
            dve.tensor_copy(k.msg[:, q % 2, :, D:D + 2], k.edge_cols[:, ds(n * TQ, TQ), :])
            dve.tensor_tensor(k.onehot[:, q % 2, :, :], k.iota[:, :].unsqueeze(1).broadcast_to([P, TQ, W]),
                              k.rel_cols[:, ds(n, 1), :].rearrange("p a j -> p (a j)").unsqueeze(2)
                              .broadcast_to([P, TQ, W]), ALU.is_equal).then_inc(self.onehot_done, 1)

        def add_sums(it, q):
            n = it * QR + q
            base = window_base(dve, k, n)
            dve.wait_ge(self.seg_done, nth(n))
            dve.wait_ge(self.sum_done, nth(n - 1))
            window = k.aggT[0:D + 2, ds(base, W)]
            dve.tensor_tensor(window, window, k.bank[4 + q % 2][0:D + 2, 0:W], ALU.add)
            dve.tensor_tensor(k.sq_sum[:, :], k.sq_sum[:, :], k.bank[6 + q % 2][0:1, 0:D], ALU.add)\
               .then_inc(self.sum_done, 1)

        def add_rows(it, q):
            it, q = it + q // QR, q % QR
            n = it * QR + q
            if q == 0:
                dve.wait_ge(self.reloaded, it * 16 + 16)
            elif q % QC == 0:
                dve.wait_ge(ring[q // QC], it * (16 * CT) + 16 * CT)
            dve.wait_ge(self.pre_done, nth(n))
            dve.wait_ge(self.relu_done, nth(n - 2))
            dve.tensor_tensor(k.pre[:, q % 2, :, :], k.gathered[:, q * TQ:(q + 1) * TQ, :],
                              k.bank[2 + q % 2][:, 0:TQ * D].rearrange("p (j d) -> p j d", j=TQ), ALU.add)\
               .then_inc(self.add_done, 1)

        def turn(it, last):
            for q in range(1, QR if last else QR + 1):
                if not last or q + 1 < QR:
                    targets_by_node(it, q + 1)
                add_rows(it, q)
                if not last or q + 1 < QR:
                    targets_by_edge(it, q + 1)
                add_sums(it, q - 1)
            if last:
                add_sums(it, QR - 1)

        targets_by_node(0, 0)
        targets_by_edge(0, 0)
        targets_by_node(0, 1)
        add_rows(0, 0)
        targets_by_edge(0, 1)
        turns_of_quads(dve, turn)


def message_pass(nc, k, ring):
    message = MessagePass(nc, k, ring)
    with nc.Block() as block:
        @block.gpsimd
        def _(pool):
            message.gpsimd(pool)

        @block.sync
        def _(sp):
            message.sync(sp)

        @block.tensor
        def _(pe):
            message.tensor(pe)

        @block.scalar
        def _(act):
            message.stage_first(act)
            message.scalar(act)

        @block.vector
        def _(dve):
            message.credit(dve)
            message.vector(dve)
    end_phase(nc, message.sems)


def gcn_pass(nc, k, ring, layer=None):
    sems = named(nc, k, "staged", "turns", "onehot_done", "seg_done", "sum_done",
                 "pick_done", "own_link")
    staged, turns, onehot_done, seg_done, sum_done, pick_done, own_link = sems
    with nc.Block() as block:
        @block.gpsimd
        def _(pool):
            gather_rows(pool, k, ring, staged, seg_done, turns, 0)

        @block.scalar
        def _(act):
            stage_first(act, k, staged, 0)
            with act.Fori(0, NIT) as it:
                for c in range(RC):
                    stage_next(act, k, it, c, ring, staged)

        @block.tensor
        def _(pe):
            pe.sem_inc(seg_done, CREDIT)
            with pe.Fori(0, NIT) as it:
                for q in range(QR):
                    n = it * QR + q
                    if q % QC == 0:
                        pe.wait_ge(ring[q // QC], it * (16 * CT) + 16 * CT)
                    pe.wait_ge(onehot_done, nth(n))
                    pe.wait_ge(sum_done, nth(n - 2))
                    for j in range(TQ):
                        ins = pe.matmul(k.bank[q % 2][0:D, 0:W], k.gathered[:, q * TQ + j, :], k.onehot[:, q % 2, j, :],
                                        start=(j == 0), stop=(j == TQ - 1))
                    ins.then_inc(seg_done, 1)

        @block.vector
        def _(dve):
            for s in (sum_done, onehot_done, pick_done):
                dve.sem_inc(s, CREDIT)
            if layer is not None:
                link = linker(dve, own_link)
                own = k.tables[:, :, 0, :]
                link(dve.tensor_tensor(own, own, k.dinv[:, :].unsqueeze(2).broadcast_to([NPART, NB, D]), ALU.mult))
                link(dve.tensor_tensor(own, own, k.b_gcn[:, layer, :].unsqueeze(1).broadcast_to([NPART, NB, D]), ALU.add))

            def weights(it, q):
                n = it * QR + q
                dve.wait_ge(seg_done, nth(n - 2))
                hot = k.onehot[:, q % 2, :, :]
                dve.tensor_tensor(hot, k.iota[:, :].unsqueeze(1).broadcast_to([P, TQ, W]),
                                  k.rel_cols[:, ds(n, 1), :].rearrange("p a j -> p (a j)").unsqueeze(2)
                                  .broadcast_to([P, TQ, W]), ALU.is_equal).then_inc(pick_done, 1)
                dve.wait_ge(pick_done, nth(n))
                dve.tensor_tensor(hot, hot, k.edge_cols[:, ds(n * TQ, TQ), 1:2].broadcast_to([P, TQ, W]), ALU.mult)\
                   .then_inc(onehot_done, 1)

            def add_sums(it, q):
                n = it * QR + q
                base = window_base(dve, k, n)
                dve.wait_ge(seg_done, nth(n))
                dve.wait_ge(sum_done, nth(n - 1))
                window = k.aggT[0:D, ds(base, W)]
                dve.tensor_tensor(window, window, k.bank[q % 2][0:D, 0:W], ALU.add).then_inc(sum_done, 1)

            with dve.Fori(0, NIT) as it:
                weights(it, 0)
                for q in range(QR):
                    if q + 1 < QR:
                        weights(it, q + 1)
                    add_sums(it, q)
    end_phase(nc, sems)


def restart_ring(nc, ring):
    nc.all_engine_barrier()
    nc.gpsimd.dma_reset(range(ring[0].num, ring[-1].num + 1))
    for s in ring:
        nc.gpsimd.sem_clear(s)
    nc.all_engine_barrier()


def further_windows(nc, k, ring, run):
    wide = nc.values_load(k.flag[0:1, 0:1], min_val=0, max_val=1)
    with nc.If(wide > 0):
        with nc.Fori(1, ROUNDS):
            restart_ring(nc, ring)
            move_windows(nc, k, W)
            run(nc, k, ring)
        move_windows(nc, k, -W * (ROUNDS - 1))


def copy_sums(act, k, g, half, read, copied):
    by_tile = k.aggT[:, 0:N].rearrange("k (p b) -> k b p", b=NB)
    act.wait_ge(read, nth(g - 2))
    act.copy(k.sumT[:, half, :, :], by_tile[:, ds(g * HB, HB), :]).then_inc(copied, 1)


def clear_sums(pool, k, copied, cleared):
    pool.wait_ge(copied, nth(2 * NIB - 1))
    pool.memset(k.aggT[0:D, :], 0.0).then_inc(cleared, 1)
    pool.wait_ge(cleared, 1)


def between_phase(nc, k):
    sems = named(nc, k, "dve_link", "square_turned", "var_ready", "root_done", "maps_ready", "maps_done", "sum_product",
                 "added", "deg_ready", "deg_root", "sum_copied", "node_copied", "norm_ready", "cleared")
    (link_sem, square_turned, var_ready, root_done, maps_ready, maps_done, sum_product, added, deg_ready,
     deg_root, sum_copied, node_copied, norm_ready, cleared) = sems
    table = TableProduct(nc, k, 0)
    c = k.aff
    with nc.Block() as block:
        @block.gpsimd
        def _(pool):
            clear_sums(pool, k, sum_copied, cleared)

        @block.tensor
        def _(pe):
            pe.matmul(k.bank[0][0:D, 0:1], k.sq_sum[0:1, :], k.ones[0:1, 0:1], start=True, stop=True)\
              .then_inc(square_turned, 1)
            pe.wait_ge(maps_ready, 1)
            for i in range(2):
                ins = pe.matmul(k.bank[1][:, i * D:(i + 1) * D], k.aff_lhs[:, i, :], k.ident[0:D, 0:D],
                                start=True, stop=True)
            ins.then_inc(maps_done, 1)
            pe.sem_inc(sum_product, CREDIT)
            pe.wait_ge(maps_ready, 2)
            with pe.Fori(0, NIB) as it:
                for half in range(2):
                    g = it * 2 + half
                    pe.wait_ge(added, nth(g - 2))
                    pe.wait_ge(sum_copied, nth(g))
                    pe.wait_ge(node_copied, nth(g))
                    for t in range(HB):
                        out = k.bank[2 + half][0:NPART, t * (D + 1):(t + 1) * (D + 1)]
                        pe.matmul(out, k.sumT[:, half, t, :], k.aff_msg[:, :], start=True, stop=False)
                        ins = pe.matmul(out, k.nodeT[:, half, t, :], k.aff_node[:, :], start=False, stop=True)
                    ins.then_inc(sum_product, 1)
            table.credit_tensor(pe)

            def step(g, half, more):
                if more or half == 0:
                    table.turn(pe, g + 1, 1 - half)
                table.products(pe, g, half)

            table.turn(pe, 0, 0)
            half_turns(pe, step)

        @block.scalar
        def _(act):
            act.sem_inc(node_copied, CREDIT)
            act.sem_inc(sum_copied, CREDIT)
            act.wait_ge(var_ready, 1)
            for o in (8, 16):
                ins = act.activation(c[:, o + 2:o + 3], c[:, o + 1:o + 2], ACT.Sqrt, bias=k.eps[0:D, :])
            ins.then_inc(root_done, 1)
            with act.Fori(0, NIB) as it:
                for half in range(2):
                    g = it * 2 + half
                    copy_sums(act, k, g, half, sum_product, sum_copied)
                    act.copy(k.nodeT[:, half, :, :].rearrange("p t n -> p (t n)"),
                             k.nfT[:, ds(g * HB * NPART, HB * NPART)]).then_inc(node_copied, 1)
            act.wait_ge(deg_ready, 1)
            act.activation(k.deg[:, 1, :], k.deg[:, 0, :], ACT.Sqrt)
            act.activation(k.small[:, 3, :], k.small[:, 2, :], ACT.Sqrt, bias=k.eps[0:NPART, :]).then_inc(deg_root, 1)
            act.wait_ge(norm_ready, 1)
            act.sem_inc(table.h_done, CREDIT)
            with act.Fori(0, NIB) as it:
                for half in range(2):
                    normal_rows(act, k, it * 2 + half, half, table.turned, table.h_done)

        @block.vector
        def _(dve):
            link = linker(dve, link_sem)
            dve.bn_aggr(c[:, 8:10], k.node_stats[:, :, :].rearrange("p a b -> p (a b)"))
            link(dve.tensor_reduce(c[:, 16:17], k.aggT[0:D, 0:N], AX.X, ALU.add))
            link(dve.tensor_scalar(c[:, 16:17], c[:, 16:17], 1.0 / E, None, ALU.mult))
            link(dve.tensor_tensor(c[:, 22:23], c[:, 16:17], c[:, 16:17], ALU.mult))
            dve.wait_ge(square_turned, 1)
            link(dve.scalar_tensor_tensor(c[:, 17:18], k.bank[0][0:D, 0:1], 1.0 / E, c[:, 22:23], ALU.mult, ALU.subtract))
            link(dve.tensor_scalar(c[:, 17:18], c[:, 17:18], 0.0, None, ALU.max))
            dve.sem_inc(var_ready, 1)
            dve.wait_ge(root_done, 1)
            affine(dve, link, k, 8, "node")
            affine(dve, link, k, 16, "msg")
            for i, o in ((0, 16), (1, 8)):
                dve.tensor_scalar(k.aff_lhs[:, i, 0:D], k.ident[0:D, 0:D], c[:, o + 4:o + 5], None, ALU.mult)
                link(dve.tensor_copy(k.aff_lhs[:, i, D:D + 1], c[:, o + 5:o + 6]))
            dve.sem_inc(maps_ready, 1)
            dve.wait_ge(maps_done, 1)
            dve.tensor_copy(k.aff_msg[:, 0:D], k.bank[1][:, 0:D])
            dve.tensor_copy(k.aff_msg[:, D:D + 1], k.ident[:, D + 1:D + 2])
            link(dve.tensor_copy(k.aff_node[:, 0:D], k.bank[1][:, D:2 * D]))
            dve.sem_inc(maps_ready, 1)
            dve.sem_inc(added, CREDIT)
            with dve.Fori(0, NIB) as it:
                for half in range(2):
                    g = it * 2 + half
                    dve.wait_ge(sum_product, nth(g))
                    got = k.bank[2 + half][0:NPART, 0:HB * (D + 1)].rearrange("p (t d) -> p t d", t=HB)
                    xt = k.xs[:, ds(g * HB, HB), :]
                    dve.tensor_scalar(k.deg[:, 0:1, ds(g * HB, HB)].rearrange("p a t -> p t a"), got[:, :, D:D + 1],
                                      1.0, None, ALU.add)
                    dve.tensor_tensor(xt, xt, got[:, :, 0:D], ALU.add).then_inc(added, 1)
                    dve.wait_ge(added, nth(g))
                    for t in range(HB):
                        dve.bn_stats(tile_of_turn(k.stats, g, t), tile_of_turn(k.xs, g, t))
            dve.wait_ge(added, nth(2 * NIB - 1))
            link(dve.tensor_scalar(k.deg[:, 2, :], k.deg[:, 0, :], 0.0, None, ALU.is_gt))
            link(dve.tensor_scalar(k.deg[:, 0, :], k.deg[:, 0, :], 1e-30, None, ALU.max))
            layernorm_sums(dve, link, k)
            dve.sem_inc(deg_ready, 1)
            dve.wait_ge(deg_root, 1)
            layernorm_map(dve, link, k)
            link(dve.reciprocal(k.dinv[:, :], k.deg[:, 1, :]))
            link(dve.tensor_tensor(k.dinv[:, :], k.dinv[:, :], k.deg[:, 2, :], ALU.mult))
            dve.sem_inc(norm_ready, 1)
            table.credit_vector(dve)

            def step(g, half, more):
                if more or half == 0:
                    table.columns(dve, g + 1, 1 - half)
                table.scale(dve, g, half)

            table.columns(dve, 0, 0)
            half_turns(dve, step)

        @block.sync
        def _(sp):
            table.sync(sp)
    end_phase(nc, sems + table.sems)


class TableProduct:

    def __init__(self, nc, k, layer):
        self.k, self.layer = k, layer
        self.sems = named(nc, k, "t_h_done", "t_turned", "t_hT_done", "t_products_done", "t_scaled", "t_stored0",
                          "t_stored1")
        self.h_done, self.turned, self.hT_done, self.products_done, self.scaled, stored0, stored1 = self.sems
        self.stored = (stored0, stored1)

    def credit_tensor(self, pe):
        for s in (self.turned, self.products_done):
            pe.sem_inc(s, CREDIT)

    def credit_vector(self, dve):
        dve.sem_inc(self.scaled, CREDIT)
        dve.memset(self.k.hT[D:P, :, :, :], 0.0).then_inc(self.hT_done, CREDIT)

    def turn(self, pe, g, half):
        turn_rows(pe, self.k, 4, g, half, self.h_done, self.hT_done, self.turned)

    def products(self, pe, g, half):
        k = self.k
        pe.wait_ge(self.hT_done, nth(g))
        pe.wait_ge(self.scaled, nth(g - 2))
        for t in range(HB):
            ins = pe.matmul(k.bank[6 + half][0:NPART, t * D:(t + 1) * D], k.hT[:, half, t, :],
                            k.w_gcn[:, self.layer, :], start=True, stop=True)
        ins.then_inc(self.products_done, 1)

    def columns(self, dve, g, half):
        columns_out(dve, self.k, 4, g, half, self.turned, self.products_done, self.hT_done)

    def scale(self, dve, g, half):
        k = self.k
        dve.wait_ge(self.products_done, nth(g))
        dve.tensor_tensor(k.tables[:, ds(g * HB, HB), 0, :],
                          k.bank[6 + half][0:NPART, 0:HB * D].rearrange("p (t d) -> p t d", t=HB),
                          by_node(k, g), ALU.mult).then_inc(self.scaled, 1)

    def sync(self, sp):
        k = self.k
        tab = k.gather_tab.rearrange("(p b) d -> p b d", b=NB)
        with sp.Fori(0, NIB) as it:
            for half in range(2):
                g = it * 2 + half
                sp.wait_ge(self.scaled, nth(g))
                sp.dma_start(tab[:, ds(g * HB, HB), :], k.tables[:, ds(g * HB, HB), 0, :])\
                    .then_inc(self.stored[half], 16)
        for s in self.stored:
            sp.wait_ge(s, NIB * 16)


def by_node(k, g):
    return k.dinv[:, ds(g * HB, HB)].unsqueeze(2).broadcast_to([NPART, HB, D])


def turn_sums(pe, k, g, half, copied, read, turned):
    pe.wait_ge(copied, nth(g))
    pe.wait_ge(read, nth(g - 2))
    for t in range(HB):
        ins = pe.transpose(k.bank[half][0:NPART, t * D:(t + 1) * D], k.sumT[0:D, half, t, :], k.ident[0:D, 0:D])
    ins.then_inc(turned, 1)


def mix_rows(dve, k, g, half, turned, spread, mixed):
    u = k.mix_room[:, half, :, :]
    dve.wait_ge(turned, nth(g))
    dve.tensor_tensor(u, k.bank[half][0:NPART, 0:HB * D].rearrange("p (t d) -> p t d", t=HB), by_node(k, g), ALU.mult)\
       .then_inc(spread, 1)
    dve.wait_ge(spread, nth(g))
    dve.tensor_tensor(u, u, k.tables[:, ds(g * HB, HB), 0, :], ALU.add).then_inc(mixed, 1)


def second_table_phase(nc, k):
    sems = named(nc, k, "sum_copied", "sum_turned", "spread", "mixed", "cleared")
    sum_copied, sum_turned, spread, mixed, cleared = sems
    table = TableProduct(nc, k, 1)
    with nc.Block() as block:
        @block.gpsimd
        def _(pool):
            clear_sums(pool, k, sum_copied, cleared)

        @block.tensor
        def _(pe):
            pe.sem_inc(sum_turned, CREDIT)
            table.credit_tensor(pe)

            def step(g, half, more):
                if more:
                    turn_sums(pe, k, g + 2, half, sum_copied, spread, sum_turned)
                if more or half == 0:
                    table.turn(pe, g + 1, 1 - half)
                table.products(pe, g, half)

            for half in range(2):
                turn_sums(pe, k, half, half, sum_copied, spread, sum_turned)
            table.turn(pe, 0, 0)
            half_turns(pe, step)

        @block.scalar
        def _(act):
            for s in (sum_copied, table.h_done):
                act.sem_inc(s, CREDIT)

            def rows(g, half):
                act.wait_ge(mixed, nth(g))
                act.wait_ge(table.turned, nth(g - 2))
                act.activation(k.h[:, half, :, :], k.mix_room[:, half, :, :], ACT.Relu).then_inc(table.h_done, 1)

            def step(g, half, more):
                if more:
                    copy_sums(act, k, g + 2, half, sum_turned, sum_copied)
                if more or half == 0:
                    rows(g + 1, 1 - half)

            for half in range(2):
                copy_sums(act, k, half, half, sum_turned, sum_copied)
            rows(0, 0)
            half_turns(act, step)

        @block.vector
        def _(dve):
            for s in (spread, mixed):
                dve.sem_inc(s, CREDIT)
            table.credit_vector(dve)

            def mix(g, half):
                dve.wait_ge(table.h_done, nth(g - 2))
                mix_rows(dve, k, g, half, sum_turned, spread, mixed)

            def step(g, half, more):
                if more:
                    mix(g + 2, half)
                if more or half == 0:
                    table.columns(dve, g + 1, 1 - half)
                table.scale(dve, g, half)

            for half in range(2):
                mix(half, half)
            table.columns(dve, 0, 0)
            half_turns(dve, step)

        @block.sync
        def _(sp):
            table.sync(sp)
    end_phase(nc, sems + table.sems)


def output_phase(nc, k, out):
    sems = named(nc, k, "sum_copied", "sum_turned", "spread", "mixed", "out_done", "stored0", "stored1")
    sum_copied, sum_turned, spread, mixed, out_done, stored0, stored1 = sems
    stored = (stored0, stored1)
    rows = out.rearrange("(p b) d -> p b d", b=NB)
    with nc.Block() as block:
        @block.scalar
        def _(act):
            act.sem_inc(sum_copied, CREDIT)
            with act.Fori(0, NIB) as it:
                for half in range(2):
                    copy_sums(act, k, it * 2 + half, half, sum_turned, sum_copied)

        @block.tensor
        def _(pe):
            pe.sem_inc(sum_turned, CREDIT)
            with pe.Fori(0, NIB) as it:
                for half in range(2):
                    turn_sums(pe, k, it * 2 + half, half, sum_copied, spread, sum_turned)

        @block.vector
        def _(dve):
            for s in (spread, mixed, out_done):
                dve.sem_inc(s, CREDIT)

            def mix(g, half):
                dve.wait_ge(out_done, nth(g - 2))
                mix_rows(dve, k, g, half, sum_turned, spread, mixed)

            def add(g, half, more):
                if more or half == 0:
                    mix(g + 1, 1 - half)
                dve.wait_ge(mixed, nth(g))
                xt = k.xs[:, ds(g * HB, HB), :]
                dve.scalar_tensor_tensor(xt, k.mix_room[:, half, :, :], 0.0, xt, ALU.max, ALU.add).then_inc(out_done, 1)

            mix(0, 0)
            half_turns(dve, add)

        @block.sync
        def _(sp):
            with sp.Fori(0, NIB) as it:
                for half in range(2):
                    g = it * 2 + half
                    sp.wait_ge(out_done, nth(g))
                    sp.dma_start(rows[:, ds(g * HB, HB), :], k.xs[:, ds(g * HB, HB), :]).then_inc(stored[half], 16)
            sp.wait_ge(stored0, NIB * 16)
            sp.wait_ge(stored1, NIB * 16)


def gnn_kernel(nc, a, out):
    k = Kernel()
    k.sems = {}
    allocate(nc, k)
    rings = [[nc.alloc_semaphore(f"{name}_landed{c}") for c in range(RC)] for name in ("message", "first", "second")]
    first_phase(nc, k, a, rings[0])
    further_windows(nc, k, rings[0], message_pass)
    between_phase(nc, k)
    gcn_pass(nc, k, rings[1], layer=0)
    further_windows(nc, k, rings[1], gcn_pass)
    second_table_phase(nc, k)
    gcn_pass(nc, k, rings[2], layer=1)
    further_windows(nc, k, rings[2], gcn_pass)
    output_phase(nc, k, out)


def laid_out(inputs):
    a = {n: np.ascontiguousarray(v) for n, v in inputs.items()}

    def padded(v, fill, n=EP):
        return np.concatenate([v, np.full((n - v.shape[0],) + v.shape[1:], fill, v.dtype)])

    dst = padded(a["dst"], int(FAR))
    a["dst"] = dst
    a["dst_cols"] = np.ascontiguousarray(dst.reshape(NT, P).T)
    a["src"] = np.ascontiguousarray(padded(a["src"], 0, NCOL * P).reshape(NCOL, P).T)
    a["edge_weight"] = np.ascontiguousarray(padded(a["edge_weight"], 0).reshape(NT, P).T)
    a["edge_attr_4"] = np.ascontiguousarray(padded(a["edge_attr_4"], 0).T).reshape(P, DE * EP // P)
    return a


def kernel(**inputs):
    import concourse.bacc as bacc
    from concourse.bass_utils import run_bass_kernel_spmd

    nc = bacc.Bacc("TRN2", target_bir_lowering=False, num_devices=1)
    arrays, args = {}, {}
    for name, v in laid_out(inputs).items():
        arrays[f"in_{name}"] = v
        args[name] = nc.dram_tensor(f"in_{name}", v.shape, mybir.dt.from_np(v.dtype), kind="ExternalInput").ap()
    out = nc.dram_tensor("out", (N, D), F32, kind="ExternalOutput").ap()
    gnn_kernel(nc, args, out)
    r = run_bass_kernel_spmd(nc, [arrays], core_ids=[0])
    return r.results[0]["out"]
```
